# Optimizing a Trainium2 kernel written in Bass

```python
import numpy as np
import jax
import jax.numpy as jnp

def _softmax(x, axis=-1):
    return jax.nn.softmax(x, axis=axis)

def _gelu(x):
    return jax.nn.gelu(x, approximate=True)

def _silu(x):
    return jax.nn.silu(x)

def _sigmoid(x):
    return jax.nn.sigmoid(x)

def _layernorm(x, axis=-1, eps=1e-05):
    m = jnp.mean(x, axis=axis, keepdims=True)
    v = jnp.var(x, axis=axis, keepdims=True)
    return (x - m) / jnp.sqrt(v + eps)

def _scatter_add(tgt, idx, src, axis=0):
    return tgt.at[idx].add(src)

def _segment_sum(src, seg, n):
    return jax.ops.segment_sum(src, seg, n)
kernel_name = 'mk_gnn_resnorm_d4_gnn_r32_032b86'

def setup_inputs(seed: int=0):
    np.random.seed(seed)
    _w = jnp.asarray

    def _rec_inputs():
        import jax
        import jax.numpy as jnp
        _gk = jax.random.key(seed)
        x = -0.0005121 + 1.001 * jax.random.normal(jax.random.fold_in(_gk, 1), (3125, 32), jnp.float32)
        src = jax.random.randint(jax.random.fold_in(_gk, 2), (100000,), 0, 3125, jnp.int32)
        dst = jnp.minimum((3125 * jax.random.uniform(jax.random.fold_in(_gk, 3), (100000,)) ** 2.0).astype(jnp.int32), 99999)
        _o = jnp.argsort(dst, stable=True)
        src = src[_o]
        dst = dst[_o]
        edge_attr_3 = 0.000549083 + 1.00031 * jax.random.normal(jax.random.fold_in(_gk, 11), (100000, 3), jnp.float32)
        edge_attr_32 = 0.000216709 + 1.00012 * jax.random.normal(jax.random.fold_in(_gk, 12), (100000, 32), jnp.float32)
        edge_attr_4 = 0.000714719 + 1.00021 * jax.random.normal(jax.random.fold_in(_gk, 13), (100000, 4), jnp.float32)
        edge_attr_5 = -0.000325185 + 1.00005 * jax.random.normal(jax.random.fold_in(_gk, 14), (100000, 5), jnp.float32)
        edge_weight = 0.000452788 + 0.999756 * jax.random.normal(jax.random.fold_in(_gk, 16), (100000,), jnp.float32)
        edge_weight1 = 0.000452788 + 0.999756 * jax.random.normal(jax.random.fold_in(_gk, 17), (100000, 1), jnp.float32)
        return (x, src, dst, edge_attr_3, edge_attr_32, edge_attr_4, edge_attr_5, edge_weight, edge_weight1)
    x, src, dst, edge_attr_3, edge_attr_32, edge_attr_4, edge_attr_5, edge_weight, edge_weight1 = _rec_inputs()

    def _L0_gnn_setup():
        import jax, jax.numpy as jnp
        import numpy as np
        N_NODES = 3125
        N_EDGES = 50000
        D_FEAT = 32
        key = jax.random.key(seed)
        k1, k2, k3 = jax.random.split(key, 3)
        x = jax.random.normal(k1, (N_NODES, D_FEAT), dtype=jnp.float32)
        a = jax.random.randint(k2, (2, N_EDGES), 0, N_NODES, dtype=jnp.int64)
        e = jax.random.normal(k3, (N_EDGES,), dtype=jnp.float32)
        return {'x': x, 'a': a, 'e': e}
    _L0_gnn_all = _L0_gnn_setup()
    _L0_gnn_in = {k: v for k, v in _L0_gnn_all.items() if k in ()}
    del _L0_gnn_all

    def _L1_gnn_setup():
        import jax, jax.numpy as jnp
        import numpy as np
        import math
        M = 8
        COMBOS = [(0, 0, 0), (0, 1, 1), (1, 0, 1), (1, 1, 0), (1, 1, 1), (2, 1, 1)]

        def _cg_coeff(j1, m1, j2, m2, j3, m3):
            if m3 != m1 + m2:
                return 0.0
            f = math.factorial
            vmin = max(0, j2 - j3 - m1, j1 + m2 - j3)
            vmax = min(j1 + j2 - j3, j1 - m1, j2 + m2)
            pref = (2 * j3 + 1) * f(j3 + j1 - j2) * f(j3 - j1 + j2) * f(j1 + j2 - j3) / f(j1 + j2 + j3 + 1)
            pref *= f(j3 + m3) * f(j3 - m3) * f(j1 - m1) * f(j1 + m1) * f(j2 - m2) * f(j2 + m2)
            s = 0.0
            for v in range(vmin, vmax + 1):
                s += (-1) ** v / (f(v) * f(j1 + j2 - j3 - v) * f(j1 - m1 - v) * f(j2 + m2 - v) * f(j3 - j2 + m1 + v) * f(j3 - j1 - m2 + v))
            return math.sqrt(pref) * s

        def _su2_cg(l1, l2, l3):
            C = np.zeros((2 * l1 + 1, 2 * l2 + 1, 2 * l3 + 1), dtype=np.complex128)
            for m1 in range(-l1, l1 + 1):
                for m2 in range(-l2, l2 + 1):
                    m3 = m1 + m2
                    if -l3 <= m3 <= l3:
                        C[m1 + l1, m2 + l2, m3 + l3] = _cg_coeff(l1, m1, l2, m2, l3, m3)
            return C

        def _qmat(l):
            q = np.zeros((2 * l + 1, 2 * l + 1), dtype=np.complex128)
            for m in range(-l, 0):
                q[l + m, l + abs(m)] = 1 / np.sqrt(2)
                q[l + m, l - abs(m)] = -1j / np.sqrt(2)
            q[l, l] = 1.0
            for m in range(1, l + 1):
                q[l + m, l + abs(m)] = (-1) ** m / np.sqrt(2)
                q[l + m, l - abs(m)] = 1j * (-1) ** m / np.sqrt(2)
            return (-1j) ** l * q

        def _so3_cg(l1, l2, l3):
            C = np.einsum('ij,kl,mn,ikn->jlm', _qmat(l1), _qmat(l2), np.conj(_qmat(l3)).T, _su2_cg(l1, l2, l3))
            assert np.abs(C.imag).max() < 1e-06
            C = C.real
            return C / np.linalg.norm(C)
        CG = {c: jnp.asarray(_so3_cg(*c), dtype=jnp.float32) for c in COMBOS}
        N, E = (3125, 50000)
        ks = jax.random.split(jax.random.key(seed), 6)
        return {'node_irreps': jax.random.normal(ks[0], (N, 4 * M), jnp.float32), 'edge_index': jax.random.randint(ks[1], (2, E), 0, N, dtype=jnp.int32), 'sh0': jax.random.normal(ks[2], (E, 1), jnp.float32), 'sh1': jax.random.normal(ks[3], (E, 3), jnp.float32), 'sh2': jax.random.normal(ks[4], (E, 5), jnp.float32), 'W': jax.random.normal(ks[5], (len(COMBOS), M, M), jnp.float32)}
    _L1_gnn_all = _L1_gnn_setup()
    _L1_gnn_in = {k: v for k, v in _L1_gnn_all.items() if k in ('W',)}
    del _L1_gnn_all

    def _L2_gnn_setup():
        import jax, jax.numpy as jnp
        import numpy as np
        MUL = 8
        N_NODES = 3125
        N_EDGES = 25000
        EDGE_DIM = 32
        MLP_DIM = 64
        W_NUMEL = 4 * MUL * MUL
        ALPHA = 0.25
        C110 = 1.0 / np.sqrt(3.0)
        SI_SCALE = 1.0 / np.sqrt(MUL)
        key = jax.random.key(seed)
        ks = jax.random.split(key, 10)
        node_attr = jax.random.normal(ks[0], (N_NODES, 4 * MUL), dtype=jnp.float32)
        edge_index = jax.random.randint(ks[1], (2, N_EDGES), 0, N_NODES, dtype=jnp.int64)
        edge_sh = jax.random.normal(ks[2], (N_EDGES, 4), dtype=jnp.float32)
        edge_feat = jax.random.normal(ks[3], (N_EDGES, EDGE_DIM), dtype=jnp.float32)
        W1 = jax.random.normal(ks[4], (EDGE_DIM, MLP_DIM), dtype=jnp.float32) / np.sqrt(EDGE_DIM)
        b1 = jnp.zeros((MLP_DIM,), dtype=jnp.float32)
        W2 = jax.random.normal(ks[5], (MLP_DIM, W_NUMEL), dtype=jnp.float32) / np.sqrt(MLP_DIM)
        b2 = jnp.zeros((W_NUMEL,), dtype=jnp.float32)
        si_w0 = jax.random.normal(ks[6], (MUL, MUL), dtype=jnp.float32)
        si_w1 = jax.random.normal(ks[7], (MUL, MUL), dtype=jnp.float32)
        return {'node_attr': node_attr, 'edge_index': edge_index, 'edge_sh': edge_sh, 'edge_feat': edge_feat, 'W1': W1, 'b1': b1, 'W2': W2, 'b2': b2, 'si_w0': si_w0, 'si_w1': si_w1}
    _L2_gnn_all = _L2_gnn_setup()
    _L2_gnn_in = {k: v for k, v in _L2_gnn_all.items() if k in ('W1', 'b1', 'W2', 'b2', 'si_w0', 'si_w1')}
    del _L2_gnn_all

    def _L3_gnn_setup():
        import jax, jax.numpy as jnp
        import numpy as np
        N_NODES = 3125
        N_EDGES = 100000
        D_IN = 32
        N_HEADS = 4
        D_HEAD = 8
        key = jax.random.key(seed)
        k1, k2, k3, k4, k5, k6, k7 = jax.random.split(key, 7)
        scale = 1.0 / np.sqrt(D_IN)
        x = jax.random.normal(k1, (N_NODES, D_IN), dtype=jnp.float32)
        Wq = jax.random.normal(k2, (D_IN, N_HEADS * D_HEAD), dtype=jnp.float32) * scale
        Wk = jax.random.normal(k3, (D_IN, N_HEADS * D_HEAD), dtype=jnp.float32) * scale
        Wv = jax.random.normal(k4, (D_IN, N_HEADS * D_HEAD), dtype=jnp.float32) * scale
        Wo = jax.random.normal(k5, (N_HEADS * D_HEAD, D_IN), dtype=jnp.float32) * scale
        src = jax.random.randint(k6, (N_EDGES,), 0, N_NODES)
        dst = jax.random.randint(k7, (N_EDGES,), 0, N_NODES)
        edge_index = jnp.stack([src, dst], axis=0).astype(jnp.int64)
        return {'x': x, 'Wq': Wq, 'Wk': Wk, 'Wv': Wv, 'Wo': Wo, 'edge_index': edge_index}
    _L3_gnn_all = _L3_gnn_setup()
    _L3_gnn_in = {k: v for k, v in _L3_gnn_all.items() if k in ('Wq', 'Wk', 'Wv', 'Wo')}
    del _L3_gnn_all
    return {'x': x, 'src': src, 'dst': dst, 'edge_attr_3': edge_attr_3, 'edge_attr_32': edge_attr_32, 'edge_attr_4': edge_attr_4, 'edge_attr_5': edge_attr_5, 'edge_weight': edge_weight, 'edge_weight1': edge_weight1, 'L1_gnn_W': _L1_gnn_in['W'], 'L2_gnn_W1': _L2_gnn_in['W1'], 'L2_gnn_b1': _L2_gnn_in['b1'], 'L2_gnn_W2': _L2_gnn_in['W2'], 'L2_gnn_b2': _L2_gnn_in['b2'], 'L2_gnn_si_w0': _L2_gnn_in['si_w0'], 'L2_gnn_si_w1': _L2_gnn_in['si_w1'], 'L3_gnn_Wq': _L3_gnn_in['Wq'], 'L3_gnn_Wk': _L3_gnn_in['Wk'], 'L3_gnn_Wv': _L3_gnn_in['Wv'], 'L3_gnn_Wo': _L3_gnn_in['Wo']}

def reference(x, src, dst, edge_attr_3, edge_attr_32, edge_attr_4, edge_attr_5, edge_weight, edge_weight1, L1_gnn_W, L2_gnn_W1, L2_gnn_b1, L2_gnn_W2, L2_gnn_b2, L2_gnn_si_w0, L2_gnn_si_w1, L3_gnn_Wq, L3_gnn_Wk, L3_gnn_Wv, L3_gnn_Wo):
    import jax
    import jax.numpy as jnp

    def _L0_gnn_ref(x, a, e):
        import jax, jax.numpy as jnp
        import numpy as np
        N_NODES = 3125
        N_EDGES = 50000
        D_FEAT = 32
        src = a[0]
        tgt = a[1]
        msgs = x[src] * e[:, None]
        out = jax.ops.segment_sum(msgs, tgt, num_segments=x.shape[0])
        return out

    def _L1_gnn_ref(node_irreps, edge_index, sh0, sh1, sh2, W):
        import jax, jax.numpy as jnp
        import numpy as np
        import math
        M = 8
        COMBOS = [(0, 0, 0), (0, 1, 1), (1, 0, 1), (1, 1, 0), (1, 1, 1), (2, 1, 1)]

        def _cg_coeff(j1, m1, j2, m2, j3, m3):
            if m3 != m1 + m2:
                return 0.0
            f = math.factorial
            vmin = max(0, j2 - j3 - m1, j1 + m2 - j3)
            vmax = min(j1 + j2 - j3, j1 - m1, j2 + m2)
            pref = (2 * j3 + 1) * f(j3 + j1 - j2) * f(j3 - j1 + j2) * f(j1 + j2 - j3) / f(j1 + j2 + j3 + 1)
            pref *= f(j3 + m3) * f(j3 - m3) * f(j1 - m1) * f(j1 + m1) * f(j2 - m2) * f(j2 + m2)
            s = 0.0
            for v in range(vmin, vmax + 1):
                s += (-1) ** v / (f(v) * f(j1 + j2 - j3 - v) * f(j1 - m1 - v) * f(j2 + m2 - v) * f(j3 - j2 + m1 + v) * f(j3 - j1 - m2 + v))
            return math.sqrt(pref) * s

        def _su2_cg(l1, l2, l3):
            C = np.zeros((2 * l1 + 1, 2 * l2 + 1, 2 * l3 + 1), dtype=np.complex128)
            for m1 in range(-l1, l1 + 1):
                for m2 in range(-l2, l2 + 1):
                    m3 = m1 + m2
                    if -l3 <= m3 <= l3:
                        C[m1 + l1, m2 + l2, m3 + l3] = _cg_coeff(l1, m1, l2, m2, l3, m3)
            return C

        def _qmat(l):
            q = np.zeros((2 * l + 1, 2 * l + 1), dtype=np.complex128)
            for m in range(-l, 0):
                q[l + m, l + abs(m)] = 1 / np.sqrt(2)
                q[l + m, l - abs(m)] = -1j / np.sqrt(2)
            q[l, l] = 1.0
            for m in range(1, l + 1):
                q[l + m, l + abs(m)] = (-1) ** m / np.sqrt(2)
                q[l + m, l - abs(m)] = 1j * (-1) ** m / np.sqrt(2)
            return (-1j) ** l * q

        def _so3_cg(l1, l2, l3):
            C = np.einsum('ij,kl,mn,ikn->jlm', _qmat(l1), _qmat(l2), np.conj(_qmat(l3)).T, _su2_cg(l1, l2, l3))
            assert np.abs(C.imag).max() < 1e-06
            C = C.real
            return C / np.linalg.norm(C)
        CG = {c: jnp.asarray(_so3_cg(*c), dtype=jnp.float32) for c in COMBOS}
        N, E = (node_irreps.shape[0], edge_index.shape[1])
        src = node_irreps[edge_index[0]]
        feats = {0: src[:, :M][:, :, None], 1: src[:, M:].reshape(E, M, 3)}
        sh = {0: sh0, 1: sh1, 2: sh2}
        msg = {0: jnp.zeros((E, M, 1), node_irreps.dtype), 1: jnp.zeros((E, M, 3), node_irreps.dtype)}
        for idx, (le, ln, lo) in enumerate(COMBOS):
            base = jnp.einsum('ijk,ei,emj->emk', CG[le, ln, lo], sh[le], feats[ln])
            msg[lo] = msg[lo] + jnp.einsum('io,eik->eok', W[idx], base)
        tgt = edge_index[1]
        agg0 = jax.ops.segment_sum(msg[0].reshape(E, M), tgt, num_segments=N)
        agg1 = jax.ops.segment_sum(msg[1].reshape(E, 3 * M), tgt, num_segments=N)
        return jnp.concatenate([agg0, agg1], axis=1)

    def _L2_gnn_ref(node_attr, edge_index, edge_sh, edge_feat, W1, b1, W2, b2, si_w0, si_w1):
        import jax, jax.numpy as jnp
        import numpy as np
        MUL = 8
        N_NODES = 3125
        N_EDGES = 25000
        EDGE_DIM = 32
        MLP_DIM = 64
        W_NUMEL = 4 * MUL * MUL
        ALPHA = 0.25
        C110 = 1.0 / np.sqrt(3.0)
        SI_SCALE = 1.0 / np.sqrt(MUL)
        n = node_attr.shape[0]
        e = edge_sh.shape[0]
        h = jax.nn.relu(edge_feat @ W1 + b1)
        w = (h @ W2 + b2).reshape(e, 4, MUL, MUL)
        w_000, w_011, w_101, w_110 = (w[:, 0], w[:, 1], w[:, 2], w[:, 3])
        s = node_attr[:, :MUL]
        v = node_attr[:, MUL:].reshape(n, MUL, 3)
        src, dst = (edge_index[0], edge_index[1])
        s_e = s[src]
        v_e = v[src]
        sh0 = edge_sh[:, 0]
        sh1 = edge_sh[:, 1:4]
        m0 = ALPHA * (jnp.einsum('ei,eio->eo', s_e * sh0[:, None], w_000) + C110 * jnp.einsum('eim,em,eio->eo', v_e, sh1, w_110))
        m1 = ALPHA * (jnp.einsum('ei,em,eio->eom', s_e, sh1, w_011) + jnp.einsum('eim,eio->eom', v_e * sh0[:, None, None], w_101))
        out0 = jax.ops.segment_sum(m0, dst, num_segments=n)
        out1 = jax.ops.segment_sum(m1.reshape(e, MUL * 3), dst, num_segments=n).reshape(n, MUL, 3)
        out0 = out0 + SI_SCALE * (s @ si_w0)
        out1 = out1 + SI_SCALE * jnp.einsum('nim,io->nom', v, si_w1)
        return jnp.concatenate([out0, out1.reshape(n, MUL * 3)], axis=-1)

    def _L3_gnn_ref(x, Wq, Wk, Wv, Wo, edge_index):
        import jax, jax.numpy as jnp
        import numpy as np
        N_NODES = 3125
        N_EDGES = 100000
        D_IN = 32
        N_HEADS = 4
        D_HEAD = 8
        N = x.shape[0]
        src, dst = (edge_index[0], edge_index[1])
        q = (x @ Wq).reshape(N, N_HEADS, D_HEAD)
        k = (x @ Wk).reshape(N, N_HEADS, D_HEAD)
        v = (x @ Wv).reshape(N, N_HEADS, D_HEAD)
        inv_sqrt_d = jnp.asarray(1.0 / np.sqrt(D_HEAD), dtype=x.dtype)
        scores = jnp.einsum('ehd,ehd->eh', q[dst], k[src]) * inv_sqrt_d
        m = jax.ops.segment_max(scores, dst, num_segments=N)
        m = jnp.where(jnp.isfinite(m), m, jnp.zeros_like(m))
        e = jnp.exp(scores - m[dst])
        denom = jax.ops.segment_sum(e, dst, num_segments=N)
        msg = jax.ops.segment_sum(e[:, :, None] * v[src], dst, num_segments=N)
        attn_out = msg / jnp.maximum(denom, 1e-16)[:, :, None]
        out = attn_out.reshape(N, N_HEADS * D_HEAD) @ Wo
        return x + out
    edge_index = jnp.stack([src, dst])
    x = _layernorm(x + _L0_gnn_ref(x, edge_index, edge_weight), axis=-1)
    x = _layernorm(x + _L1_gnn_ref(x, edge_index, edge_weight1, edge_attr_3, edge_attr_5, L1_gnn_W), axis=-1)
    x = _layernorm(x + _L2_gnn_ref(x, edge_index, edge_attr_4, edge_attr_32, L2_gnn_W1, L2_gnn_b1, L2_gnn_W2, L2_gnn_b2, L2_gnn_si_w0, L2_gnn_si_w1), axis=-1)
    x = _layernorm(x + _L3_gnn_ref(x, L3_gnn_Wq, L3_gnn_Wk, L3_gnn_Wv, L3_gnn_Wo, edge_index), axis=-1)
    return x

_drawn_inputs = setup_inputs


def setup_inputs(seed=0):
    import zlib

    import numpy as np

    out = dict(_drawn_inputs(seed))
    spreads = {'L2_gnn_b1': (0.0, 0.1), 'L2_gnn_b2': (0.0, 0.1)}
    factors = {}
    for name, (base, spread) in spreads.items():
        noise = np.random.default_rng([zlib.crc32(name.encode()), seed]).standard_normal(out[name].shape)
        drawn = base * np.exp(spread * noise) if base else spread * noise
        out[name] = jnp.asarray(drawn.astype(out[name].dtype))
    for name, factor in factors.items():
        out[name] = (out[name] * factor).astype(out[name].dtype)
    return out
```

```python
from contextlib import ExitStack
import math

import numpy as np
import concourse.bass as bass
from concourse import mybir

F32 = mybir.dt.float32
I32 = mybir.dt.int32
BF16 = mybir.dt.bfloat16
ALU = mybir.AluOpType
ACT = mybir.ActivationFunctionType
AX = mybir.AxisListType

N, E, D = 3125, 100000, 32
P = 125
TE = E // P
T = 20
B = 2 * T
ITERS = TE // B
L = 128
H = -(-N // L)
NPAD = L * H
HF = N // L
REST = N - L * HF
M = 8
HEADS, DH = 4, 8
HID = 64
GW = 15 * M
KV = 2 * D
RW = D + HEADS
EB = 50
EPS = 1e-5
BIG = 1e30
DUMP = E


class Chain:

    def __init__(self, eng, sem):
        self.eng, self.sem, self.count, self.loop = eng, sem, 0, None

    def step(self, inst):
        inst.then_inc(self.sem, 1)
        self.count += 1

    def settle(self):
        if self.loop:
            i, per, first, _ = self.loop
            self.eng.wait_ge(self.sem, (i - first) * per + self.count)
        else:
            self.eng.wait_ge(self.sem, self.count)

    def enter(self, i, per, first=0):
        self.loop = (i, per, first, self.count)

    def leave(self, iters):
        _, per, _, base = self.loop
        assert self.count - base == per, (self.count - base, per)
        self.count, self.loop = base + iters * per, None


def gnn_kernel(nc, x, src, dst, ea3, ea32, ea4, ea5, ew, ew1, w_tp, w_mlp1, b_mlp1, w_mlp2,
               b_mlp2, si0, si1, wq, wk, wv, wo, out):
    ctx = ExitStack()
    with ctx:
        def sb(name, shape, dt=F32):
            return ctx.enter_context(nc.sbuf_tensor(name, shape, dt))

        def sem(name):
            return ctx.enter_context(nc.semaphore(name))

        def dram(name, shape, dt=F32):
            return nc.dram_tensor(name, shape, dt).ap()

        node_g = dram("node_g", (NPAD, GW))
        node_x = dram("node_x", (NPAD, D))
        node_kv = dram("node_kv", (NPAD, KV))
        node_q = dram("node_q", (NPAD, D))
        qstart = dram("qstart", (E + NPAD, D))
        sums = dram("sums", (E, D))
        sums3 = dram("sums3", (E, RW))
        bounds = dram("bounds", (1, NPAD + 1))

        big = sb("big", [128, 25600])
        at = 0
        wide = big[:, 0:T * 4 * M * M].rearrange("p (t i c) -> p t i c", t=T, i=M)
        at += T * 4 * M * M
        prod = big[:, at:at + T * M * 48].rearrange("p (t i c) -> p t i c", t=T, i=M)
        at += T * M * 48
        sh4 = big[:, at:at + TE * 4].rearrange("p (t c) -> p t c", c=4)
        sh4_flat = big[:, at:at + TE * 4]
        at += TE * 4
        ew_s = big[:, at:at + TE]
        at += TE
        ew1_s = big[:, at:at + TE]
        at += TE
        ef = big[:, at:at + 2 * T * D].rearrange("p (s n) -> p s n", s=2)
        at += 2 * T * D
        efT = big[:, at:at + T // 4 * P]
        at += T // 4 * P
        hid = big[:, at:at + 2 * (T // 4) * P].rearrange("p (r n) -> p r n", r=2)
        at += 2 * (T // 4) * P
        sh5_flat = big[:, at:at + TE * 5]
        sh5 = sh5_flat.rearrange("p (t c) -> p t c", c=5)
        at += TE * 5
        assert at <= 25600
        quad = big[:, 0:9 * TE].rearrange("p (t c) -> p t c", c=9)
        xT = big[:, 0:NPAD]
        vals = big[:, :].rearrange("p (t c) -> p t c", c=D)

        xg = sb("xg", [128, B * GW])
        rows0 = xg[:, 0:B * D].rearrange("p (t c) -> p t c", c=D)
        rows1 = xg[:, :].rearrange("p (t c) -> p t c", c=GW)
        rows3 = xg[:, 0:B * KV].rearrange("p (t c) -> p t c", c=KV)
        nodeout = xg[:, 0:H * GW].rearrange("p (h c) -> p h c", h=H)
        kvout = xg[:, 0:H * KV].rearrange("p (h c) -> p h c", h=H)
        qout = xg[:, H * KV:H * (KV + D)].rearrange("p (h c) -> p h c", h=H)
        centred = xg[:, 3000:3000 + H * D].rearrange("p (h c) -> p h c", h=H)
        squares = xg[:, 3800:3800 + H * D].rearrange("p (h c) -> p h c", h=H)
        fwd = xg[:, 0:HEADS * TE].rearrange("p (h t) -> p h t", h=HEADS)

        acc2 = sb("acc2", [128, 2 * EB * RW])
        acc = acc2[:, 0:B * D].rearrange("p (t c) -> p t c", c=D)
        accs = [acc2[:, s * EB * RW:(s + 1) * EB * RW].rearrange("p (t c) -> p t c", c=RW) for s in range(2)]
        lo_le = acc2[:, 1280:2560].bitcast(BF16).rearrange("p (t c) -> p t c", c=L)
        hi_eq = acc2[:, 2560:2560 + T * H // 2].bitcast(BF16).rearrange("p (t c) -> p t c", c=H)
        bwd = acc2[:, 0:HEADS * TE].rearrange("p (h t) -> p h t", h=HEADS)

        work = sb("work", [128, 2 * B * D])
        msg = work[:, 0:B * D].rearrange("p (t c) -> p t c", c=D)
        tmp = work[:, B * D:B * D + T * 24].rearrange("p (t c) -> p t c", c=24)
        tmp2 = work[:, B * D + T * 24:B * D + 2 * T * 24].rearrange("p (t c) -> p t c", c=24)
        shx = work[:, B * D + 2 * T * 24:B * D + 2 * T * 24 + 4 * T].rearrange("p (t c) -> p t c", c=4)
        qs = work[:, 0:B * D].rearrange("p (t c) -> p t c", c=D)
        qe = work[:, B * D:2 * B * D].rearrange("p (t c) -> p t c", c=D)

        sc_flat = sb("sc", [128, HEADS * TE])
        sc = sc_flat[:, :].rearrange("p (h t) -> p h t", h=HEADS)
        sh3_flat = sc_flat[:, 0:TE * 3]
        sh3 = sh3_flat.rearrange("p (t c) -> p t c", c=3)
        spill = sb("spill", [128, NPAD])
        keep = sb("keep", [128, TE])
        neg = sb("neg", [128, TE + 1])
        dst_i = neg[:, 0:TE].bitcast(I32)
        idx = [sb(f"idx{s}", [128, T], I32) for s in range(2)]
        carry = sb("carry", [128, RW])
        qfirst = sb("qfirst", [128, D])
        before = sb("before", [128, 8], I32)
        beforef = sb("beforef", [128, 4])
        ends = sb("ends", [128, H * RW])
        xn = sb("xn", [128, H, D])
        stat = sb("stat", [128, 2, H])
        has = sb("has", [128, H])
        end_c = sb("end_c", [128, H])
        start_c = sb("start_c", [128, H])
        end_i = sb("end_i", [128, H], I32)
        start_i = sb("start_i", [128, H], I32)
        tot = sb("tot", [128, H])
        hist = sb("hist", [128, H])
        cum = sb("cum", [128, H])
        si_s = sb("si_s", [128, H, D])
        red = sb("red", [128, T, 48])
        dots = sb("dots", [128, T, M])
        inits = sb("inits", [128, 2 * HEADS])
        packed = sb("packed", [128, 4, HEADS])
        stretch = sb("stretch", [128, 1])
        brow = sb("brow", [H, L])
        hilo = sb("hilo", [128, 2, T], I32)
        hilof = sb("hilof", [128, 2, T])
        iota_l = sb("iota_l", [128, L])
        iota_i = sb("iota_i", [128, L], I32)
        edge_end = sb("edge_end", [128, 2])
        ident = sb("ident", [128, 128])
        last_l = sb("last_l", [128, 128])
        wmix = sb("wmix", [D, GW])
        w1blk = sb("w1blk", [128, 2, 128])
        w2 = sb("w2", [128, 4 * M * M])
        w2v = w2[:, :].rearrange("p (i c) -> p i c", i=M)
        b1 = sb("b1", [128, 1])
        b2f = sb("b2f", [1, 4 * M * M])
        b2fv = b2f[:, :].rearrange("p (i c) -> p i c", i=M)
        b2p = sb("b2p", [1, 3, 4 * M * M], BF16)
        b2rows = sb("b2rows", [3, 4 * M * M], BF16)
        ones3 = sb("ones3", [3, 128], BF16)
        wsi = sb("wsi", [D, D])
        wkvq = sb("wkvq", [D, 3 * D])
        wos = sb("wos", [D, D])
        zero = sb("zero", [128, 800])
        fT = sb("fT", [HEADS, 7, 128])
        qcarry = sb("qcarry", [128, D])

        bank = [ctx.enter_context(nc.psum_tensor(f"bank{i}", [128, 512], F32)) for i in range(8)]

        s_dst = sem("dst_loaded")
        s_prev = sem("before_loaded")
        s_prev0 = sem("before_cleared")
        s_x = sem("x_loaded")
        s_attr = sem("attrs_loaded")
        s_ew = sem("edge_weight_loaded")
        s_wts = sem("weights_loaded")
        s_wclr = sem("weights_cleared")
        s_b2 = sem("b2_rows_split")
        s_b2m = sem("b2_rows_moved")
        s_const = sem("pool_constants_done")
        s_iota = sem("pool_iota_done")
        s_idx = [[sem(f"idx_loaded_{l}_{s}") for s in range(2)] for l in range(4)]
        s_gat = [[sem(f"rows_gathered_{l}_{s}") for s in range(2)] for l in range(4)]
        s_use = [[sem(f"rows_used_{l}_{s}") for s in range(2)] for l in range(4)]
        s_val = [sem(f"values_kept_{s}") for s in range(2)]
        s_hidx = sem("end_rows_ready")
        s_begun = sem("gathers_begun")
        s_acc = sem("sums_ready")
        s_sum = sem("sums_written")
        s_acc3 = [sem(f"sums3_ready_{s}") for s in range(2)]
        s_sum3 = [sem(f"sums3_written_{s}") for s in range(2)]
        s_onehot = sem("onehots_ready")
        s_hist = sem("histogram_ready")
        s_zero = sem("zero_ready")
        s_qz = sem("qstart_cleared")
        v_done = sem("vector_done")
        s_tail = sem("vector_to_tensor")
        s_tback = sem("tensor_to_vector")
        s_bnd = sem("bounds_written")
        s_bld = sem("bounds_loaded")
        s_gidx = sem("node_indices_ready")
        s_attn = sem("attention_ready")
        s_quad = sem("quadrupoles_done")
        s_end = sem("ends_gathered")
        s_spill = sem("spill_summed")
        s_carry = sem("carry_ready")
        s_var = sem("variance_ready")
        s_std = sem("deviation_ready")
        s_xn = sem("x_ready")
        s_tp = sem("x_transposed")
        s_tc = sem("xT_copied")
        s_pj = sem("projected")
        s_pc = sem("projection_copied")
        s_nw = sem("node_rows_written")
        s_qg = sem("first_queries_gathered")
        s_qw = sem("queries_scattered")
        s_ql = sem("qstart_loaded")
        s_qu = sem("qstart_used")
        s_ef = [sem(f"edge_feat_loaded_{s}") for s in range(2)]
        s_eft = [sem(f"edge_feat_transposed_{s}") for s in range(2)]
        s_efc = sem("edge_feat_T_copied")
        s_hp = sem("hidden_summed")
        s_hc = sem("hidden_ready")
        s_wp = sem("edge_weights_summed")
        s_wc = sem("edge_weights_copied")
        s_wu = sem("edge_weights_used")
        s_exp = sem("exponentials_ready")
        s_max = sem("maxima_subtracted")
        s_out = sem("out_written")

        NG = -(-H // 4)
        PROJ = [GW, D, 3 * D, D]
        SCOL = [16, 16, 16, 14]
        SWID = [D, D, D, RW]
        ZERO_DMAS = TE * D // 800
        WBANKS = [0, 1, 2, 7]
        TQ = T // 4
        PAIRS = T // 2

        def rep(ap, dims):
            return ap.unsqueeze(len(ap.shape)).broadcast_to(dims)

        wlist = [(wmix[0:M, 0:M], w_tp[0, :, :]), (wmix[0:M, 7 * M:8 * M], w_tp[2, :, :])]
        for c, first, comps in ((1, 1, (0, 1, 2)), (3, 4, (0, 1, 2)), (4, 8, (1, 2, 0, 1)), (5, 12, (0, 1, 2))):
            for n, j in enumerate(comps):
                wlist.append((wmix[M + j:M + j + 22:3, (first + n) * M:(first + n + 1) * M], w_tp[c, :, :]))
        for r in range(2):
            for q in range(2):
                k = 2 * r + q
                wlist.append((w1blk[k * D:(k + 1) * D, r, q * HID:(q + 1) * HID], w_mlp1))
        for q in range(2):
            for n, b in enumerate((0, 1, 3, 2)):
                wlist.append((w2v[q * HID:(q + 1) * HID, :, n * M:(n + 1) * M],
                              w_mlp2.rearrange("k (b i o) -> k b i o", b=4, i=M)[:, b, :, :]))
            wlist.append((b1[q * HID:(q + 1) * HID, :], b_mlp1.rearrange("(k a) -> k a", a=1)))
        for n, b in enumerate((0, 1, 3, 2)):
            wlist.append((b2fv[:, :, n * M:(n + 1) * M],
                          b_mlp2.rearrange("(a b i o) -> a b i o", a=1, b=4, i=M)[:, b, :, :]))
        wlist.append((wsi[0:M, 0:M], si0))
        for m in range(3):
            wlist.append((wsi[M + m:M + m + 22:3, M + m:M + m + 22:3], si1))
        wlist += [(wkvq[:, 0:D], wk), (wkvq[:, D:2 * D], wv), (wkvq[:, 2 * D:3 * D], wq), (wos[:, :], wo)]

        block = ctx.enter_context(nc.Block())

        @block.sync
        def _(sp):
            dst2 = dst.rearrange("(p t) -> p t", p=P)
            src2 = src.rearrange("(p t) -> p t", p=P)
            sums_v = sums.rearrange("(p t) c -> p t c", p=P)
            sums3_v = sums3.rearrange("(p t) c -> p t c", p=P)
            ef_v = ea32.rearrange("(p t) c -> p (t c)", p=P)
            qs_v = qstart[0:E, :].rearrange("(p t) c -> p (t c)", p=P)
            bounds_hl = [bounds[0:1, k:k + NPAD].rearrange("a (h l) -> (a h) l", l=L) for k in range(2)]

            sp.dma_start(dst_i[0:P, :], dst2).then_inc(s_dst, 16)
            sp.dma_start(ew_s[0:P, :], ew.rearrange("(p t) -> p t", p=P)).then_inc(s_ew, 16)
            sp.wait_ge(s_prev0, 1)
            sp.dma_start(before[1:P, 0:1], dst2[0:P - 1, TE - 1:TE], allow_slow_non_contiguous=True).then_inc(s_prev, 16)
            sp.dma_start(before[0:P, 1:2], dst2[:, 0:1], allow_slow_non_contiguous=True).then_inc(s_prev, 16)

            def node_rows(l):
                if l == 1:
                    sp.wait_ge(s_pc, NG)
                    sp.dma_start(node_g.rearrange("(h l) c -> l h c", l=L), nodeout).then_inc(s_nw, 16)
                elif l == 2:
                    sp.wait_ge(s_xn, 2)
                    sp.dma_start(node_x.rearrange("(h l) c -> l h c", l=L), xn[:, :, :]).then_inc(s_nw, 16)
                else:
                    sp.wait_ge(s_pc, 3 * NG)
                    sp.dma_start(node_kv.rearrange("(h l) c -> l h c", l=L), kvout).then_inc(s_nw, 16)
                    sp.dma_start(node_q.rearrange("(h l) c -> l h c", l=L), qout).then_inc(s_nw, 16)

            for l in range(4):
                if l:
                    for s in range(2):
                        sp.wait_ge(s_gat[l - 1][s], ITERS * 16 * T)
                if l == 3:
                    sp.wait_ge(s_qw, 16 * H)

                def loads(i):
                    for s in range(2):
                        if not isinstance(i, int):
                            sp.wait_ge(s_gat[l][s], i * (16 * T))
                        sp.dma_start(idx[s][0:P, :], src2[:, bass.ds(i * B + s * T, T)]).then_inc(s_idx[l][s], 16)
                        if l == 2:
                            if not isinstance(i, int):
                                sp.wait_ge(s_eft[s], i)
                            sp.dma_start(ef[0:P, s, :], ef_v[:, bass.ds((i * B + s * T) * D, T * D)]).then_inc(s_ef[s], 16)
                        if l == 3 and s == 0:
                            if not isinstance(i, int):
                                sp.wait_ge(s_qu, i)
                            sp.dma_start(qs[0:P, :, :].rearrange("p t c -> p (t c)"),
                                         qs_v[:, bass.ds(i * (B * D), B * D)]).then_inc(s_ql, 16)

                def sums_out(i):
                    sp.wait_ge(s_acc, i + (l * ITERS + 1))
                    sp.dma_start(sums_v[:, bass.ds(i * B, B), :], acc[0:P, :, :]).then_inc(s_sum, 16)

                loads(0)
                with sp.Fori(1, ITERS) as i:
                    loads(i)
                    if l < 3:
                        sums_out(i - 1)
                if l < 3:
                    sums_out(ITERS - 1)
                if l == 0:
                    sp.wait_ge(s_tail, 2)
                    sp.dma_start(bounds_hl[1], brow[:, :]).then_inc(s_bnd, 16)
                    sp.dma_start(bounds[0:1, 0:1], zero[0:1, 0:1]).then_inc(s_bnd, 16)
                    sp.wait_ge(s_bnd, 32)
                    sp.dma_start(brow[:, :], bounds_hl[0]).then_inc(s_bld, 16)
                    sp.dma_start(spill[0:P, :], bounds[0:1, 0:NPAD].broadcast_to([P, NPAD])).then_inc(s_bld, 16)
                    sp.dma_start(xg[0:P, 0:NPAD], bounds[0:1, 1:NPAD + 1].broadcast_to([P, NPAD])).then_inc(s_bld, 16)
                if l < 3:
                    node_rows(l + 1)
            with sp.Fori(0, TE // EB // 2) as i:
                for s in range(2):
                    sp.wait_ge(s_acc3[s], i + 1)
                    sp.dma_start(sums3_v[:, bass.ds((i * 2 + s) * EB, EB), :], accs[s][0:P, :, :]).then_inc(s_sum3[s], 16)
            sp.wait_ge(s_xn, 4)
            sp.dma_start(out[0:L * HF, :].rearrange("(h l) c -> l h c", l=L), xn[:, 0:HF, :]).then_inc(s_out, 16)
            sp.dma_start(out[L * HF:N, :], xn[0:REST, HF, :]).then_inc(s_out, 16)
            sp.wait_ge(s_out, 32)

        @block.gpsimd
        def _(pool):
            pool.iota(iota_i[:, :], [[1, L]], base=0, channel_multiplier=0).then_inc(s_iota, 1)
            pool.iota(before[:, 2:3], [[0, 1]], base=TE, channel_multiplier=TE).then_inc(s_iota, 1)
            pool.iota(start_i[:, :], [[L, H]], base=DUMP, channel_multiplier=1).then_inc(s_iota, 1)
            pool.memset(ident[:, :], 0.0).then_inc(s_iota, 1)
            pool.memset(last_l[:, :], 0.0).then_inc(s_iota, 1)
            pool.wait_ge(s_iota, 5)
            pool.affine_select(out=ident[:, :], in_=ident[:, :], compare_op=ALU.not_equal, fill=1.0,
                               base=0, pattern=[[-1, 128]], channel_multiplier=1).then_inc(s_const, 1)
            pool.affine_select(out=last_l[:, :], in_=last_l[:, :], compare_op=ALU.not_equal, fill=1.0,
                               base=-127, pattern=[[0, 128]], channel_multiplier=1).then_inc(s_const, 1)
            for l in range(4):
                for s in range(2):
                    pool.sem_inc(s_use[l][s], 1)
            for s in range(2):
                pool.sem_inc(s_val[s], 1)
            tables = [x, node_g, node_x, node_kv]
            slots = [rows0, rows1, rows0, rows3]
            for l in range(4):
                if l:
                    pool.wait_ge(s_nw, (16, 32, 64)[l - 1])
                if l == 3:
                    pool.indirect_dma_start(qcarry[0:P, :], None, node_q,
                                            bass.IndirectOffsetOnAxis(ap=before[0:P, 1:2], axis=0)).then_inc(s_qg, 16)
                    pool.wait_ge(s_qz, 16 * ZERO_DMAS)
                    for h in range(H):
                        pool.indirect_dma_start(qstart, bass.IndirectOffsetOnAxis(ap=start_i[:, h:h + 1], axis=0),
                                                qout[:, h, :], None).then_inc(s_qw, 16)
                    pool.wait_ge(s_qw, 16 * H)
                with pool.Fori(0, ITERS) as i:
                    for s in range(2):
                        pool.wait_ge(s_idx[l][s], i * 16 + 16)
                        pool.wait_ge(s_use[l][s], i + 1)
                        if l == 3:
                            pool.wait_ge(s_val[s], i + 1)
                        pool.sem_inc(s_begun, 1)
                        for t in range(T):
                            pool.indirect_dma_start(slots[l][0:P, s * T + t, :], None, tables[l],
                                                    bass.IndirectOffsetOnAxis(ap=idx[s][0:P, t:t + 1], axis=0)
                                                    ).then_inc(s_gat[l][s], 16)
                if l == 0:
                    pool.wait_ge(s_gidx, 1)
                if l < 3:
                    pool.wait_ge(s_sum, (l + 1) * ITERS * 16)
                else:
                    for s in range(2):
                        pool.wait_ge(s_sum3[s], TE // EB // 2 * 16)
                w = SWID[l]
                for h in range(H):
                    pool.indirect_dma_start(ends[:, h * w:(h + 1) * w], None, sums if l < 3 else sums3,
                                            bass.IndirectOffsetOnAxis(ap=end_i[:, h:h + 1], axis=0)).then_inc(s_end, 16)

        @block.vector
        def _(vec):
            ch = Chain(vec, v_done)

            vec.memset(before[:, 0:1], -1).then_inc(s_prev0, 1)
            vec.memset(xn[:, :, :], 0.0).then_inc(s_wclr, 1)
            vec.memset(wmix[:, :], 0.0).then_inc(s_wclr, 1)
            vec.memset(w1blk[:, :, :], 0.0).then_inc(s_wclr, 1)
            vec.memset(wsi[:, :], 0.0).then_inc(s_wclr, 1)
            vec.memset(zero[:, :], 0.0).then_inc(s_zero, 1)
            ch.step(vec.memset(carry[:, :], 0.0))
            ch.step(vec.memset(hist[:, :], 0.0))
            ch.step(vec.memset(ones3[:, :], 1.0))
            vec.wait_ge(s_dst, 16)
            vec.wait_ge(s_prev, 32)
            ch.step(vec.tensor_tensor(keep[0:P, 1:TE], dst_i[0:P, 1:TE], dst_i[0:P, 0:TE - 1], ALU.is_equal))
            ch.step(vec.tensor_tensor(keep[0:P, 0:1], before[0:P, 0:1], before[0:P, 1:2], ALU.is_equal))
            vec.wait_ge(s_const, 2)
            ch.step(vec.tensor_copy(iota_l[:, :], iota_i[:, :]))
            ch.step(vec.tensor_copy(edge_end[:, 0:1], before[:, 2:3]))
            ch.step(vec.tensor_copy(start_c[:, :], start_i[:, :]))
            ch.settle()

            def scans(i, l):
                if l or not isinstance(i, int):
                    vec.wait_ge(s_sum, i * 16 + l * (ITERS * 16))
                for f in range(D):
                    ch.step(vec.tensor_tensor_scan(acc[0:P, :, f], keep[0:P, bass.ds(i * B, B)], msg[0:P, :, f],
                                                   carry[0:P, f:f + 1], ALU.mult, ALU.add))
                ch.settle()
                vec.tensor_copy(carry[0:P, 0:D], acc[0:P, B - 1, :]).then_inc(s_acc, 1)
                vec.wait_ge(s_acc, i + (l * ITERS + 1))

            def gathered(l, s, i):
                vec.wait_ge(s_gat[l][s], (i + 1) * (16 * T))

            vec.wait_ge(s_ew, 16)
            def weighted(i):
                for s in range(2):
                    col = i * B + s * T
                    here = slice(s * T, (s + 1) * T)
                    ch.step(vec.tensor_scalar(hilo[0:P, 0, :], dst_i[0:P, bass.ds(col, T)], 7, None, ALU.arith_shift_right))
                    ch.step(vec.tensor_scalar(hilo[0:P, 1, :], dst_i[0:P, bass.ds(col, T)], L - 1, None, ALU.bitwise_and))
                    ch.settle()
                    ch.step(vec.tensor_copy(hilof[0:P, :, :], hilo[0:P, :, :]))
                    ch.settle()
                    ch.step(vec.tensor_tensor(hi_eq[0:P, :, :], iota_l[0:P, 0:H].unsqueeze(1).broadcast_to([P, T, H]),
                                              rep(hilof[0:P, 0, :], [P, T, H]), ALU.is_equal))
                    vec.tensor_tensor(lo_le[0:P, :, :], iota_l[0:P, :].unsqueeze(1).broadcast_to([P, T, L]),
                                      rep(hilof[0:P, 1, :], [P, T, L]), ALU.is_ge).then_inc(s_onehot, 1)
                    gathered(0, s, i)
                    vec.tensor_tensor(msg[0:P, here, :], rows0[0:P, here, :],
                                      rep(ew_s[0:P, bass.ds(col, T)], [P, T, D]), ALU.mult).then_inc(s_use[0][s], 1)
                    vec.wait_ge(s_hist, i * 2 + s + 1)
                    ch.step(vec.tensor_tensor(hist[:, :], hist[:, :], bank[0][:, 0:H], ALU.add))
                for s in range(2):
                    vec.wait_ge(s_use[0][s], i + 2)
                scans(i, 0)

            weighted(0)
            with vec.Fori(1, ITERS) as i:
                ch.enter(i, 2 * 5 + D, 1)
                weighted(i)
            ch.leave(ITERS - 1)

            ch.settle()
            vec.tensor_copy(tot[:, :], hist[:, :]).then_inc(s_tail, 1)
            vec.wait_ge(s_tback, 1)
            ch.step(vec.tensor_copy(tot[:, :], bank[0][:, 64:64 + H]))
            ch.settle()
            ch.step(vec.tensor_tensor_scan(cum[:, :], tot[:, :], zero[:, 0:H], 0.0, ALU.add, ALU.add))
            ch.step(vec.tensor_copy(end_c[:, 0:1], hist[:, 0:1]))
            ch.settle()
            vec.tensor_tensor(end_c[:, 1:H], hist[:, 1:H], cum[:, 0:H - 1], ALU.add).then_inc(s_hidx, 1)
            vec.wait_ge(s_tback, 2)
            vec.tensor_copy(brow[:, :], bank[0][0:H, 128:256]).then_inc(s_tail, 1)
            vec.wait_ge(s_tback, 3)
            ch.step(vec.tensor_copy(cum[:, :], bank[0][:, 256:256 + H]))
            vec.wait_ge(s_bld, 48)
            ch.settle()
            ch.step(vec.tensor_tensor(has[:, :], end_c[:, :], cum[:, :], ALU.is_gt))
            ch.step(vec.tensor_scalar(tot[:, :], end_c[:, :], -1.0, 0.0, ALU.add, ALU.max))
            ch.step(vec.tensor_tensor(cum[:, :], cum[:, :], start_c[:, :], ALU.subtract))
            ch.step(vec.tensor_scalar(spill[0:P, :], spill[0:P, :], edge_end[0:P, 0:1], None, ALU.is_lt))
            ch.settle()
            ch.step(vec.tensor_copy(end_i[:, :], tot[:, :]))
            ch.step(vec.tensor_tensor(cum[:, :], cum[:, :], has[:, :], ALU.mult))
            ch.step(vec.scalar_tensor_tensor(spill[0:P, :], xg[0:P, 0:NPAD], edge_end[0:P, 0:1], spill[0:P, :],
                                             ALU.is_gt, ALU.mult))
            ch.settle()
            vec.tensor_tensor(start_i[:, :], cum[:, :], start_c[:, :], ALU.add).then_inc(s_gidx, 1)
            vec.wait_ge(s_x, 32)

            def weights():
                alpha = 0.25
                vec.wait_ge(s_wts, 16 * len(wlist))
                ch.step(vec.tensor_scalar(wmix[:, M:8 * M], wmix[:, M:8 * M], 1 / math.sqrt(3), None, ALU.mult))
                ch.step(vec.tensor_scalar(wmix[:, 8 * M:12 * M], wmix[:, 8 * M:12 * M], 1 / math.sqrt(6), None, ALU.mult))
                for v in (w2v, b2fv):
                    for n, c in ((0, alpha), (1, alpha), (2, alpha / math.sqrt(3)), (3, alpha)):
                        ch.step(vec.tensor_scalar(v[:, :, n * M:(n + 1) * M], v[:, :, n * M:(n + 1) * M], c, None, ALU.mult))
                ch.step(vec.tensor_scalar(wsi[:, :], wsi[:, :], 1 / math.sqrt(M), None, ALU.mult))
                ch.step(vec.tensor_scalar(wkvq[:, 2 * D:3 * D], wkvq[:, 2 * D:3 * D], 1 / math.sqrt(DH), None, ALU.mult))
                ch.settle()
                for k in range(3):
                    ch.step(vec.tensor_copy(b2p[:, k, :], b2f[:, :]))
                    ch.settle()
                    ch.step(vec.tensor_tensor(b2f[:, :], b2f[:, :], b2p[:, k, :], ALU.subtract))
                    ch.settle()
                vec.memset(beforef[:, 2:3], 0.0).then_inc(s_b2, 1)

            weights()

            def summed(l):
                w, cols = SWID[l], SCOL[l]
                rows = ends[:, 0:H * w].rearrange("p (h c) -> p h c", h=H)
                vec.wait_ge(s_end, (l + 1) * H * 16)
                ch.step(vec.tensor_tensor(rows, rows, rep(has[:, :], [L, H, w]), ALU.mult))
                vec.wait_ge(s_spill, l + 1)
                ch.settle()
                for n, (a, b) in enumerate(((0, cols), (cols, H))):
                    ch.step(vec.tensor_tensor(rows[:, a:b, :], rows[:, a:b, :],
                                              bank[1 + n][:, 0:(b - a) * w].rearrange("p (h c) -> p h c", c=w), ALU.add))
                ch.settle()
                return rows

            def layernorm(l):
                ch.settle()
                ch.step(vec.tensor_reduce(stat[:, 0, :], xn[:, :, :], AX.X, ALU.add))
                ch.settle()
                ch.step(vec.tensor_scalar(stat[:, 0, :], stat[:, 0, :], 1 / D, None, ALU.mult))
                ch.settle()
                ch.step(vec.tensor_tensor(centred, xn[:, :, :], rep(stat[:, 0, :], [L, H, D]), ALU.subtract))
                ch.settle()
                ch.step(vec.tensor_tensor(squares, centred, centred, ALU.mult))
                ch.settle()
                ch.step(vec.tensor_reduce(stat[:, 1, :], squares, AX.X, ALU.add))
                ch.settle()
                vec.tensor_scalar(stat[:, 1, :], stat[:, 1, :], 1 / D, EPS, ALU.mult, ALU.add).then_inc(s_var, 1)
                vec.wait_ge(s_std, l + 1)
                ch.step(vec.reciprocal(stat[:, 1, :], stat[:, 0, :]))
                ch.settle()
                vec.tensor_tensor(xn[:, :, :], centred, rep(stat[:, 1, :], [L, H, D]), ALU.mult).then_inc(s_xn, 1)

            rows = summed(0)
            ch.step(vec.tensor_tensor(xn[:, :, :], xn[:, :, :], rows, ALU.add))
            layernorm(0)

            ch.step(vec.memset(carry[:, :], 0.0))
            vec.wait_ge(s_pj, NG)
            vec.wait_ge(s_attr, 4 * 16)
            a, d = math.sqrt(0.1), math.sqrt(1 / 30)
            for j, k, c, f in ((0, 2, 0, a), (2, 0, 0, a), (0, 1, 1, a), (1, 0, 1, a), (1, 1, 2, 2 * d),
                               (1, 2, 3, a), (2, 1, 3, a), (0, 0, 4, -a), (2, 2, 4, a)):
                ch.step(vec.tensor_scalar(quad[0:P, :, 3 * j + k], sh5[0:P, :, c], f, None, ALU.mult))
            ch.settle()
            for jk in (0, 8):
                ch.step(vec.scalar_tensor_tensor(quad[0:P, :, jk], sh5[0:P, :, 2], -d, quad[0:P, :, jk], ALU.mult, ALU.add))
            ch.settle()

            def by3(ap):
                return ap.rearrange("p t (k o) -> p t k o", k=3)

            with vec.Fori(0, ITERS) as i:
                ch.enter(i, 2 * 17 + D)
                for s in range(2):
                    col = i * B + s * T
                    here = slice(s * T, (s + 1) * T)
                    r, m = rows1[0:P, here, :], msg[0:P, here, :]
                    sh = sh3[0:P, bass.ds(col, T), :]
                    ta, tb = tmp[0:P, :, :], tmp2[0:P, :, :]
                    ch.settle()
                    ch.step(vec.tensor_copy(shx[0:P, :, 0:2], sh[:, :, 1:3]))
                    ch.step(vec.tensor_copy(shx[0:P, :, 2:4], sh[:, :, 0:2]))
                    gathered(1, s, i)
                    ch.step(vec.tensor_tensor(m, r[:, :, 0:4 * M], rep(ew1_s[0:P, bass.ds(col, T)], [P, T, D]), ALU.mult))
                    ch.step(vec.tensor_tensor(by3(ta), by3(r[:, :, 4 * M:7 * M]), rep(sh, [P, T, 3, M]), ALU.mult))
                    ch.step(vec.tensor_tensor(by3(tb), r[:, :, 7 * M:8 * M].unsqueeze(2).broadcast_to([P, T, 3, M]),
                                              rep(sh, [P, T, 3, M]), ALU.mult))
                    ch.settle()
                    ch.step(vec.tensor_reduce(dots[0:P, :, :], ta.rearrange("p t (k o) -> p t o k", k=3), AX.X, ALU.add))
                    ch.step(vec.tensor_tensor(m[:, :, M:D], m[:, :, M:D], tb, ALU.add))
                    ch.settle()
                    ch.step(vec.tensor_tensor(m[:, :, 0:M], m[:, :, 0:M], dots[0:P, :, :], ALU.add))
                    ch.step(vec.tensor_tensor(by3(ta), by3(r[:, :, 9 * M:12 * M]), rep(shx[0:P, :, 0:3], [P, T, 3, M]), ALU.mult))
                    ch.step(vec.tensor_tensor(by3(tb), by3(r[:, :, 8 * M:11 * M]), rep(shx[0:P, :, 1:4], [P, T, 3, M]), ALU.mult))
                    ch.settle()
                    ch.step(vec.tensor_tensor(m[:, :, M:D], m[:, :, M:D], ta, ALU.add))
                    ch.settle()
                    ch.step(vec.tensor_tensor(m[:, :, M:D], m[:, :, M:D], tb, ALU.subtract))
                    for j in range(3):
                        t_ = ta if j % 2 == 0 else tb
                        g5 = r[:, :, (12 + j) * M:(13 + j) * M].unsqueeze(2).broadcast_to([P, T, 3, M])
                        q3 = rep(quad[0:P, bass.ds(col, T), 3 * j:3 * j + 3], [P, T, 3, M])
                        if j < 2:
                            ch.step(vec.tensor_tensor(by3(t_), g5, q3, ALU.mult))
                            ch.settle()
                        else:
                            vec.tensor_tensor(by3(t_), g5, q3, ALU.mult).then_inc(s_use[1][s], 1)
                            vec.wait_ge(s_use[1][s], i + 2)
                        ch.step(vec.tensor_tensor(m[:, :, M:D], m[:, :, M:D], t_, ALU.add))
                ch.settle()
                scans(i, 1)
            ch.leave(ITERS)

            def add_swapped(rows):
                ch.step(vec.tensor_tensor(xn[:, :, 0:M], xn[:, :, 0:M], rows[:, :, 0:M], ALU.add))
                ch.step(vec.tensor_tensor(xn[:, :, M:D].rearrange("p h (o k) -> p h k o", k=3),
                                          xn[:, :, M:D].rearrange("p h (o k) -> p h k o", k=3),
                                          rows[:, :, M:D].rearrange("p h (k o) -> p h k o", k=3), ALU.add))

            rows = summed(1)
            add_swapped(rows)
            layernorm(1)

            ch.step(vec.memset(carry[:, :], 0.0))
            ch.settle()
            with vec.Fori(0, ITERS) as i:
                ch.enter(i, 2 * 11 + D)
                for s in range(2):
                    col = i * B + s * T
                    here = slice(s * T, (s + 1) * T)
                    r, m, w, pr, rd = rows0[0:P, here, :], msg[0:P, here, :], wide[0:P], prod[0:P], red[0:P, :, :]
                    v = r[:, :, M:D].rearrange("p t (i m) -> p t i m", m=3)
                    sh0 = sh4[0:P, bass.ds(col, T), 0]
                    sh1 = sh4[0:P, bass.ds(col, T), 1:4]
                    gathered(2, s, i)
                    ch.settle()
                    ch.step(vec.tensor_tensor(tmp[0:P, :, :].rearrange("p t (i m) -> p t i m", m=3), v,
                                              sh1.unsqueeze(2).broadcast_to([P, T, M, 3]), ALU.mult))
                    ch.settle()
                    ch.step(vec.tensor_reduce(dots[0:P, :, :], tmp[0:P, :, :].rearrange("p t (i m) -> p t i m", m=3), AX.X, ALU.add))
                    ch.settle()
                    vec.wait_ge(s_wc, i * (2 * PAIRS) + (s + 1) * PAIRS)
                    ch.step(vec.tensor_tensor(pr[:, :, :, 0:2 * M], w[:, :, :, 0:2 * M], rep(r[:, :, 0:M], [P, T, M, 2 * M]), ALU.mult))
                    ch.step(vec.tensor_tensor(pr[:, :, :, 2 * M:3 * M], w[:, :, :, 2 * M:3 * M], rep(dots[0:P, :, :], [P, T, M, M]), ALU.mult))
                    for k in range(2):
                        ch.step(vec.tensor_tensor(pr[:, :, :, (3 + k) * M:(4 + k) * M], w[:, :, :, 3 * M:4 * M],
                                                  rep(v[:, :, :, k], [P, T, M, M]), ALU.mult))
                    vec.tensor_tensor(pr[:, :, :, 5 * M:6 * M], w[:, :, :, 3 * M:4 * M],
                                      rep(v[:, :, :, 2], [P, T, M, M]), ALU.mult).then_inc(s_use[2][s], 1)
                    vec.wait_ge(s_use[2][s], i + 2)
                    vec.tensor_reduce(rd, pr.rearrange("p t i c -> p t c i"), AX.X, ALU.add).then_inc(s_wu, 1)
                    vec.wait_ge(s_wu, i * 2 + s + 2)
                    ch.step(vec.tensor_tensor(m[:, :, 0:M], rd[:, :, 0:M], rep(sh0, [P, T, M]), ALU.mult))
                    ch.step(vec.tensor_tensor(m[:, :, M:D], rd[:, :, 3 * M:6 * M], rep(sh0, [P, T, 3 * M]), ALU.mult))
                    ch.step(vec.tensor_tensor(by3(tmp2[0:P, :, :]), rd[:, :, M:2 * M].unsqueeze(2).broadcast_to([P, T, 3, M]),
                                              rep(sh1, [P, T, 3, M]), ALU.mult))
                    ch.settle()
                    ch.step(vec.tensor_tensor(m[:, :, 0:M], m[:, :, 0:M], rd[:, :, 2 * M:3 * M], ALU.add))
                    ch.step(vec.tensor_tensor(m[:, :, M:D], m[:, :, M:D], tmp2[0:P, :, :], ALU.add))
                ch.settle()
                scans(i, 2)
            ch.leave(ITERS)

            rows = summed(2)
            add_swapped(rows)
            ch.settle()
            vec.wait_ge(s_pc, 2 * NG)
            ch.step(vec.tensor_tensor(xn[:, :, :], xn[:, :, :], si_s[:, :, :], ALU.add))
            layernorm(2)

            ch.step(vec.memset(carry[:, :], 0.0))
            ch.step(vec.memset(neg[:, :], 0.0))
            ch.settle()
            ch.step(vec.tensor_scalar(neg[0:P, 0:TE], keep[0:P, :], -1.0, BIG, ALU.add, ALU.mult))
            vec.wait_ge(s_qg, 16)
            with vec.Fori(0, ITERS) as i:
                ch.enter(i, D + 1 + 2)
                vec.wait_ge(s_ql, i * 16 + 16)
                for f in range(D):
                    ch.step(vec.tensor_tensor_scan(qe[0:P, :, f], keep[0:P, bass.ds(i * B, B)], qs[0:P, :, f],
                                                   qcarry[0:P, f:f + 1], ALU.mult, ALU.add))
                ch.settle()
                vec.tensor_copy(qcarry[0:P, :], qe[0:P, B - 1, :]).then_inc(s_qu, 1)
                vec.wait_ge(s_qu, i + 1)
                ch.step(vec.memset(beforef[:, 3:4], 0.0))
                for s in range(2):
                    here = slice(s * T, (s + 1) * T)
                    gathered(3, s, i)
                    ch.step(vec.tensor_tensor(rows3[0:P, here, 0:D], rows3[0:P, here, 0:D], qe[0:P, here, :], ALU.mult))
                    ch.settle()
                    vec.tensor_reduce(sc[0:P, :, bass.ds(i * B + s * T, T)].rearrange("p h t -> p t h"),
                                      rows3[0:P, here, 0:D].rearrange("p t (h d) -> p t h d", h=HEADS),
                                      AX.X, ALU.add).then_inc(s_use[3][s], 1)
            ch.leave(ITERS)

            for s in range(2):
                vec.wait_ge(s_use[3][s], ITERS + 1)

            def maxima(first_f, first_b):
                for h in range(HEADS):
                    ch.step(vec.tensor_tensor_scan(fwd[0:P, h, :], neg[0:P, 0:TE], sc[0:P, h, :],
                                                   first_f(h), ALU.add, ALU.max))
                    ch.step(vec.tensor_tensor_scan(bwd[0:P, h, ::-1], neg[0:P, TE:0:-1], sc[0:P, h, ::-1],
                                                   first_b(h), ALU.add, ALU.max))

            for s in range(2):
                vec.wait_ge(s_val[s], ITERS + 1)
            maxima(lambda h: -BIG, lambda h: -BIG)
            ch.step(vec.tensor_reduce(stretch[0:P, :], keep[0:P, :], AX.X, ALU.min))
            ch.settle()
            ch.step(vec.tensor_copy(packed[0:P, 0, :], fwd[0:P, :, TE - 1]))
            ch.step(vec.tensor_copy(packed[0:P, 1, :], bwd[0:P, :, 0]))
            ch.step(vec.tensor_copy(packed[0:P, 2, :], stretch[0:P, 0:1].broadcast_to([P, HEADS])))
            ch.step(vec.memset(fT[:, :, :], -BIG))
            ch.settle()
            vec.tensor_copy(packed[0:P, 3, :], keep[0:P, 0:1].broadcast_to([P, HEADS])).then_inc(s_tail, 1)
            vec.wait_ge(s_tback, 4)
            pk = bank[0][0:HEADS, :].rearrange("p (a c) -> p a c", a=4)
            ch.step(vec.tensor_copy(fT[:, 0:2, 0:P], pk[:, 0:2, 0:P]))
            ch.step(vec.tensor_scalar(fT[:, 2:4, 0:P], pk[:, 2:4, 0:P], -1.0, BIG, ALU.add, ALU.mult))
            ch.settle()
            ch.step(vec.tensor_tensor_scan(fT[:, 4, 1:P + 1], fT[:, 2, 0:P], fT[:, 0, 0:P], -BIG, ALU.add, ALU.max))
            ch.step(vec.tensor_tensor(fT[:, 2, 0:P], fT[:, 2, 0:P], fT[:, 3, 1:P + 1], ALU.add))
            ch.settle()
            ch.step(vec.tensor_tensor_scan(fT[:, 5, P - 1::-1], fT[:, 2, P - 1::-1], fT[:, 1, P - 1::-1], -BIG, ALU.add, ALU.max))
            ch.settle()
            vec.tensor_tensor(fT[:, 6, 0:P], fT[:, 5, 1:P + 1], fT[:, 3, 1:P + 1], ALU.add).then_inc(s_tail, 1)
            vec.wait_ge(s_tback, 5)
            ch.step(vec.tensor_copy(inits[0:P, :], bank[0][0:P, 0:2 * HEADS]))
            ch.settle()
            maxima(lambda h: inits[0:P, h:h + 1], lambda h: inits[0:P, HEADS + h:HEADS + h + 1])
            ch.settle()
            ch.step(vec.tensor_tensor(fwd[0:P], fwd[0:P], bwd[0:P], ALU.max))
            ch.settle()
            vec.tensor_tensor(sc[0:P], sc[0:P], fwd[0:P], ALU.subtract).then_inc(s_max, 1)
            ch.step(vec.memset(accs[1][:, EB - 1, :], 0.0))
            ch.settle()

            vec.wait_ge(s_exp, 1)
            def weighted_values(i):
                for s in range(2):
                    cols = bass.ds((i * 2 + s) * EB, EB)
                    for h in range(HEADS):
                        ch.step(vec.tensor_tensor(vals[0:P, cols, h * DH:(h + 1) * DH], vals[0:P, cols, h * DH:(h + 1) * DH],
                                                  rep(sc[0:P, h, cols], [P, EB, DH]), ALU.mult))
                    ch.settle()
                    if not isinstance(i, int):
                        vec.wait_ge(s_sum3[s], i * 16)
                    for f in range(RW):
                        val = vals[0:P, cols, f] if f < D else sc[0:P, f - D, cols]
                        scan = vec.tensor_tensor_scan(accs[s][0:P, :, f], keep[0:P, cols], val,
                                                      accs[1 - s][0:P, EB - 1, f:f + 1], ALU.mult, ALU.add)
                        if f < RW - 1:
                            ch.step(scan)
                        else:
                            scan.then_inc(s_acc3[s], 1)
                            vec.wait_ge(s_acc3[s], i + 1)

            weighted_values(0)
            with vec.Fori(1, TE // EB // 2) as i:
                ch.enter(i, 2 * (HEADS + RW - 1), 1)
                weighted_values(i)
            ch.leave(TE // EB // 2 - 1)

            rows = summed(3)
            den = rows[:, :, D:RW]
            ch.step(vec.tensor_scalar(den, den, 1e-16, None, ALU.max))
            ch.settle()
            ch.step(vec.reciprocal(den, den))
            ch.settle()
            for h in range(HEADS):
                o = vec.tensor_tensor(si_s[:, :, h * DH:(h + 1) * DH], rows[:, :, h * DH:(h + 1) * DH],
                                      rep(rows[:, :, D + h], [L, H, DH]), ALU.mult)
                if h < HEADS - 1:
                    ch.step(o)
                else:
                    o.then_inc(s_attn, 1)
            vec.wait_ge(s_pc, 4 * NG)
            ch.step(vec.scalar_tensor_tensor(xn[:, :, :], xn[:, :, :], 2.0, si_s[:, :, :], ALU.mult, ALU.add))
            layernorm(3)

        @block.tensor
        def _(pe):
            def spilled(l):
                w, cols = SWID[l], SCOL[l]
                if l < 3:
                    pe.wait_ge(s_acc, (l + 1) * ITERS)
                    state = carry[0:P, 0:D]
                else:
                    pe.wait_ge(s_acc3[1], TE // EB // 2)
                    state = accs[1][0:P, EB - 1, :]
                for h in range(H):
                    n, c = (0, h) if h < cols else (1, h - cols)
                    last = pe.matmul(bank[1 + n][:, c * w:(c + 1) * w], spill[0:P, h * L:(h + 1) * L], state,
                                     start=True, stop=True)
                last.then_inc(s_spill, 1)

            def project(call, rows, weights):
                w = PROJ[call]
                for g in range(NG + 1):
                    if g < NG:
                        if g >= 2:
                            pe.wait_ge(s_tc, call * NG + g - 1)
                        for k in range(min(4, H - 4 * g)):
                            last = pe.transpose(bank[3 + g % 2][0:D, k * L:(k + 1) * L], rows[:, 4 * g + k, :], ident[:, :])
                        last.then_inc(s_tp, 1)
                    if g:
                        j = g - 1
                        pe.wait_ge(s_tc, call * NG + j + 1)
                        if j >= 2:
                            pe.wait_ge(s_pc, call * NG + j - 1)
                        for k in range(min(4, H - 4 * j)):
                            h = 4 * j + k
                            last = pe.matmul(bank[5 + j % 2][:, k * w:(k + 1) * w], xT[0:D, h * L:(h + 1) * L], weights,
                                             start=True, stop=True)
                        last.then_inc(s_pj, 1)

            pe.wait_ge(s_const, 2)
            with pe.Fori(0, ITERS) as i:
                for s in range(2):
                    pe.wait_ge(s_onehot, i * 2 + s + 1)
                    for t in range(T):
                        last = pe.matmul(bank[0][:, 0:H], lo_le[0:P, t, :], hi_eq[0:P, t, :], start=(t == 0), stop=(t == T - 1))
                    last.then_inc(s_hist, 1)
            pe.wait_ge(s_tail, 1)
            pe.matmul(bank[0][:, 64:64 + H], last_l[:, :], tot[:, :], start=True, stop=True).then_inc(s_tback, 1)
            pe.wait_ge(s_hidx, 1)
            pe.transpose(bank[0][0:H, 128:256], end_c[:, :], ident[:, :]).then_inc(s_tback, 1)
            pe.wait_ge(s_bld, 48)
            pe.transpose(bank[0][:, 256:256 + H], brow[:, :], ident[0:H, 0:H]).then_inc(s_tback, 1)
            pe.wait_ge(s_gidx, 1)
            spilled(0)
            pe.wait_ge(s_b2, 1)
            pe.wait_ge(s_xn, 1)
            project(0, xn, wmix[:, :])
            spilled(1)
            pe.wait_ge(s_xn, 2)
            project(1, xn, wsi[:, :])

            pe.wait_ge(s_b2m, 48)
            pe.wait_ge(s_tc, 2 * NG)
            pe.wait_ge(s_pc, 2 * NG)
            with pe.Fori(0, ITERS) as i:
                for s in range(2):
                    pe.wait_ge(s_ef[s], i * 16 + 16)
                    for g in range(TQ):
                        place = bank[3][:, g * P:(g + 1) * P] if g < 4 else bank[4][:, 0:P]
                        last = pe.transpose(place, ef[0:P, s, g * 4 * D:(g + 1) * 4 * D], ident[0:P, 0:P])
                    last.then_inc(s_eft[s], 1)
                    pe.wait_ge(s_efc, i * 4 + 2 * s + 2)
                    for r in range(2):
                        pe.matmul(bank[5 + r][:, 0:4 * P], w1blk[:, r, :], efT[:, 0:4 * P], start=True, stop=True)
                    for r in range(2):
                        last = pe.matmul(bank[4][:, (1 + r) * 128:(1 + r) * 128 + P], w1blk[:, r, :], efT[:, 4 * P:5 * P],
                                         start=True, stop=True)
                    last.then_inc(s_hp, 1)
                    pe.wait_ge(s_hc, i * 8 + 4 * s + 4)
                    for j in range(PAIRS):
                        g, q = j // 2, j % 2
                        if j >= 4:
                            pe.wait_ge(s_wc, i * (2 * PAIRS) + s * PAIRS + j - 3)
                        for r in range(2):
                            o = bank[WBANKS[(s * PAIRS + j) % 4]][0:P, r * 256:(r + 1) * 256]
                            pe.matmul(o, ones3[:, 0:P], b2rows[:, :], start=True, stop=False)
                            last = pe.matmul(o, hid[q * HID:(q + 1) * HID, r, g * P:(g + 1) * P],
                                             w2[q * HID:(q + 1) * HID, :], start=False, stop=True)
                        last.then_inc(s_wp, 1)
            pe.wait_ge(s_wc, ITERS * 2 * PAIRS)
            spilled(2)
            pe.wait_ge(s_xn, 3)
            project(2, xn, wkvq[:, :])

            pe.wait_ge(s_tail, 3)
            for k in range(4):
                last = pe.transpose(bank[0][0:HEADS, k * 128:k * 128 + P], packed[0:P, k, :], ident[0:P, 0:P])
            last.then_inc(s_tback, 1)
            pe.wait_ge(s_tail, 4)
            pe.transpose(bank[0][0:P, 0:HEADS], fT[:, 4, 0:P], ident[0:HEADS, 0:HEADS])
            pe.transpose(bank[0][0:P, HEADS:2 * HEADS], fT[:, 6, 0:P], ident[0:HEADS, 0:HEADS]).then_inc(s_tback, 1)
            spilled(3)
            pe.wait_ge(s_attn, 1)
            project(3, si_s, wos[:, :])

        @block.scalar
        def _(act):
            act.dma_start(ew1_s[0:P, :], ew1.rearrange("(p t) c -> p (t c)", p=P)).then_inc(s_attr, 16)
            act.dma_start(sh3_flat[0:P, :], ea3.rearrange("(p t) c -> p (t c)", p=P)).then_inc(s_attr, 16)
            act.dma_start(sh4_flat[0:P, :], ea4.rearrange("(p t) c -> p (t c)", p=P)).then_inc(s_attr, 16)
            act.dma_start(sh5_flat[0:P, :], ea5.rearrange("(p t) c -> p (t c)", p=P)).then_inc(s_attr, 16)
            act.wait_ge(s_wclr, 4)
            act.dma_start(xn[:, 0:HF, :], x[0:L * HF, :].rearrange("(h l) c -> l h c", l=L)).then_inc(s_x, 16)
            act.dma_start(xn[0:REST, HF, :], x[L * HF:N, :]).then_inc(s_x, 16)
            for place, weights in wlist:
                act.dma_start(place, weights, allow_slow_non_contiguous=True).then_inc(s_wts, 16)
            act.wait_ge(s_zero, 1)
            cleared = qstart[0:E, :].rearrange("(p t) c -> p (t c)", p=P)
            for r in range(ZERO_DMAS):
                act.dma_start(cleared[:, r * 800:(r + 1) * 800], zero[0:P, :]).then_inc(s_qz, 16)
            act.wait_ge(s_b2, 1)
            for k in range(3):
                act.dma_start(b2rows[k:k + 1, :], b2p[:, k, :]).then_inc(s_b2m, 16)

            def root(l):
                act.wait_ge(s_var, l + 1)
                act.activation(stat[:, 0, :], stat[:, 1, :], ACT.Sqrt).then_inc(s_std, 1)

            def evacuate(call):
                w = PROJ[call]
                for g in range(NG + 1):
                    if g < NG:
                        n = min(4, H - 4 * g)
                        act.wait_ge(s_tp, call * NG + g + 1)
                        act.copy(xT[0:D, 4 * g * L:(4 * g + n) * L], bank[3 + g % 2][0:D, 0:n * L]).then_inc(s_tc, 1)
                    if g:
                        j = g - 1
                        n = min(4, H - 4 * j)
                        hs = slice(4 * j, 4 * j + n)
                        got = bank[5 + j % 2][:, 0:n * w].rearrange("p (h c) -> p h c", c=w)
                        act.wait_ge(s_pj, call * NG + j + 1)
                        if call == 0:
                            act.copy(nodeout[:, hs, :], got).then_inc(s_pc, 1)
                        elif call == 2:
                            act.copy(kvout[:, hs, :], got[:, :, 0:KV])
                            act.copy(qout[:, hs, :], got[:, :, KV:3 * D]).then_inc(s_pc, 1)
                        else:
                            act.copy(si_s[:, hs, :], got).then_inc(s_pc, 1)

            root(0)
            evacuate(0)
            root(1)
            evacuate(1)
            act.sem_inc(s_wu, 1)
            with act.Fori(0, ITERS) as i:
                for s in range(2):
                    act.wait_ge(s_eft[s], i + 1)
                    act.copy(efT[:, 0:4 * P], bank[3][:, 0:4 * P]).then_inc(s_efc, 1)
                    act.copy(efT[:, 4 * P:5 * P], bank[4][:, 0:P]).then_inc(s_efc, 1)
                    act.wait_ge(s_hp, i * 2 + s + 1)
                    for r in range(2):
                        act.activation(hid[:, r, 0:4 * P], bank[5 + r][:, 0:4 * P], ACT.Relu, bias=b1[:, 0:1]).then_inc(s_hc, 1)
                    for r in range(2):
                        act.activation(hid[:, r, 4 * P:5 * P], bank[4][:, (1 + r) * 128:(1 + r) * 128 + P], ACT.Relu,
                                       bias=b1[:, 0:1]).then_inc(s_hc, 1)
                    act.wait_ge(s_wu, i * 2 + s + 1)
                    for j in range(PAIRS):
                        act.wait_ge(s_wp, i * (2 * PAIRS) + s * PAIRS + j + 1)
                        t = 4 * (j // 2) + j % 2
                        act.copy(wide[0:P, t:t + 3:2, :, :].rearrange("p t i c -> p t (i c)"),
                                 bank[WBANKS[(s * PAIRS + j) % 4]][0:P, :].rearrange("p (t c) -> p t c", t=2)).then_inc(s_wc, 1)
            root(2)
            evacuate(2)
            with act.Fori(0, ITERS) as i:
                for s in range(2):
                    act.wait_ge(s_gat[3][s], (i + 1) * (16 * T))
                    act.copy(vals[0:P, bass.ds(i * B + s * T, T), :], rows3[0:P, s * T:(s + 1) * T, D:KV]).then_inc(s_val[s], 1)
            act.wait_ge(s_max, 1)
            act.activation(sc[0:P], sc[0:P], ACT.Exp).then_inc(s_exp, 1)
            evacuate(3)
            root(3)


_INS = ['x', 'src', 'dst', 'edge_attr_3', 'edge_attr_32', 'edge_attr_4', 'edge_attr_5', 'edge_weight', 'edge_weight1',
        'L1_gnn_W', 'L2_gnn_W1', 'L2_gnn_b1', 'L2_gnn_W2', 'L2_gnn_b2', 'L2_gnn_si_w0', 'L2_gnn_si_w1',
        'L3_gnn_Wq', 'L3_gnn_Wk', 'L3_gnn_Wv', 'L3_gnn_Wo']


def kernel(**inputs):
    import numpy as _np
    import concourse.bacc as _bacc
    from concourse import mybir as _mybir
    from concourse.bass_utils import run_bass_kernel_spmd as _run

    nc = _bacc.Bacc("TRN2", target_bir_lowering=False, num_devices=1)
    arrays, args = {}, []
    for name in _INS:
        a = _np.ascontiguousarray(inputs[name])
        arrays[f"in_{name}_dram"] = a
        args.append(nc.dram_tensor(f"in_{name}_dram", a.shape, _mybir.dt.from_np(a.dtype), kind="ExternalInput").ap())
    out = nc.dram_tensor("out_0_dram", (N, D), F32, kind="ExternalOutput").ap()
    gnn_kernel(nc, *args, out)
    r = _run(nc, [arrays], core_ids=[0])
    return r.results[0]["out_0_dram"]
```

```python
from contextlib import ExitStack
import math

import numpy as np
import concourse.bass as bass
from concourse import mybir

F32 = mybir.dt.float32
I32 = mybir.dt.int32
BF16 = mybir.dt.bfloat16
ALU = mybir.AluOpType
ACT = mybir.ActivationFunctionType
AX = mybir.AxisListType

N, E, D = 3125, 100000, 32
P = 125
TE = E // P
T = 20
B = 2 * T
ITERS = TE // B
L = 128
H = -(-N // L)
NPAD = L * H
HF = N // L
REST = N - L * HF
M = 8
HEADS, DH = 4, 8
HID = 64
GW = 15 * M
KV = 2 * D
RW = D + HEADS
EB = 50
EPS = 1e-5
A, C, S = 7, 4, 3
Q = 4
LOOK = [2, 1, 0, 2]
LOOKED = [2 * ITERS * sum(LOOK[:l]) for l in range(5)]
GATHERED = [T - Q * g for g in LOOK]
F16 = mybir.dt.float16
BIG = 1e30
DUMP = E


class Chain:

    def __init__(self, eng, sem):
        self.eng, self.sem, self.count, self.loop = eng, sem, 0, None

    def step(self, inst):
        inst.then_inc(self.sem, 1)
        self.count += 1

    def settle(self):
        if self.loop:
            i, per, first, _ = self.loop
            self.eng.wait_ge(self.sem, (i - first) * per + self.count)
        else:
            self.eng.wait_ge(self.sem, self.count)

    def enter(self, i, per, first=0):
        self.loop = (i, per, first, self.count)

    def leave(self, iters):
        _, per, _, base = self.loop
        assert self.count - base == per, (self.count - base, per)
        self.count, self.loop = base + iters * per, None


def gnn_kernel(nc, x, src, dst, ea3, ea32, ea4, ea5, ew, ew1, w_tp, w_mlp1, b_mlp1, w_mlp2,
               b_mlp2, si0, si1, wq, wk, wv, wo, out):
    ctx = ExitStack()
    with ctx:
        def sb(name, shape, dt=F32):
            return ctx.enter_context(nc.sbuf_tensor(name, shape, dt))

        def sem(name):
            return ctx.enter_context(nc.semaphore(name))

        def dram(name, shape, dt=F32):
            return nc.dram_tensor(name, shape, dt).ap()

        node_g = dram("node_g", (NPAD, GW))
        node_x = dram("node_x", (NPAD, D))
        node_kv = dram("node_kv", (NPAD, KV))
        node_q = dram("node_q", (NPAD, D))
        qstart = dram("qstart", (E + NPAD, D))
        sums = dram("sums", (E, D))
        sums3 = dram("sums3", (E, RW))
        rcrow = dram("rcrow", (2, E), F16)
        bounds = dram("bounds", (1, NPAD + 1))

        big = sb("big", [128, 25600])
        at = 0
        wide = big[:, 0:T * 4 * M * M].rearrange("p (t i c) -> p t i c", t=T, i=M)
        at += T * 4 * M * M
        prod = big[:, at:at + T * M * 48].rearrange("p (t i c) -> p t i c", t=T, i=M)
        at += T * M * 48
        sh4 = big[:, at:at + TE * 4].rearrange("p (t c) -> p t c", c=4)
        sh4_flat = big[:, at:at + TE * 4]
        at += TE * 4
        ew_s = big[:, at:at + TE]
        at += TE
        ew1_s = big[:, at:at + TE]
        at += TE
        ef = big[:, at:at + 2 * T * D].rearrange("p (s n) -> p s n", s=2)
        at += 2 * T * D
        efT = big[:, at:at + T // 4 * P]
        at += T // 4 * P
        hid_last = big[:, at:at + Q * P].rearrange("p (k e) -> p k e", k=Q)
        at += Q * P
        sh5_flat = big[:, at:at + TE * 5]
        sh5 = sh5_flat.rearrange("p (t c) -> p t c", c=5)
        at += TE * 5
        zero = big[:, at:at + 800]
        at += 800
        assert at <= 25600
        lo_le = big[:, 0:T * L // 2].bitcast(BF16).rearrange("p (t c) -> p t c", c=L)
        hi_eq = big[:, 1280:1280 + T * H // 2].bitcast(BF16).rearrange("p (t c) -> p t c", c=H)
        src_f = big[:, 2000:2000 + 3 * TE].rearrange("p (a t) -> p a t", a=3)
        src_i = big[:, 4400:4400 + TE].bitcast(I32)
        turned = big[:, 5200:5200 + 8 * P].bitcast(F16).rearrange("p (b a e) -> p b a e", b=8, a=2)
        quad = big[:, 0:9 * TE].rearrange("p (t c) -> p t c", c=9)
        xT = big[:, 0:NPAD]
        vals = big[:, :].rearrange("p (t c) -> p t c", c=D)

        xg = sb("xg", [128, B * GW])
        rows0 = xg[:, 0:B * D].rearrange("p (t c) -> p t c", c=D)
        rows1 = xg[:, :].rearrange("p (t c) -> p t c", c=GW)
        rows3 = xg[:, 0:B * KV].rearrange("p (t c) -> p t c", c=KV)
        nodeout = xg[:, 0:H * GW].rearrange("p (h c) -> p h c", h=H)
        kvout = xg[:, 0:H * KV].rearrange("p (h c) -> p h c", h=H)
        qout = xg[:, H * KV:H * (KV + D)].rearrange("p (h c) -> p h c", h=H)
        centred = xg[:, 3000:3000 + H * D].rearrange("p (h c) -> p h c", h=H)
        squares = xg[:, 3800:3800 + H * D].rearrange("p (h c) -> p h c", h=H)
        ends = xg[:, 0:H * RW]
        si_s = xg[:, 1280:1280 + H * D].rearrange("p (h c) -> p h c", h=H)
        fwd = xg[:, 0:HEADS * TE].rearrange("p (h t) -> p h t", h=HEADS)

        acc2 = sb("acc2", [128, 2 * EB * RW])
        acc = acc2[:, 0:B * D].rearrange("p (t c) -> p t c", c=D)
        accs = [acc2[:, s * EB * RW:(s + 1) * EB * RW].rearrange("p (t c) -> p t c", c=RW) for s in range(2)]
        onehot = acc2[:, 1280:1280 + A * 250].bitcast(BF16).rearrange("p (a e) -> p a e", a=A)
        masked = acc2[:, 3040:3540]
        hid = acc2[:, 1280:1280 + 16 * P].rearrange("p (k n) -> p k n", k=Q)
        bwd = acc2[:, 0:HEADS * TE].rearrange("p (h t) -> p h t", h=HEADS)

        work = sb("work", [128, 2 * B * D])
        msg = work[:, 0:B * D].rearrange("p (t c) -> p t c", c=D)
        tmp = work[:, B * D:B * D + T * 24].rearrange("p (t c) -> p t c", c=24)
        tmp2 = work[:, B * D + T * 24:B * D + 2 * T * 24].rearrange("p (t c) -> p t c", c=24)
        shx = work[:, B * D + 2 * T * 24:B * D + 2 * T * 24 + 4 * T].rearrange("p (t c) -> p t c", c=4)
        rest = work[:, B * D:B * D + H * D].rearrange("p (h c) -> p h c", h=H)
        qs = work[:, 0:B * D].rearrange("p (t c) -> p t c", c=D)
        qe = work[:, B * D:2 * B * D].rearrange("p (t c) -> p t c", c=D)

        sc_flat = sb("sc", [128, HEADS * TE])
        sc = sc_flat[:, :].rearrange("p (h t) -> p h t", h=HEADS)
        sh3_flat = sc_flat[:, 0:TE * 3]
        sh3 = sh3_flat.rearrange("p (t c) -> p t c", c=3)
        table = sb("table", [128, A, Q * P], F16)
        parts = sb("parts", [128, A, S, C * D], BF16)
        rc_f = sb("rc", [128, 2 * 2 * Q * P])
        rc = [rc_f[:, s_ * 1000:(s_ + 1) * 1000].bitcast(F16).rearrange("p (a e) -> p a e", a=2) for s_ in range(2)]
        red = rc_f[:, 0:T * 48].rearrange("p (t c) -> p t c", c=48)
        stack_i = sb("stack_i", [128, D])
        stack_mix = sb("stack_mix", [128, GW])
        stack_kv = sb("stack_kv", [128, KV])
        stacks = [stack_i, stack_mix, None, stack_kv]
        pnum = sb("pnum", [128, 1 + A], I32)
        cval = sb("cval", [128, 3])
        spill = sb("spill", [128, NPAD])
        keep = sb("keep", [128, TE])
        neg = sb("neg", [128, TE + 1])
        dst_i = neg[:, 0:TE].bitcast(I32)
        idx = [sb(f"idx{s}", [128, T], I32) for s in range(2)]
        carry = sb("carry", [128, RW])
        before = sb("before", [128, 8], I32)
        beforef = sb("beforef", [128, 4])
        xn = sb("xn", [128, H, D])
        stat = sb("stat", [128, 2, H])
        has = sb("has", [128, H])
        end_c = sb("end_c", [128, H])
        start_c = sb("start_c", [128, H])
        end_i = sb("end_i", [128, H], I32)
        start_i = sb("start_i", [128, H], I32)
        tot = sb("tot", [128, H])
        hist = sb("hist", [128, H])
        cum = sb("cum", [128, H])
        dots = sb("dots", [128, T, M])
        inits = sb("inits", [128, 2 * HEADS])
        packed = sb("packed", [128, 4, HEADS])
        stretch = sb("stretch", [128, 1])
        brow = sb("brow", [H, L])
        hilo = sb("hilo", [128, 2, T], I32)
        hilof = sb("hilof", [128, 2, T])
        iota_l = sb("iota_l", [128, L])
        iota_i = big[:, 6200:6200 + L].bitcast(I32)
        edge_end = sb("edge_end", [128, 2])
        ident = sb("ident", [128, 128])
        last_l = sb("last_l", [128, 128])
        wmix = sb("wmix", [D, GW])
        w1blk = sb("w1blk", [128, Q, 128])
        w2 = sb("w2", [128, 4 * M * M])
        w2v = w2[:, :].rearrange("p (i c) -> p i c", i=M)
        b1 = sb("b1", [128, 1])
        wsi = sb("wsi", [D, D])
        wkvq = sb("wkvq", [D, 3 * D])
        wos = sb("wos", [D, D])
        fT = work[0:HEADS, 0:7 * 128].rearrange("h (a p) -> h a p", a=7)
        qcarry = sb("qcarry", [128, D])

        bank = [ctx.enter_context(nc.psum_tensor(f"bank{i}", [128, 512], F32)) for i in range(8)]

        s_dst = sem("dst_loaded")
        s_prev = sem("before_loaded")
        s_prev0 = sem("before_cleared")
        s_x = sem("x_loaded")
        s_attr = sem("attrs_loaded")
        s_ew = sem("edge_weight_loaded")
        s_wts = sem("weights_loaded")
        s_wclr = sem("weights_cleared")
        s_scaled = sem("weights_scaled")
        s_const = sem("pool_constants_done")
        s_iota = sem("pool_iota_done")
        s_idx = [[sem(f"idx_loaded_{l}_{s}") for s in range(2)] for l in range(4)]
        s_gat = [[sem(f"rows_gathered_{l}_{s}") for s in range(2)] for l in range(4)]
        s_use = [[sem(f"rows_used_{l}_{s}") for s in range(2)] for l in range(4)]
        s_val = [sem(f"values_kept_{s}") for s in range(2)]
        s_hidx = sem("end_rows_ready")
        s_begun = sem("gathers_begun")
        s_acc = sem("sums_ready")
        s_sum = sem("sums_written")
        s_acc3 = [sem(f"sums3_ready_{s}") for s in range(2)]
        s_sum3 = [sem(f"sums3_written_{s}") for s in range(2)]
        s_onehot = sem("onehots_ready")
        s_hist = sem("histogram_ready")
        s_zero = sem("zero_ready")
        s_qz = sem("qstart_cleared")
        v_done = sem("vector_done")
        s_tail = sem("vector_to_tensor")
        s_tback = sem("tensor_to_vector")
        s_bnd = sem("bounds_written")
        s_bld = sem("bounds_loaded")
        s_gidx = sem("node_indices_ready")
        s_attn = sem("attention_ready")
        s_quad = sem("quadrupoles_done")
        s_end = sem("ends_gathered")
        s_spill = sem("spill_summed")
        s_carry = sem("carry_ready")
        s_var = sem("variance_ready")
        s_std = sem("deviation_ready")
        s_xn = sem("x_ready")
        s_tp = sem("x_transposed")
        s_tc = sem("xT_copied")
        s_pj = sem("projected")
        s_pc = sem("projection_copied")
        s_nw = sem("node_rows_written")
        s_qg = sem("first_queries_gathered")
        s_qw = sem("queries_scattered")
        s_ql = sem("qstart_loaded")
        s_qu = sem("qstart_used")
        s_ef = [sem(f"edge_feat_loaded_{s}") for s in range(2)]
        s_eft = [sem(f"edge_feat_transposed_{s}") for s in range(2)]
        s_efc = sem("edge_feat_T_copied")
        s_hp = sem("hidden_summed")
        s_hc = sem("hidden_ready")
        s_wp = sem("edge_weights_summed")
        s_wc = sem("edge_weights_copied")
        s_exp = sem("exponentials_ready")
        s_max = sem("maxima_subtracted")
        s_out = sem("out_written")
        s_src = sem("src_loaded")
        s_rcf = sem("src_split")
        s_rct = sem("src_split_turned")
        s_rcc = sem("src_turned_copied")
        s_rcw = sem("rcrow_written")
        s_rc = [sem(f"rc_loaded_{s}") for s in range(2)]
        s_stk = sem("stacks_loaded")
        s_parts = sem("parts_ready")
        s_oh = sem("onehot_halves_ready")
        s_lk = sem("candidates_summed")
        s_mk = sem("candidates_masked")
        s_lp = sem("rows_turned")
        s_lc = sem("looked_up_rows_copied")

        NG = -(-H // 4)
        PROJ = [GW, D, 3 * D, D]
        SCOL = [16, 16, 16, 14]
        SWID = [D, D, D, RW]
        ZERO_DMAS = TE * D // 800
        WBANKS = [0, 1, 2, 7]
        TQ = T // 4
        PAIRS = T // 2

        def rep(ap, dims):
            return ap.unsqueeze(len(ap.shape)).broadcast_to(dims)

        RC0 = [0, 16 * ITERS, 0, 2 * 16 * ITERS]

        wlist = [(wmix[0:M, 0:M], w_tp[0, :, :]), (wmix[0:M, 7 * M:8 * M], w_tp[2, :, :])]
        for c, first, comps in ((1, 1, (0, 1, 2)), (3, 4, (0, 1, 2)), (4, 8, (1, 2, 0, 1)), (5, 12, (0, 1, 2))):
            for n, j in enumerate(comps):
                wlist.append((wmix[M + j:M + j + 22:3, (first + n) * M:(first + n + 1) * M], w_tp[c, :, :]))
        for k in range(Q):
            wlist.append((w1blk[k * D:(k + 1) * D, k, 0:HID], w_mlp1))
        wlist.append((b1[0:HID, :], b_mlp1.rearrange("(k a) -> k a", a=1)))
        for n, b in enumerate((0, 1, 3, 2)):
            wlist.append((w2v[0:HID, :, n * M:(n + 1) * M],
                          w_mlp2.rearrange("k (b i o) -> k b i o", b=4, i=M)[:, b, :, :]))
            wlist.append((w2v[HID:HID + 1, :, n * M:(n + 1) * M],
                          b_mlp2.rearrange("(a b i o) -> a b i o", a=1, b=4, i=M)[:, b, :, :]))
        wlist.append((wsi[0:M, 0:M], si0))
        for m in range(3):
            wlist.append((wsi[M + m:M + m + 22:3, M + m:M + m + 22:3], si1))
        wlist += [(wkvq[:, 0:D], wk), (wkvq[:, D:2 * D], wv), (wkvq[:, 2 * D:3 * D], wq), (wos[:, :], wo)]

        block = ctx.enter_context(nc.Block())

        @block.sync
        def _(sp):
            dst2 = dst.rearrange("(p t) -> p t", p=P)
            src2 = src.rearrange("(p t) -> p t", p=P)
            sums_v = sums.rearrange("(p t) c -> p t c", p=P)
            sums3_v = sums3.rearrange("(p t) c -> p t c", p=P)
            ef_v = ea32.rearrange("(p t) c -> p (t c)", p=P)
            qs_v = qstart[0:E, :].rearrange("(p t) c -> p (t c)", p=P)
            bounds_hl = [bounds[0:1, k:k + NPAD].rearrange("a (h l) -> (a h) l", l=L) for k in range(2)]

            sp.dma_start(dst_i[0:P, :], dst2).then_inc(s_dst, 16)
            sp.dma_start(src_i[0:P, :], src2).then_inc(s_src, 16)
            sp.dma_start(ew_s[0:P, :], ew.rearrange("(p t) -> p t", p=P)).then_inc(s_ew, 16)
            sp.wait_ge(s_prev0, 1)
            sp.dma_start(before[1:P, 0:1], dst2[0:P - 1, TE - 1:TE], allow_slow_non_contiguous=True).then_inc(s_prev, 16)
            sp.dma_start(before[0:P, 1:2], dst2[:, 0:1], allow_slow_non_contiguous=True).then_inc(s_prev, 16)

            def node_rows(l):
                if l == 1:
                    sp.wait_ge(s_pc, NG)
                    sp.dma_start(node_g.rearrange("(h l) c -> l h c", l=L), nodeout).then_inc(s_nw, 16)
                elif l == 2:
                    sp.wait_ge(s_xn, 2)
                    sp.dma_start(node_x.rearrange("(h l) c -> l h c", l=L), xn[:, :, :]).then_inc(s_nw, 16)
                else:
                    sp.wait_ge(s_pc, 3 * NG)
                    sp.dma_start(node_kv.rearrange("(h l) c -> l h c", l=L), kvout).then_inc(s_nw, 16)
                    sp.dma_start(node_q.rearrange("(h l) c -> l h c", l=L), qout).then_inc(s_nw, 16)

            for l in range(4):
                if l:
                    for s in range(2):
                        sp.wait_ge(s_gat[l - 1][s], ITERS * 16 * GATHERED[l - 1])
                if l == 3:
                    sp.wait_ge(s_qw, 16 * H)

                if l == 0:
                    def rc_out():
                        for b in range(8):
                            for a in range(2):
                                sp.dma_start(rcrow[a:a + 1, b * 100 * P:(b + 1) * 100 * P].rearrange("a (t e) -> (a t) e", e=P),
                                             turned[0:100, b, a, :]).then_inc(s_rcw, 16)
                        sp.wait_ge(s_rcw, 256)

                def rc_in(i, s):
                    n = Q * LOOK[l] * P
                    if not isinstance(i, int):
                        sp.wait_ge(s_mk, i * (2 * LOOK[l]) + (LOOKED[l] + (s - 1) * LOOK[l]))
                    sp.dma_start(rc[s][:, :, 0:n],
                                 rcrow[:, bass.ds((i * B + s * T + GATHERED[l]) * P, n)].partition_broadcast(128)).then_inc(s_rc[s], 16)

                def loads(i):
                    for s in range(2):
                        if not isinstance(i, int):
                            sp.wait_ge(s_gat[l][s], i * (16 * GATHERED[l]))
                        sp.dma_start(idx[s][0:P, :], src2[:, bass.ds(i * B + s * T, T)]).then_inc(s_idx[l][s], 16)
                        if l == 0 and s == 1 and isinstance(i, int):
                            sp.wait_ge(s_rcc, 16)
                            rc_out()
                            for k in range(2):
                                rc_in(0, k)
                        elif LOOK[l] and (l or not isinstance(i, int)):
                            rc_in(i, s)
                        if l == 2:
                            if not isinstance(i, int):
                                sp.wait_ge(s_eft[s], i)
                            sp.dma_start(ef[0:P, s, :], ef_v[:, bass.ds((i * B + s * T) * D, T * D)]).then_inc(s_ef[s], 16)
                        if l == 3 and s == 0:
                            if not isinstance(i, int):
                                sp.wait_ge(s_qu, i)
                            sp.dma_start(qs[0:P, :, :].rearrange("p t c -> p (t c)"),
                                         qs_v[:, bass.ds(i * (B * D), B * D)]).then_inc(s_ql, 16)

                def sums_out(i):
                    sp.wait_ge(s_acc, i + (l * ITERS + 1))
                    sp.dma_start(sums_v[:, bass.ds(i * B, B), :], acc[0:P, :, :]).then_inc(s_sum, 16)

                loads(0)
                with sp.Fori(1, ITERS) as i:
                    loads(i)
                    if l < 3:
                        sums_out(i - 1)
                if l < 3:
                    sums_out(ITERS - 1)
                if l == 0:
                    sp.wait_ge(s_tail, 2)
                    sp.dma_start(bounds_hl[1], brow[:, :]).then_inc(s_bnd, 16)
                    sp.dma_start(bounds[0:1, 0:1], zero[0:1, 0:1]).then_inc(s_bnd, 16)
                    sp.wait_ge(s_bnd, 32)
                    sp.dma_start(brow[:, :], bounds_hl[0]).then_inc(s_bld, 16)
                    sp.dma_start(spill[0:P, :], bounds[0:1, 0:NPAD].broadcast_to([P, NPAD])).then_inc(s_bld, 16)
                    sp.dma_start(xg[0:P, 0:NPAD], bounds[0:1, 1:NPAD + 1].broadcast_to([P, NPAD])).then_inc(s_bld, 16)
                if l < 3:
                    node_rows(l + 1)
            with sp.Fori(0, TE // EB // 2) as i:
                for s in range(2):
                    sp.wait_ge(s_acc3[s], i + 1)
                    sp.dma_start(sums3_v[:, bass.ds((i * 2 + s) * EB, EB), :], accs[s][0:P, :, :]).then_inc(s_sum3[s], 16)
            sp.wait_ge(s_xn, 4)
            sp.dma_start(out[0:L * HF, :].rearrange("(h l) c -> l h c", l=L), xn[:, 0:HF, :]).then_inc(s_out, 16)
            sp.dma_start(out[L * HF:N, :], xn[0:REST, HF, :]).then_inc(s_out, 16)
            sp.wait_ge(s_out, 32)

        @block.gpsimd
        def _(pool):
            pool.iota(iota_i[:, :], [[1, L]], base=0, channel_multiplier=0).then_inc(s_iota, 1)
            pool.iota(before[:, 2:3], [[0, 1]], base=TE, channel_multiplier=TE).then_inc(s_iota, 1)
            pool.iota(start_i[:, :], [[L, H]], base=DUMP, channel_multiplier=1).then_inc(s_iota, 1)
            pool.iota(pnum[:, 0:1], [[0, 1]], base=0, channel_multiplier=1).then_inc(s_iota, 1)
            pool.iota(pnum[:, 1:1 + A], [[L, A]], base=0, channel_multiplier=1).then_inc(s_iota, 1)
            pool.memset(ident[:, :], 0.0).then_inc(s_iota, 1)
            pool.memset(last_l[:, :], 0.0).then_inc(s_iota, 1)
            pool.wait_ge(s_iota, 7)
            pool.affine_select(out=ident[:, :], in_=ident[:, :], compare_op=ALU.not_equal, fill=1.0,
                               base=0, pattern=[[-1, 128]], channel_multiplier=1).then_inc(s_const, 1)
            pool.affine_select(out=last_l[:, :], in_=last_l[:, :], compare_op=ALU.not_equal, fill=1.0,
                               base=-127, pattern=[[0, 128]], channel_multiplier=1).then_inc(s_const, 1)
            for l in range(4):
                for s in range(2):
                    pool.sem_inc(s_use[l][s], 1)
            for s in range(2):
                pool.sem_inc(s_val[s], 1)
            tables = [x, node_g, node_x, node_kv]
            slots = [rows0, rows1, rows0, rows3]
            for l in range(4):
                if l:
                    pool.wait_ge(s_nw, (16, 32, 64)[l - 1])
                if l == 3:
                    pool.indirect_dma_start(qcarry[0:P, :], None, node_q,
                                            bass.IndirectOffsetOnAxis(ap=before[0:P, 1:2], axis=0)).then_inc(s_qg, 16)
                    pool.wait_ge(s_qz, 16 * ZERO_DMAS)
                    for h in range(H):
                        pool.indirect_dma_start(qstart, bass.IndirectOffsetOnAxis(ap=start_i[:, h:h + 1], axis=0),
                                                qout[:, h, :], None).then_inc(s_qw, 16)
                    pool.wait_ge(s_qw, 16 * H)
                with pool.Fori(0, ITERS) as i:
                    for s in range(2):
                        pool.wait_ge(s_idx[l][s], i * 16 + 16)
                        pool.wait_ge(s_use[l][s], i + 1)
                        if l == 3:
                            pool.wait_ge(s_val[s], i + 1)
                        pool.sem_inc(s_begun, 1)
                        for t in range(GATHERED[l]):
                            pool.indirect_dma_start(slots[l][0:P, s * T + t, :], None, tables[l],
                                                    bass.IndirectOffsetOnAxis(ap=idx[s][0:P, t:t + 1], axis=0)
                                                    ).then_inc(s_gat[l][s], 16)
                if l == 0:
                    pool.wait_ge(s_gidx, 1)
                if l < 3:
                    pool.wait_ge(s_sum, (l + 1) * ITERS * 16)
                else:
                    for s in range(2):
                        pool.wait_ge(s_sum3[s], TE // EB // 2 * 16)
                w = SWID[l]
                for h in range(H):
                    pool.indirect_dma_start(ends[:, h * w:(h + 1) * w], None, sums if l < 3 else sums3,
                                            bass.IndirectOffsetOnAxis(ap=end_i[:, h:h + 1], axis=0)).then_inc(s_end, 16)

        @block.vector
        def _(vec):
            ch = Chain(vec, v_done)

            vec.memset(before[:, 0:1], -1).then_inc(s_prev0, 1)
            vec.memset(xn[:, :, :], 0.0).then_inc(s_wclr, 1)
            vec.memset(wmix[:, :], 0.0).then_inc(s_wclr, 1)
            vec.memset(w1blk[:, :, :], 0.0).then_inc(s_wclr, 1)
            vec.memset(wsi[:, :], 0.0).then_inc(s_wclr, 1)
            vec.memset(w2[:, :], 0.0).then_inc(s_wclr, 1)
            vec.memset(b1[HID:128, :], 0.0).then_inc(s_wclr, 1)
            vec.wait_ge(s_wclr, 6)
            vec.memset(b1[HID:HID + 1, :], 1.0).then_inc(s_wclr, 1)
            vec.memset(zero[:, :], 0.0).then_inc(s_zero, 1)
            ch.step(vec.memset(carry[:, :], 0.0))
            ch.step(vec.memset(hist[:, :], 0.0))
            vec.wait_ge(s_dst, 16)
            vec.wait_ge(s_prev, 32)
            ch.step(vec.tensor_tensor(keep[0:P, 1:TE], dst_i[0:P, 1:TE], dst_i[0:P, 0:TE - 1], ALU.is_equal))
            ch.step(vec.tensor_tensor(keep[0:P, 0:1], before[0:P, 0:1], before[0:P, 1:2], ALU.is_equal))
            vec.wait_ge(s_const, 2)
            ch.step(vec.tensor_copy(iota_l[:, :], iota_i[:, :]))
            ch.step(vec.tensor_copy(edge_end[:, 0:1], before[:, 2:3]))
            ch.step(vec.tensor_copy(start_c[:, :], start_i[:, :]))
            ch.settle()

            vec.wait_ge(s_src, 16)
            ch.step(vec.tensor_copy(src_f[0:P, 0, :], src_i[0:P, :]))
            ch.step(vec.tensor_copy(cval[:, 0:1], pnum[:, 0:1]))
            ch.step(vec.tensor_copy(table[:, :, :], rep(pnum[:, 1:1 + A], [128, A, Q * P])))
            ch.step(vec.tensor_reduce(stack_i[:, :], ident[:, :].rearrange("p (c f) -> p f c", c=C), AX.X, ALU.add))
            ch.step(vec.memset(parts[:, :, :, :], 0.0))
            ch.settle()
            ch.step(vec.tensor_scalar(src_f[0:P, 2, :], src_f[0:P, 0, :], float(L * A), None, ALU.is_ge))
            ch.step(vec.tensor_scalar(cval[:, 1:2], cval[:, 0:1], float(D), None, ALU.is_ge))
            for c in range(2, C):
                ch.settle()
                ch.step(vec.scalar_tensor_tensor(src_f[0:P, 2, :], src_f[0:P, 0, :], float(L * A * c), src_f[0:P, 2, :], ALU.is_ge, ALU.add))
                ch.step(vec.scalar_tensor_tensor(cval[:, 1:2], cval[:, 0:1], float(D * c), cval[:, 1:2], ALU.is_ge, ALU.add))
            ch.settle()
            vec.scalar_tensor_tensor(src_f[0:P, 1, :], src_f[0:P, 2, :], -float(L * A), src_f[0:P, 0, :], ALU.mult, ALU.add).then_inc(s_rcf, 1)

            def split(l):
                if l:
                    vec.wait_ge(s_lk, LOOKED[l])
                    vec.wait_ge(s_xn, l)
                def at_(k, a, c0, c1):
                    return parts[:, 0:a, k, c0 * D:c1 * D].rearrange("p a (c f) -> p c a f", f=D)
                views = [(slice(0, 21), 7, 0, 3), (slice(21, 25), 4, 3, 4)]
                ch.settle()
                for k in range(S):
                    for hs, a, c0, c1 in views:
                        from_ = (xn[:, hs, :] if k == 0 else rest[:, hs, :]).rearrange("p (c a) f -> p c a f", a=a)
                        ch.step(vec.tensor_copy(at_(k, a, c0, c1), from_))
                    ch.settle()
                    if k < S - 1:
                        for hs, a, c0, c1 in views:
                            from_ = (xn[:, hs, :] if k == 0 else rest[:, hs, :]).rearrange("p (c a) f -> p c a f", a=a)
                            ch.step(vec.tensor_tensor(rest[:, hs, :].rearrange("p (c a) f -> p c a f", a=a), from_,
                                                      at_(k, a, c0, c1), ALU.subtract))
                        ch.settle()
                vec.memset(beforef[:, 3:4], 0.0).then_inc(s_parts, 1)

            def onehots(l, i, s, g):
                if g == 0:
                    vec.wait_ge(s_rc[s], RC0[l] + i * 16 + 16)
                n = i * (2 * LOOK[l]) + (LOOKED[l] + s * LOOK[l] + g)
                if not isinstance(n, int) or n:
                    vec.wait_ge(s_lk, n)
                for a, b in ((0, 4), (4, A)):
                    vec.tensor_tensor(onehot[:, a:b, :], rc[s][:, 0, g * Q * P:(g + 1) * Q * P].unsqueeze(1).broadcast_to([128, b - a, Q * P]),
                                      table[:, a:b, :], ALU.is_equal).then_inc(s_oh, 1)

            def mask(l, i, s, g):
                n = i * (2 * LOOK[l]) + (LOOKED[l] + s * LOOK[l] + g)
                vec.wait_ge(s_lk, n + 1)
                if not isinstance(n, int) or n:
                    vec.wait_ge(s_lp, n)
                vec.scalar_tensor_tensor(masked[:, :], rc[s][:, 1, g * Q * P:(g + 1) * Q * P], cval[:, 1:2],
                                         bank[3][:, 0:Q * P], ALU.is_equal, ALU.mult).then_inc(s_mk, 1)

            def ahead(l, i, s, stage, last):
                if LOOK[l] == 0 or (last and s == 1):
                    return
                i, s = (i, 1) if s == 0 else (i + 1, 0)
                if stage == 0:
                    onehots(l, i, s, 0)
                elif stage == 1:
                    mask(l, i, s, 0)
                    if LOOK[l] == 2:
                        onehots(l, i, s, 1)
                elif LOOK[l] == 2:
                    mask(l, i, s, 1)

            def first_lookups(l):
                for g in range(LOOK[l]):
                    onehots(l, 0, 0, g)
                    mask(l, 0, 0, g)

            def bodies(l, body, per):
                first = 0
                if l == 0:
                    body(0, False)
                    first = 1
                with vec.Fori(first, ITERS - 1) as i:
                    ch.enter(i, per, first)
                    body(i, False)
                ch.leave(ITERS - 1 - first)
                body(ITERS - 1, True)

            def scans(i, l):
                if l or not isinstance(i, int) or i:
                    vec.wait_ge(s_sum, i * 16 + l * (ITERS * 16))
                for f in range(D):
                    ch.step(vec.tensor_tensor_scan(acc[0:P, :, f], keep[0:P, bass.ds(i * B, B)], msg[0:P, :, f],
                                                   carry[0:P, f:f + 1], ALU.mult, ALU.add))
                ch.settle()
                vec.tensor_copy(carry[0:P, 0:D], acc[0:P, B - 1, :]).then_inc(s_acc, 1)
                vec.wait_ge(s_acc, i + (l * ITERS + 1))

            def looked_up(l, s, i):
                vec.wait_ge(s_lc, i * (2 * LOOK[l]) + (LOOKED[l] + (s + 1) * LOOK[l]))

            def gathered(l, s, i):
                vec.wait_ge(s_gat[l][s], (i + 1) * (16 * GATHERED[l]))
                if LOOK[l]:
                    looked_up(l, s, i)

            vec.wait_ge(s_ew, 16)
            vec.wait_ge(s_x, 32)
            split(0)
            first_lookups(0)

            def weighted(i, last):
                for s in range(2):
                    col = i * B + s * T
                    here = slice(s * T, (s + 1) * T)
                    ahead(0, i, s, 0, last)
                    ch.step(vec.tensor_scalar(hilo[0:P, 0, :], dst_i[0:P, bass.ds(col, T)], 7, None, ALU.arith_shift_right))
                    ch.step(vec.tensor_scalar(hilo[0:P, 1, :], dst_i[0:P, bass.ds(col, T)], L - 1, None, ALU.bitwise_and))
                    ch.settle()
                    ch.step(vec.tensor_copy(hilof[0:P, :, :], hilo[0:P, :, :]))
                    ch.settle()
                    ch.step(vec.tensor_tensor(hi_eq[0:P, :, :], iota_l[0:P, 0:H].unsqueeze(1).broadcast_to([P, T, H]),
                                              rep(hilof[0:P, 0, :], [P, T, H]), ALU.is_equal))
                    vec.tensor_tensor(lo_le[0:P, :, :], iota_l[0:P, :].unsqueeze(1).broadcast_to([P, T, L]),
                                      rep(hilof[0:P, 1, :], [P, T, L]), ALU.is_ge).then_inc(s_onehot, 1)
                    looked_up(0, s, i)
                    ahead(0, i, s, 1, last)
                    gathered(0, s, i)
                    vec.tensor_tensor(msg[0:P, here, :], rows0[0:P, here, :],
                                      rep(ew_s[0:P, bass.ds(col, T)], [P, T, D]), ALU.mult).then_inc(s_use[0][s], 1)
                    vec.wait_ge(s_hist, i * 2 + s + 1)
                    ch.step(vec.tensor_tensor(hist[:, :], hist[:, :], bank[0][:, 0:H], ALU.add))
                    ahead(0, i, s, 2, last)
                for s in range(2):
                    vec.wait_ge(s_use[0][s], i + 2)
                scans(i, 0)

            bodies(0, weighted, 2 * 5 + D)

            ch.settle()
            vec.tensor_copy(tot[:, :], hist[:, :]).then_inc(s_tail, 1)
            vec.wait_ge(s_tback, 1)
            ch.step(vec.tensor_copy(tot[:, :], bank[0][:, 64:64 + H]))
            ch.settle()
            ch.step(vec.tensor_tensor_scan(cum[:, :], tot[:, :], zero[:, 0:H], 0.0, ALU.add, ALU.add))
            ch.step(vec.tensor_copy(end_c[:, 0:1], hist[:, 0:1]))
            ch.settle()
            vec.tensor_tensor(end_c[:, 1:H], hist[:, 1:H], cum[:, 0:H - 1], ALU.add).then_inc(s_hidx, 1)
            vec.wait_ge(s_tback, 2)
            vec.tensor_copy(brow[:, :], bank[0][0:H, 128:256]).then_inc(s_tail, 1)
            vec.wait_ge(s_tback, 3)
            ch.step(vec.tensor_copy(cum[:, :], bank[0][:, 256:256 + H]))
            vec.wait_ge(s_bld, 48)
            ch.settle()
            ch.step(vec.tensor_tensor(has[:, :], end_c[:, :], cum[:, :], ALU.is_gt))
            ch.step(vec.tensor_scalar(tot[:, :], end_c[:, :], -1.0, 0.0, ALU.add, ALU.max))
            ch.step(vec.tensor_tensor(cum[:, :], cum[:, :], start_c[:, :], ALU.subtract))
            ch.step(vec.tensor_scalar(spill[0:P, :], spill[0:P, :], edge_end[0:P, 0:1], None, ALU.is_lt))
            ch.settle()
            ch.step(vec.tensor_copy(end_i[:, :], tot[:, :]))
            ch.step(vec.tensor_tensor(cum[:, :], cum[:, :], has[:, :], ALU.mult))
            ch.step(vec.scalar_tensor_tensor(spill[0:P, :], xg[0:P, 0:NPAD], edge_end[0:P, 0:1], spill[0:P, :],
                                             ALU.is_gt, ALU.mult))
            ch.settle()
            vec.tensor_tensor(start_i[:, :], cum[:, :], start_c[:, :], ALU.add).then_inc(s_gidx, 1)

            def weights():
                alpha = 0.25
                vec.wait_ge(s_wts, 16 * len(wlist))
                ch.step(vec.tensor_scalar(wmix[:, M:8 * M], wmix[:, M:8 * M], 1 / math.sqrt(3), None, ALU.mult))
                ch.step(vec.tensor_scalar(wmix[:, 8 * M:12 * M], wmix[:, 8 * M:12 * M], 1 / math.sqrt(6), None, ALU.mult))
                for n, c in ((0, alpha), (1, alpha), (2, alpha / math.sqrt(3)), (3, alpha)):
                    ch.step(vec.tensor_scalar(w2v[:, :, n * M:(n + 1) * M], w2v[:, :, n * M:(n + 1) * M], c, None, ALU.mult))
                ch.step(vec.tensor_scalar(wsi[:, :], wsi[:, :], 1 / math.sqrt(M), None, ALU.mult))
                ch.settle()
                vec.tensor_scalar(wkvq[:, 2 * D:3 * D], wkvq[:, 2 * D:3 * D], 1 / math.sqrt(DH), None, ALU.mult).then_inc(s_scaled, 1)

            weights()

            def summed(l):
                w, cols = SWID[l], SCOL[l]
                rows = ends[:, 0:H * w].rearrange("p (h c) -> p h c", h=H)
                vec.wait_ge(s_end, (l + 1) * H * 16)
                ch.step(vec.tensor_tensor(rows, rows, rep(has[:, :], [L, H, w]), ALU.mult))
                vec.wait_ge(s_spill, l + 1)
                ch.settle()
                for n, (a, b) in enumerate(((0, cols), (cols, H))):
                    ch.step(vec.tensor_tensor(rows[:, a:b, :], rows[:, a:b, :],
                                              bank[1 + n][:, 0:(b - a) * w].rearrange("p (h c) -> p h c", c=w), ALU.add))
                ch.settle()
                return rows

            def layernorm(l):
                ch.settle()
                ch.step(vec.tensor_reduce(stat[:, 0, :], xn[:, :, :], AX.X, ALU.add))
                ch.settle()
                ch.step(vec.tensor_scalar(stat[:, 0, :], stat[:, 0, :], 1 / D, None, ALU.mult))
                ch.settle()
                ch.step(vec.tensor_tensor(centred, xn[:, :, :], rep(stat[:, 0, :], [L, H, D]), ALU.subtract))
                ch.settle()
                ch.step(vec.tensor_tensor(squares, centred, centred, ALU.mult))
                ch.settle()
                ch.step(vec.tensor_reduce(stat[:, 1, :], squares, AX.X, ALU.add))
                ch.settle()
                vec.tensor_scalar(stat[:, 1, :], stat[:, 1, :], 1 / D, EPS, ALU.mult, ALU.add).then_inc(s_var, 1)
                vec.wait_ge(s_std, l + 1)
                ch.step(vec.reciprocal(stat[:, 1, :], stat[:, 0, :]))
                ch.settle()
                vec.tensor_tensor(xn[:, :, :], centred, rep(stat[:, 1, :], [L, H, D]), ALU.mult).then_inc(s_xn, 1)

            rows = summed(0)
            ch.step(vec.tensor_tensor(xn[:, :, :], xn[:, :, :], rows, ALU.add))
            layernorm(0)

            split(1)
            ch.step(vec.memset(carry[:, :], 0.0))
            vec.wait_ge(s_pj, NG)
            vec.wait_ge(s_attr, 4 * 16)
            a, d = math.sqrt(0.1), math.sqrt(1 / 30)
            for j, k, c, f in ((0, 2, 0, a), (2, 0, 0, a), (0, 1, 1, a), (1, 0, 1, a), (1, 1, 2, 2 * d),
                               (1, 2, 3, a), (2, 1, 3, a), (0, 0, 4, -a), (2, 2, 4, a)):
                ch.step(vec.tensor_scalar(quad[0:P, :, 3 * j + k], sh5[0:P, :, c], f, None, ALU.mult))
            ch.settle()
            for jk in (0, 8):
                ch.step(vec.scalar_tensor_tensor(quad[0:P, :, jk], sh5[0:P, :, 2], -d, quad[0:P, :, jk], ALU.mult, ALU.add))
            ch.settle()

            def by3(ap):
                return ap.rearrange("p t (k o) -> p t k o", k=3)

            def mixed(i, last):
                for s in range(2):
                    col = i * B + s * T
                    here = slice(s * T, (s + 1) * T)
                    r, m = rows1[0:P, here, :], msg[0:P, here, :]
                    sh = sh3[0:P, bass.ds(col, T), :]
                    ta, tb = tmp[0:P, :, :], tmp2[0:P, :, :]
                    ch.settle()
                    ch.step(vec.tensor_copy(shx[0:P, :, 0:2], sh[:, :, 1:3]))
                    ch.step(vec.tensor_copy(shx[0:P, :, 2:4], sh[:, :, 0:2]))
                    gathered(1, s, i)
                    ahead(1, i, s, 0, last)
                    ch.step(vec.tensor_tensor(m, r[:, :, 0:4 * M], rep(ew1_s[0:P, bass.ds(col, T)], [P, T, D]), ALU.mult))
                    ch.step(vec.tensor_tensor(by3(ta), by3(r[:, :, 4 * M:7 * M]), rep(sh, [P, T, 3, M]), ALU.mult))
                    ch.step(vec.tensor_tensor(by3(tb), r[:, :, 7 * M:8 * M].unsqueeze(2).broadcast_to([P, T, 3, M]),
                                              rep(sh, [P, T, 3, M]), ALU.mult))
                    ch.settle()
                    ch.step(vec.tensor_reduce(dots[0:P, :, :], ta.rearrange("p t (k o) -> p t o k", k=3), AX.X, ALU.add))
                    ch.step(vec.tensor_tensor(m[:, :, M:D], m[:, :, M:D], tb, ALU.add))
                    ch.settle()
                    ch.step(vec.tensor_tensor(m[:, :, 0:M], m[:, :, 0:M], dots[0:P, :, :], ALU.add))
                    ahead(1, i, s, 1, last)
                    ch.step(vec.tensor_tensor(by3(ta), by3(r[:, :, 9 * M:12 * M]), rep(shx[0:P, :, 0:3], [P, T, 3, M]), ALU.mult))
                    ch.step(vec.tensor_tensor(by3(tb), by3(r[:, :, 8 * M:11 * M]), rep(shx[0:P, :, 1:4], [P, T, 3, M]), ALU.mult))
                    ch.settle()
                    ch.step(vec.tensor_tensor(m[:, :, M:D], m[:, :, M:D], ta, ALU.add))
                    ch.settle()
                    ch.step(vec.tensor_tensor(m[:, :, M:D], m[:, :, M:D], tb, ALU.subtract))
                    for j in range(3):
                        t_ = ta if j % 2 == 0 else tb
                        g5 = r[:, :, (12 + j) * M:(13 + j) * M].unsqueeze(2).broadcast_to([P, T, 3, M])
                        q3 = rep(quad[0:P, bass.ds(col, T), 3 * j:3 * j + 3], [P, T, 3, M])
                        if j < 2:
                            ch.step(vec.tensor_tensor(by3(t_), g5, q3, ALU.mult))
                            ch.settle()
                        else:
                            vec.tensor_tensor(by3(t_), g5, q3, ALU.mult).then_inc(s_use[1][s], 1)
                            vec.wait_ge(s_use[1][s], i + 2)
                        ch.step(vec.tensor_tensor(m[:, :, M:D], m[:, :, M:D], t_, ALU.add))
                ch.settle()
                scans(i, 1)

            first_lookups(1)
            bodies(1, mixed, 2 * 17 + D)

            def add_swapped(rows):
                ch.step(vec.tensor_tensor(xn[:, :, 0:M], xn[:, :, 0:M], rows[:, :, 0:M], ALU.add))
                ch.step(vec.tensor_tensor(xn[:, :, M:D].rearrange("p h (o k) -> p h k o", k=3),
                                          xn[:, :, M:D].rearrange("p h (o k) -> p h k o", k=3),
                                          rows[:, :, M:D].rearrange("p h (k o) -> p h k o", k=3), ALU.add))

            rows = summed(1)
            add_swapped(rows)
            layernorm(1)

            ch.step(vec.memset(carry[:, :], 0.0))
            ch.settle()
            def weighed(i, last):
                for s in range(2):
                    col = i * B + s * T
                    here = slice(s * T, (s + 1) * T)
                    r, m, w, pr, rd = rows0[0:P, here, :], msg[0:P, here, :], wide[0:P], prod[0:P], red[0:P, :, :]
                    v = r[:, :, M:D].rearrange("p t (i m) -> p t i m", m=3)
                    sh0 = sh4[0:P, bass.ds(col, T), 0]
                    sh1 = sh4[0:P, bass.ds(col, T), 1:4]
                    gathered(2, s, i)
                    ch.settle()
                    ch.step(vec.tensor_tensor(tmp[0:P, :, :].rearrange("p t (i m) -> p t i m", m=3), v,
                                              sh1.unsqueeze(2).broadcast_to([P, T, M, 3]), ALU.mult))
                    ch.settle()
                    ch.step(vec.tensor_reduce(dots[0:P, :, :], tmp[0:P, :, :].rearrange("p t (i m) -> p t i m", m=3), AX.X, ALU.add))
                    ch.settle()
                    vec.wait_ge(s_wc, i * (2 * PAIRS) + (s + 1) * PAIRS)
                    ch.step(vec.tensor_tensor(pr[:, :, :, 0:2 * M], w[:, :, :, 0:2 * M], rep(r[:, :, 0:M], [P, T, M, 2 * M]), ALU.mult))
                    ch.step(vec.tensor_tensor(pr[:, :, :, 2 * M:3 * M], w[:, :, :, 2 * M:3 * M], rep(dots[0:P, :, :], [P, T, M, M]), ALU.mult))
                    for k in range(2):
                        ch.step(vec.tensor_tensor(pr[:, :, :, (3 + k) * M:(4 + k) * M], w[:, :, :, 3 * M:4 * M],
                                                  rep(v[:, :, :, k], [P, T, M, M]), ALU.mult))
                    vec.tensor_tensor(pr[:, :, :, 5 * M:6 * M], w[:, :, :, 3 * M:4 * M],
                                      rep(v[:, :, :, 2], [P, T, M, M]), ALU.mult).then_inc(s_use[2][s], 1)
                    vec.wait_ge(s_use[2][s], i + 2)
                    ch.step(vec.tensor_reduce(rd, pr.rearrange("p t i c -> p t c i"), AX.X, ALU.add))
                    ch.settle()
                    ch.step(vec.tensor_tensor(m[:, :, 0:M], rd[:, :, 0:M], rep(sh0, [P, T, M]), ALU.mult))
                    ch.step(vec.tensor_tensor(m[:, :, M:D], rd[:, :, 3 * M:6 * M], rep(sh0, [P, T, 3 * M]), ALU.mult))
                    ch.step(vec.tensor_tensor(by3(tmp2[0:P, :, :]), rd[:, :, M:2 * M].unsqueeze(2).broadcast_to([P, T, 3, M]),
                                              rep(sh1, [P, T, 3, M]), ALU.mult))
                    ch.settle()
                    ch.step(vec.tensor_tensor(m[:, :, 0:M], m[:, :, 0:M], rd[:, :, 2 * M:3 * M], ALU.add))
                    ch.step(vec.tensor_tensor(m[:, :, M:D], m[:, :, M:D], tmp2[0:P, :, :], ALU.add))
                ch.settle()
                scans(i, 2)

            first_lookups(2)
            bodies(2, weighed, 2 * 12 + D)

            rows = summed(2)
            add_swapped(rows)
            ch.settle()
            vec.wait_ge(s_pc, 2 * NG)
            ch.step(vec.tensor_tensor(xn[:, :, :], xn[:, :, :], si_s[:, :, :], ALU.add))
            layernorm(2)

            split(3)
            ch.step(vec.memset(carry[:, :], 0.0))
            ch.step(vec.memset(neg[:, :], 0.0))
            ch.settle()
            ch.step(vec.tensor_scalar(neg[0:P, 0:TE], keep[0:P, :], -1.0, BIG, ALU.add, ALU.mult))
            vec.wait_ge(s_qg, 16)
            def scored(i, last):
                vec.wait_ge(s_ql, i * 16 + 16)
                for f in range(D):
                    ch.step(vec.tensor_tensor_scan(qe[0:P, :, f], keep[0:P, bass.ds(i * B, B)], qs[0:P, :, f],
                                                   qcarry[0:P, f:f + 1], ALU.mult, ALU.add))
                ch.settle()
                vec.tensor_copy(qcarry[0:P, :], qe[0:P, B - 1, :]).then_inc(s_qu, 1)
                vec.wait_ge(s_qu, i + 1)
                ch.step(vec.memset(beforef[:, 3:4], 0.0))
                for s in range(2):
                    here = slice(s * T, (s + 1) * T)
                    ahead(3, i, s, 0, last)
                    looked_up(3, s, i)
                    gathered(3, s, i)
                    ch.step(vec.tensor_tensor(rows3[0:P, here, 0:D], rows3[0:P, here, 0:D], qe[0:P, here, :], ALU.mult))
                    ahead(3, i, s, 1, last)
                    ch.settle()
                    vec.tensor_reduce(sc[0:P, :, bass.ds(i * B + s * T, T)].rearrange("p h t -> p t h"),
                                      rows3[0:P, here, 0:D].rearrange("p t (h d) -> p t h d", h=HEADS),
                                      AX.X, ALU.add).then_inc(s_use[3][s], 1)
                    ahead(3, i, s, 2, last)

            first_lookups(3)
            bodies(3, scored, D + 1 + 2)

            for s in range(2):
                vec.wait_ge(s_use[3][s], ITERS + 1)

            def maxima(first_f, first_b):
                for h in range(HEADS):
                    ch.step(vec.tensor_tensor_scan(fwd[0:P, h, :], neg[0:P, 0:TE], sc[0:P, h, :],
                                                   first_f(h), ALU.add, ALU.max))
                    ch.step(vec.tensor_tensor_scan(bwd[0:P, h, ::-1], neg[0:P, TE:0:-1], sc[0:P, h, ::-1],
                                                   first_b(h), ALU.add, ALU.max))

            for s in range(2):
                vec.wait_ge(s_val[s], ITERS + 1)
            maxima(lambda h: -BIG, lambda h: -BIG)
            ch.step(vec.tensor_reduce(stretch[0:P, :], keep[0:P, :], AX.X, ALU.min))
            ch.settle()
            ch.step(vec.tensor_copy(packed[0:P, 0, :], fwd[0:P, :, TE - 1]))
            ch.step(vec.tensor_copy(packed[0:P, 1, :], bwd[0:P, :, 0]))
            ch.step(vec.tensor_copy(packed[0:P, 2, :], stretch[0:P, 0:1].broadcast_to([P, HEADS])))
            ch.step(vec.memset(fT[:, :, :], -BIG))
            ch.settle()
            vec.tensor_copy(packed[0:P, 3, :], keep[0:P, 0:1].broadcast_to([P, HEADS])).then_inc(s_tail, 1)
            vec.wait_ge(s_tback, 4)
            pk = bank[0][0:HEADS, :].rearrange("p (a c) -> p a c", a=4)
            ch.step(vec.tensor_copy(fT[:, 0:2, 0:P], pk[:, 0:2, 0:P]))
            ch.step(vec.tensor_scalar(fT[:, 2:4, 0:P], pk[:, 2:4, 0:P], -1.0, BIG, ALU.add, ALU.mult))
            ch.settle()
            ch.step(vec.tensor_tensor_scan(fT[:, 4, 1:P + 1], fT[:, 2, 0:P], fT[:, 0, 0:P], -BIG, ALU.add, ALU.max))
            ch.step(vec.tensor_tensor(fT[:, 2, 0:P], fT[:, 2, 0:P], fT[:, 3, 1:P + 1], ALU.add))
            ch.settle()
            ch.step(vec.tensor_tensor_scan(fT[:, 5, P - 1::-1], fT[:, 2, P - 1::-1], fT[:, 1, P - 1::-1], -BIG, ALU.add, ALU.max))
            ch.settle()
            vec.tensor_tensor(fT[:, 6, 0:P], fT[:, 5, 1:P + 1], fT[:, 3, 1:P + 1], ALU.add).then_inc(s_tail, 1)
            vec.wait_ge(s_tback, 5)
            ch.step(vec.tensor_copy(inits[0:P, :], bank[0][0:P, 0:2 * HEADS]))
            ch.settle()
            maxima(lambda h: inits[0:P, h:h + 1], lambda h: inits[0:P, HEADS + h:HEADS + h + 1])
            ch.settle()
            ch.step(vec.tensor_tensor(fwd[0:P], fwd[0:P], bwd[0:P], ALU.max))
            ch.settle()
            vec.tensor_tensor(sc[0:P], sc[0:P], fwd[0:P], ALU.subtract).then_inc(s_max, 1)
            ch.step(vec.memset(accs[1][:, EB - 1, :], 0.0))
            ch.settle()

            vec.wait_ge(s_exp, 1)
            def weighted_values(i):
                for s in range(2):
                    cols = bass.ds((i * 2 + s) * EB, EB)
                    for h in range(HEADS):
                        ch.step(vec.tensor_tensor(vals[0:P, cols, h * DH:(h + 1) * DH], vals[0:P, cols, h * DH:(h + 1) * DH],
                                                  rep(sc[0:P, h, cols], [P, EB, DH]), ALU.mult))
                    ch.settle()
                    if not isinstance(i, int):
                        vec.wait_ge(s_sum3[s], i * 16)
                    for f in range(RW):
                        val = vals[0:P, cols, f] if f < D else sc[0:P, f - D, cols]
                        scan = vec.tensor_tensor_scan(accs[s][0:P, :, f], keep[0:P, cols], val,
                                                      accs[1 - s][0:P, EB - 1, f:f + 1], ALU.mult, ALU.add)
                        if f < RW - 1:
                            ch.step(scan)
                        else:
                            scan.then_inc(s_acc3[s], 1)
                            vec.wait_ge(s_acc3[s], i + 1)

            weighted_values(0)
            with vec.Fori(1, TE // EB // 2) as i:
                ch.enter(i, 2 * (HEADS + RW - 1), 1)
                weighted_values(i)
            ch.leave(TE // EB // 2 - 1)

            rows = summed(3)
            den = rows[:, :, D:RW]
            ch.step(vec.tensor_scalar(den, den, 1e-16, None, ALU.max))
            ch.settle()
            ch.step(vec.reciprocal(den, den))
            ch.settle()
            for h in range(HEADS):
                o = vec.tensor_tensor(si_s[:, :, h * DH:(h + 1) * DH], rows[:, :, h * DH:(h + 1) * DH],
                                      rep(rows[:, :, D + h], [L, H, DH]), ALU.mult)
                if h < HEADS - 1:
                    ch.step(o)
                else:
                    o.then_inc(s_attn, 1)
            vec.wait_ge(s_pc, 4 * NG)
            ch.step(vec.scalar_tensor_tensor(xn[:, :, :], xn[:, :, :], 2.0, si_s[:, :, :], ALU.mult, ALU.add))
            layernorm(3)

        @block.tensor
        def _(pe):
            def spilled(l):
                w, cols = SWID[l], SCOL[l]
                if l < 3:
                    pe.wait_ge(s_acc, (l + 1) * ITERS)
                    state = carry[0:P, 0:D]
                else:
                    pe.wait_ge(s_acc3[1], TE // EB // 2)
                    state = accs[1][0:P, EB - 1, :]
                for h in range(H):
                    n, c = (0, h) if h < cols else (1, h - cols)
                    last = pe.matmul(bank[1 + n][:, c * w:(c + 1) * w], spill[0:P, h * L:(h + 1) * L], state,
                                     start=True, stop=True)
                last.then_inc(s_spill, 1)

            def candidates(l, i, s, g):
                n = i * (2 * LOOK[l]) + (LOOKED[l] + s * LOOK[l] + g)
                for half, (a0, a1) in enumerate(((0, 4), (4, A))):
                    pe.wait_ge(s_oh, n * 2 + half + 1)
                    for a in range(a0, a1):
                        for k in range(S):
                            last = pe.matmul(bank[3][:, 0:Q * P], parts[:, a, k, :], onehot[:, a, :],
                                             start=(a == 0 and k == 0), stop=(a == A - 1 and k == S - 1))
                last.then_inc(s_lk, 1)

            def turned_rows(l, i, s, g):
                n = i * (2 * LOOK[l]) + (LOOKED[l] + s * LOOK[l] + g)
                pe.wait_ge(s_mk, n + 1)
                w = stacks[l].shape[1]
                for j in range(Q):
                    last = pe.matmul(bank[5 + (s * LOOK[l] + g) % 2][0:P, j * w:(j + 1) * w], masked[:, j * P:(j + 1) * P],
                                     stacks[l][:, :], start=True, stop=True)
                last.then_inc(s_lp, 1)

            def lookups(l):
                pe.wait_ge(s_parts, (1, 2, 0, 3)[l])
                if l:
                    with pe.Fori(0, ITERS) as i:
                        for s in range(2):
                            for g in range(LOOK[l]):
                                candidates(l, i, s, g)
                                turned_rows(l, i, s, g)
                    return
                for g in range(LOOK[0]):
                    candidates(0, 0, 0, g)
                    turned_rows(0, 0, 0, g)

                def step(i, s, i1, s1):
                    candidates(0, i1, s1, 0)
                    count(i, s)
                    turned_rows(0, i1, s1, 0)
                    candidates(0, i1, s1, 1)
                    turned_rows(0, i1, s1, 1)

                with pe.Fori(0, ITERS - 1) as i:
                    step(i, 0, i, 1)
                    step(i, 1, i + 1, 0)
                step(ITERS - 1, 0, ITERS - 1, 1)
                count(ITERS - 1, 1)

            def project(call, rows, weights):
                w = PROJ[call]
                for g in range(NG + 1):
                    if g < NG:
                        if g >= 2:
                            pe.wait_ge(s_tc, call * NG + g - 1)
                        for k in range(min(4, H - 4 * g)):
                            last = pe.transpose(bank[3 + g % 2][0:D, k * L:(k + 1) * L], rows[:, 4 * g + k, :], ident[:, :])
                        last.then_inc(s_tp, 1)
                    if g:
                        j = g - 1
                        pe.wait_ge(s_tc, call * NG + j + 1)
                        if j >= 2:
                            pe.wait_ge(s_pc, call * NG + j - 1)
                        for k in range(min(4, H - 4 * j)):
                            h = 4 * j + k
                            last = pe.matmul(bank[5 + j % 2][:, k * w:(k + 1) * w], xT[0:D, h * L:(h + 1) * L], weights,
                                             start=True, stop=True)
                        last.then_inc(s_pj, 1)

            pe.wait_ge(s_const, 2)
            pe.wait_ge(s_rcf, 1)
            for b in range(8):
                if b >= 2:
                    pe.wait_ge(s_rcc, 2 * (b - 1))
                for a in range(2):
                    pe.transpose(bank[5 + b % 2][0:100, a * 128:a * 128 + P], src_f[0:P, 1 + a, b * 100:(b + 1) * 100],
                                 ident[0:P, 0:P]).then_inc(s_rct, 1)

            def count(i, s):
                pe.wait_ge(s_onehot, i * 2 + s + 1)
                for t in range(T):
                    last = pe.matmul(bank[0][:, 0:H], lo_le[0:P, t, :], hi_eq[0:P, t, :], start=(t == 0), stop=(t == T - 1))
                last.then_inc(s_hist, 1)

            lookups(0)
            pe.wait_ge(s_tail, 1)
            pe.matmul(bank[0][:, 64:64 + H], last_l[:, :], tot[:, :], start=True, stop=True).then_inc(s_tback, 1)
            pe.wait_ge(s_hidx, 1)
            pe.transpose(bank[0][0:H, 128:256], end_c[:, :], ident[:, :]).then_inc(s_tback, 1)
            pe.wait_ge(s_bld, 48)
            pe.transpose(bank[0][:, 256:256 + H], brow[:, :], ident[0:H, 0:H]).then_inc(s_tback, 1)
            pe.wait_ge(s_gidx, 1)
            spilled(0)
            pe.wait_ge(s_scaled, 1)
            pe.wait_ge(s_xn, 1)
            project(0, xn, wmix[:, :])
            pe.wait_ge(s_stk, 16 * 8)
            lookups(1)
            spilled(1)
            pe.wait_ge(s_xn, 2)
            project(1, xn, wsi[:, :])

            pe.wait_ge(s_tc, 2 * NG)
            pe.wait_ge(s_pc, 2 * NG)
            with pe.Fori(0, ITERS) as i:
                for s in range(2):
                    pe.wait_ge(s_ef[s], i * 16 + 16)
                    for g in range(TQ):
                        place = bank[3][:, g * P:(g + 1) * P] if g < 4 else bank[4][:, 0:P]
                        last = pe.transpose(place, ef[0:P, s, g * 4 * D:(g + 1) * 4 * D], ident[0:P, 0:P])
                    last.then_inc(s_eft[s], 1)
                    pe.wait_ge(s_efc, i * 4 + 2 * s + 2)
                    for k in range(Q):
                        if k >= 2:
                            pe.wait_ge(s_hc, i * 10 + (5 * s + k - 1))
                        pe.matmul(bank[5 + k % 2][:, 0:4 * P], w1blk[:, k, :], efT[:, 0:4 * P], start=True, stop=True).then_inc(s_hp, 1)
                    for k in range(Q):
                        last = pe.matmul(bank[3][:, k * P:(k + 1) * P], w1blk[:, k, :], efT[:, 4 * P:5 * P], start=True, stop=True)
                    last.then_inc(s_hp, 1)
                    pe.wait_ge(s_hc, i * 10 + (5 * s + 5))
                    for j in range(PAIRS):
                        if j >= 4:
                            pe.wait_ge(s_wc, i * (2 * PAIRS) + (s * PAIRS + j - 3))
                        for r in range(2):
                            g, k = divmod(2 * j + r, Q)
                            h_ = hid[:, k, g * P:(g + 1) * P] if g < 4 else hid_last[:, k, :]
                            last = pe.matmul(bank[WBANKS[(s * PAIRS + j) % 4]][0:P, r * 256:(r + 1) * 256], h_, w2[:, :],
                                             start=True, stop=True)
                        last.then_inc(s_wp, 1)
            pe.wait_ge(s_wc, ITERS * 2 * PAIRS)
            spilled(2)
            pe.wait_ge(s_xn, 3)
            project(2, xn, wkvq[:, :])

            lookups(3)

            pe.wait_ge(s_tail, 3)
            for k in range(4):
                last = pe.transpose(bank[0][0:HEADS, k * 128:k * 128 + P], packed[0:P, k, :], ident[0:P, 0:P])
            last.then_inc(s_tback, 1)
            pe.wait_ge(s_tail, 4)
            pe.transpose(bank[0][0:P, 0:HEADS], fT[:, 4, 0:P], ident[0:HEADS, 0:HEADS])
            pe.transpose(bank[0][0:P, HEADS:2 * HEADS], fT[:, 6, 0:P], ident[0:HEADS, 0:HEADS]).then_inc(s_tback, 1)
            spilled(3)
            pe.wait_ge(s_attn, 1)
            project(3, si_s, wos[:, :])

        @block.scalar
        def _(act):
            act.dma_start(ew1_s[0:P, :], ew1.rearrange("(p t) c -> p (t c)", p=P)).then_inc(s_attr, 16)
            act.dma_start(sh3_flat[0:P, :], ea3.rearrange("(p t) c -> p (t c)", p=P)).then_inc(s_attr, 16)
            act.dma_start(sh4_flat[0:P, :], ea4.rearrange("(p t) c -> p (t c)", p=P)).then_inc(s_attr, 16)
            act.dma_start(sh5_flat[0:P, :], ea5.rearrange("(p t) c -> p (t c)", p=P)).then_inc(s_attr, 16)
            for b in range(8):
                act.wait_ge(s_rct, 2 * b + 2)
                for a in range(2):
                    act.copy(turned[0:100, b, a, :], bank[5 + b % 2][0:100, a * 128:a * 128 + P]).then_inc(s_rcc, 1)
            act.wait_ge(s_wclr, 7)
            act.dma_start(xn[:, 0:HF, :], x[0:L * HF, :].rearrange("(h l) c -> l h c", l=L)).then_inc(s_x, 16)
            act.dma_start(xn[0:REST, HF, :], x[L * HF:N, :]).then_inc(s_x, 16)
            for place, weights in wlist:
                act.dma_start(place, weights, allow_slow_non_contiguous=True).then_inc(s_wts, 16)
            act.wait_ge(s_zero, 1)
            cleared = qstart[0:E, :].rearrange("(p t) c -> p (t c)", p=P)
            for r in range(ZERO_DMAS):
                act.dma_start(cleared[:, r * 800:(r + 1) * 800], zero[0:P, :]).then_inc(s_qz, 16)


            def copies(l, i, s):
                for g in range(LOOK[l]):
                    w = stacks[l].shape[1]
                    n = i * (2 * LOOK[l]) + (LOOKED[l] + s * LOOK[l] + g)
                    t = s * T + GATHERED[l] + g * Q
                    act.wait_ge(s_use[l][s], i + 1)
                    act.wait_ge(s_lp, n + 1)
                    act.copy([rows0, rows1, None, rows3][l][0:P, t:t + Q, :],
                             bank[5 + (s * LOOK[l] + g) % 2][0:P, 0:Q * w].rearrange("p (t c) -> p t c", c=w)).then_inc(s_lc, 1)

            def root(l):
                act.wait_ge(s_var, l + 1)
                act.activation(stat[:, 0, :], stat[:, 1, :], ACT.Sqrt).then_inc(s_std, 1)

            def evacuate(call):
                w = PROJ[call]
                for g in range(NG + 1):
                    if g < NG:
                        n = min(4, H - 4 * g)
                        act.wait_ge(s_tp, call * NG + g + 1)
                        act.copy(xT[0:D, 4 * g * L:(4 * g + n) * L], bank[3 + g % 2][0:D, 0:n * L]).then_inc(s_tc, 1)
                    if g:
                        j = g - 1
                        n = min(4, H - 4 * j)
                        hs = slice(4 * j, 4 * j + n)
                        got = bank[5 + j % 2][:, 0:n * w].rearrange("p (h c) -> p h c", c=w)
                        act.wait_ge(s_pj, call * NG + j + 1)
                        if call == 0:
                            act.copy(nodeout[:, hs, :], got).then_inc(s_pc, 1)
                        elif call == 2:
                            act.copy(kvout[:, hs, :], got[:, :, 0:KV])
                            act.copy(qout[:, hs, :], got[:, :, KV:3 * D]).then_inc(s_pc, 1)
                        else:
                            act.copy(si_s[:, hs, :], got).then_inc(s_pc, 1)

            with act.Fori(0, ITERS) as i:
                for s in range(2):
                    copies(0, i, s)
            act.wait_ge(s_scaled, 1)
            for c in range(C):
                act.dma_start(stack_mix[c * D:(c + 1) * D, :], wmix[:, :]).then_inc(s_stk, 16)
                act.dma_start(stack_kv[c * D:(c + 1) * D, :], wkvq[:, 0:KV]).then_inc(s_stk, 16)
            root(0)
            evacuate(0)
            with act.Fori(0, ITERS) as i:
                for s in range(2):
                    copies(1, i, s)
            root(1)
            evacuate(1)
            with act.Fori(0, ITERS) as i:
                for s in range(2):
                    act.wait_ge(s_eft[s], i + 1)
                    act.copy(efT[:, 0:4 * P], bank[3][:, 0:4 * P]).then_inc(s_efc, 1)
                    act.copy(efT[:, 4 * P:5 * P], bank[4][:, 0:P]).then_inc(s_efc, 1)
                    for k in range(Q):
                        act.wait_ge(s_hp, i * 10 + (5 * s + k + 1))
                        act.activation(hid[:, k, :], bank[5 + k % 2][:, 0:4 * P], ACT.Relu, bias=b1[:, 0:1]).then_inc(s_hc, 1)
                    act.wait_ge(s_hp, i * 10 + (5 * s + 5))
                    act.activation(hid_last, bank[3][:, 0:4 * P].rearrange("p (k e) -> p k e", k=Q), ACT.Relu,
                                   bias=b1[:, 0:1]).then_inc(s_hc, 1)
                    act.wait_ge(s_use[2][1 - s], i + (1 + s))
                    for j in range(PAIRS):
                        act.wait_ge(s_wp, i * (2 * PAIRS) + (s * PAIRS + j + 1))
                        act.copy(wide[0:P, 2 * j:2 * j + 2, :, :].rearrange("p t i c -> p (t i c)"),
                                 bank[WBANKS[(s * PAIRS + j) % 4]][0:P, :]).then_inc(s_wc, 1)
            root(2)
            evacuate(2)
            def keep_values(i, s):
                act.wait_ge(s_gat[3][s], (i + 1) * (16 * GATHERED[3]))
                act.wait_ge(s_lc, i * (2 * LOOK[3]) + (LOOKED[3] + (s + 1) * LOOK[3]))
                act.copy(vals[0:P, bass.ds(i * B + s * T, T), :], rows3[0:P, s * T:(s + 1) * T, D:KV]).then_inc(s_val[s], 1)

            copies(3, 0, 0)
            with act.Fori(0, ITERS - 1) as i:
                keep_values(i, 0)
                copies(3, i, 1)
                keep_values(i, 1)
                copies(3, i + 1, 0)
            keep_values(ITERS - 1, 0)
            copies(3, ITERS - 1, 1)
            keep_values(ITERS - 1, 1)
            act.wait_ge(s_max, 1)
            act.activation(sc[0:P], sc[0:P], ACT.Exp).then_inc(s_exp, 1)
            evacuate(3)
            root(3)


_INS = ['x', 'src', 'dst', 'edge_attr_3', 'edge_attr_32', 'edge_attr_4', 'edge_attr_5', 'edge_weight', 'edge_weight1',
        'L1_gnn_W', 'L2_gnn_W1', 'L2_gnn_b1', 'L2_gnn_W2', 'L2_gnn_b2', 'L2_gnn_si_w0', 'L2_gnn_si_w1',
        'L3_gnn_Wq', 'L3_gnn_Wk', 'L3_gnn_Wv', 'L3_gnn_Wo']


def kernel(**inputs):
    import numpy as _np
    import concourse.bacc as _bacc
    from concourse import mybir as _mybir
    from concourse.bass_utils import run_bass_kernel_spmd as _run

    nc = _bacc.Bacc("TRN2", target_bir_lowering=False, num_devices=1)
    arrays, args = {}, []
    for name in _INS:
        a = _np.ascontiguousarray(inputs[name])
        arrays[f"in_{name}_dram"] = a
        args.append(nc.dram_tensor(f"in_{name}_dram", a.shape, _mybir.dt.from_np(a.dtype), kind="ExternalInput").ap())
    out = nc.dram_tensor("out_0_dram", (N, D), F32, kind="ExternalOutput").ap()
    gnn_kernel(nc, *args, out)
    r = _run(nc, [arrays], core_ids=[0])
    return r.results[0]["out_0_dram"]
```

```python
from contextlib import ExitStack
import math

import numpy as np
import concourse.bass as bass
from concourse import mybir

F32 = mybir.dt.float32
I32 = mybir.dt.int32
BF16 = mybir.dt.bfloat16
ALU = mybir.AluOpType
ACT = mybir.ActivationFunctionType
AX = mybir.AxisListType

N, E, D = 3125, 100000, 32
P = 125
TE = E // P
T = 20
B = 2 * T
BX = B + 1
ITERS = TE // B
L = 128
H = -(-N // L)
NPAD = L * H
HF = N // L
REST = N - L * HF
M = 8
HEADS, DH = 4, 8
HID = 64
GW = 15 * M
KV = 2 * D
RW = D + HEADS
EB = 50
EX, BLOCKS = EB + 1, TE // EB
EPS = 1e-5
A, C, S = 7, 4, 3
Q = 4
LOOK = [(2, 2), (2, 1), (0, 0), (2, 2)]
PER = [sum(g) for g in LOOK]
LOOKED = [ITERS * sum(PER[:l]) for l in range(5)]
GATHERED = [[T - Q * g for g in halves] for halves in LOOK]
F16 = mybir.dt.float16
K = 32
NB, TB = E // K, TE // K
BIG = 1e30
DUMP = E


def group(l, i, s, g):
    return i * PER[l] + (LOOKED[l] + sum(LOOK[l][:s]) + g)


def slot_of(l, s, g):
    js = list(range(PER[l]))
    j = sum(LOOK[l][:s]) + g
    slots = [k % 2 for k in js] * 2
    back = max(k for k in range(PER[l] + j) if slots[k] == slots[PER[l] + j])
    return j % 2, PER[l] + j - back


class Chain:

    def __init__(self, eng, sem):
        self.eng, self.sem, self.count, self.loop = eng, sem, 0, None

    def step(self, inst):
        inst.then_inc(self.sem, 1)
        self.count += 1

    def settle(self):
        if self.loop:
            i, per, first, _ = self.loop
            self.eng.wait_ge(self.sem, (i - first) * per + self.count)
        else:
            self.eng.wait_ge(self.sem, self.count)

    def enter(self, i, per, first=0):
        self.loop = (i, per, first, self.count)

    def leave(self, iters):
        _, per, _, base = self.loop
        assert self.count - base == per, (self.count - base, per)
        self.count, self.loop = base + iters * per, None


def gnn_kernel(nc, x, src, dst, ea3, ea32, ea4, ea5, ew, ew1, w_tp, w_mlp1, b_mlp1, w_mlp2,
               b_mlp2, si0, si1, wq, wk, wv, wo, out):
    ctx = ExitStack()
    with ctx:
        def sb(name, shape, dt=F32):
            return ctx.enter_context(nc.sbuf_tensor(name, shape, dt))

        def sem(name):
            return ctx.enter_context(nc.semaphore(name))

        def dram(name, shape, dt=F32):
            return nc.dram_tensor(name, shape, dt).ap()

        node_g = dram("node_g", (NPAD, GW))
        node_x = dram("node_x", (NPAD, D))
        node_kv = dram("node_kv", (NPAD, KV))
        node_q = dram("node_q", (NPAD, D))
        qstart = dram("qstart", (E + NPAD, D))
        sums = dram("sums", (E, D))
        sums3 = dram("sums3", (E, RW))
        rcrow = dram("rcrow", (2, E), F16)
        bounds = dram("bounds", (1, NPAD + 1))

        big = sb("big", [128, 25600])
        at = 0
        wide = big[:, 0:T * 4 * M * M].rearrange("p (t i c) -> p t i c", t=T, i=M)
        at += T * 4 * M * M
        prod = big[:, at:at + T * M * 48].rearrange("p (t i c) -> p t i c", t=T, i=M)
        at += T * M * 48
        sh4 = big[:, at:at + TE * 4].rearrange("p (t c) -> p t c", c=4)
        sh4_flat = big[:, at:at + TE * 4]
        at += TE * 4
        ew_s = big[:, at:at + TE]
        at += TE
        ew1_s = big[:, at:at + TE]
        at += TE
        ef = big[:, at:at + 2 * T * D].rearrange("p (s n) -> p s n", s=2)
        at += 2 * T * D
        efT = big[:, at:at + T // 4 * P]
        at += T // 4 * P
        hid_last = big[:, at:at + Q * P].rearrange("p (k e) -> p k e", k=Q)
        at += Q * P
        sh5_flat = big[:, at:at + TE * 5]
        sh5 = sh5_flat.rearrange("p (t c) -> p t c", c=5)
        at += TE * 5
        zero = big[:, at:at + 800]
        at += 800
        assert at <= 25600
        lo_le = big[:, 0:TB * L // 2].bitcast(BF16).rearrange("p (t c) -> p t c", c=L)
        hi_eq = big[:, 1600:1600 + TB * H // 2 + 1].bitcast(BF16)[:, 0:TB * H].rearrange("p (t c) -> p t c", c=H)
        next_b = big[:, 6400:6400 + NPAD]
        block_i = big[:, 9600:9600 + H * K].bitcast(I32).rearrange("p (h k) -> p h k", k=K)
        block_f = big[:, 10400:10400 + H * K].rearrange("p (h k) -> p h k", k=K)
        src_f = big[:, 2000:2000 + 3 * TE].rearrange("p (a t) -> p a t", a=3)
        src_i = big[:, 4400:4400 + TE].bitcast(I32)
        turned = big[:, 5200:5200 + 8 * P].bitcast(F16).rearrange("p (b a e) -> p b a e", b=8, a=2)
        quad = big[:, 0:9 * TE].rearrange("p (t c) -> p t c", c=9)
        xT = big[:, 0:NPAD]
        vals = big[:, :].rearrange("p (t c) -> p t c", c=D)

        xg = sb("xg", [128, B * GW])
        rows0 = xg[:, 0:B * D].rearrange("p (t c) -> p t c", c=D)
        rows1 = xg[:, :].rearrange("p (t c) -> p t c", c=GW)
        rows3 = xg[:, 0:B * KV].rearrange("p (t c) -> p t c", c=KV)
        nodeout = xg[:, 0:H * GW].rearrange("p (h c) -> p h c", h=H)
        kvout = xg[:, 0:H * KV].rearrange("p (h c) -> p h c", h=H)
        qout = xg[:, H * KV:H * (KV + D)].rearrange("p (h c) -> p h c", h=H)
        centred = xg[:, 3000:3000 + H * D].rearrange("p (h c) -> p h c", h=H)
        squares = xg[:, 3800:3800 + H * D].rearrange("p (h c) -> p h c", h=H)
        ends = xg[:, 0:H * RW]
        si_s = xg[:, 1280:1280 + H * D].rearrange("p (h c) -> p h c", h=H)
        fwd = xg[:, 0:HEADS * TE].rearrange("p (h t) -> p h t", h=HEADS)

        acc2 = sb("acc2", [128, 2 * EB * RW])
        acc_flat = acc2[:, 0:D * BX]
        acc = acc_flat.rearrange("p (f t) -> p f t", f=D)
        accs = [acc2[:, s * EB * RW:(s + 1) * EB * RW].rearrange("p (t c) -> p t c", c=RW) for s in range(2)]
        OHW, AT1 = A * Q * P // 2, D * BX

        def as_onehot(ap):
            return ap.bitcast(BF16).rearrange("p (a e) -> p a e", a=A)

        onehot0, masked0 = as_onehot(acc2[:, AT1:AT1 + OHW]), acc2[:, AT1 + OHW:AT1 + OHW + Q * P]
        onehots_of = [[onehot0, as_onehot(xg[:, 2560:2560 + OHW])], [onehot0, as_onehot(big[:, 7200:7200 + OHW])], None,
                      [onehot0, as_onehot(xg[:, 2560:2560 + OHW])]]
        hid = acc2[:, AT1:AT1 + 16 * P].rearrange("p (k n) -> p k n", k=Q)
        bwd = acc2[:, 0:HEADS * TE].rearrange("p (h t) -> p h t", h=HEADS)

        work = sb("work", [128, 2 * B * D])
        msgT_flat = work[:, 0:D * BX]
        msgT = msgT_flat.rearrange("p (f t) -> p f t", f=D)
        msg = msgT_flat.rearrange("p (f t) -> p t f", f=D)[:, 1:BX, :]
        tmp = work[:, AT1:AT1 + T * 24].rearrange("p (t c) -> p t c", c=24)
        tmp2 = work[:, AT1 + T * 24:AT1 + 2 * T * 24].rearrange("p (t c) -> p t c", c=24)
        shx = work[:, AT1 + 2 * T * 24:AT1 + 2 * T * 24 + 4 * T].rearrange("p (t c) -> p t c", c=4)
        rest = work[:, AT1:AT1 + H * D].rearrange("p (h c) -> p h c", h=H)
        qs = work[:, 0:B * D].rearrange("p (t c) -> p t c", c=D)
        qe = work[:, B * D:2 * B * D].rearrange("p (t c) -> p t c", c=D)
        krep_of = [big[:, 0:D * BX], big[:, 9500:9500 + D * BX], xg[:, 2080:2080 + D * BX]]
        sumrows_of = [ap.rearrange("p (t c) -> p t c", c=D) for ap in
                      (big[:, 2000:2000 + B * D], big[:, 10900:10900 + B * D], xg[:, 3400:3400 + B * D])]
        masked_of = [[masked0, xg[:, 1280:1780]], [masked0, big[:, 9000:9500]], None, [masked0, acc2[:, 0:500]]]

        wvT_flat, wkrep = work[:, 0:RW * EX], xg[:, 0:RW * EX]
        wvT = wvT_flat.rearrange("p (f t) -> p f t", f=RW)
        sc_flat = sb("sc", [128, HEADS * TE])
        sc = sc_flat[:, :].rearrange("p (h t) -> p h t", h=HEADS)
        sh3_flat = sc_flat[:, 0:TE * 3]
        sh3 = sh3_flat.rearrange("p (t c) -> p t c", c=3)
        table = sb("table", [128, A, Q * P], F16)
        parts = sb("parts", [128, A, S, C * D], BF16)
        rc_f = sb("rc", [128, 2 * 2 * Q * P])
        rc = [rc_f[:, s_ * 1000:(s_ + 1) * 1000].bitcast(F16).rearrange("p (a e) -> p a e", a=2) for s_ in range(2)]
        red = rc_f[:, 0:T * 32].rearrange("p (t c) -> p t c", c=32)
        waccT_flat = [xg[:, RW * EX:2 * RW * EX], rc_f[:, 0:RW * EX]]
        waccT = [ap.rearrange("p (f t) -> p f t", f=RW) for ap in waccT_flat]
        stack_i = sb("stack_i", [128, D])
        stack_mix = sb("stack_mix", [128, GW])
        stack_kv = sb("stack_kv", [128, KV])
        stacks = [stack_i, stack_mix, None, stack_kv]
        pnum = sb("pnum", [128, 1 + A], I32)
        cval = sb("cval", [128, 3])
        spill = sb("spill", [128, NPAD])
        keep = sb("keep", [128, TE])
        neg = sb("neg", [128, TE + 1])
        dst_i = neg[:, 0:TE].bitcast(I32)
        idx = [sb(f"idx{s}", [128, T], I32) for s in range(2)]
        before = sb("before", [128, 8], I32)
        beforef = sb("beforef", [128, 4])
        xn = sb("xn", [128, H, D])
        stat = sb("stat", [128, 2, H])
        has = sb("has", [128, H])
        end_c = sb("end_c", [128, H])
        start_c = sb("start_c", [128, H])
        end_i = sb("end_i", [128, H], I32)
        start_i = sb("start_i", [128, H], I32)
        tot = sb("tot", [128, H])
        hist = sb("hist", [128, H])
        cum = sb("cum", [128, H])
        dots = sb("dots", [128, T, M])
        inits = sb("inits", [128, 2 * HEADS])
        packed = sb("packed", [128, 4, HEADS])
        stretch = sb("stretch", [128, 1])
        brow = sb("brow", [H, L])
        hilo = sb("hilo", [128, 2, TB], I32)
        hilof = sb("hilof", [128, 2, TB])
        iota_l = sb("iota_l", [128, L])
        iota_i = big[:, 6200:6200 + L].bitcast(I32)
        edge_end = sb("edge_end", [128, 2])
        ident = sb("ident", [128, 128])
        last_l = sb("last_l", [128, 128])
        wmix = sb("wmix", [D, GW])
        w1blk = sb("w1blk", [128, Q, 128])
        w2 = sb("w2", [128, 4 * M * M])
        w2v = w2[:, :].rearrange("p (i c) -> p i c", i=M)
        b1 = sb("b1", [128, 1])
        wsi = sb("wsi", [D, D])
        wkvq = sb("wkvq", [D, 3 * D])
        wos = sb("wos", [D, D])
        fT = work[0:HEADS, 0:7 * 128].rearrange("h (a p) -> h a p", a=7)
        qcarry = sb("qcarry", [128, D])

        bank = [ctx.enter_context(nc.psum_tensor(f"bank{i}", [128, 512], F32)) for i in range(8)]

        s_dst = sem("dst_loaded")
        s_prev = sem("before_loaded")
        s_prev0 = sem("before_cleared")
        s_x = sem("x_loaded")
        s_attr = sem("attrs_loaded")
        s_ew = sem("edge_weight_loaded")
        s_wts = sem("weights_loaded")
        s_wclr = sem("weights_cleared")
        s_scaled = sem("weights_scaled")
        s_const = sem("pool_constants_done")
        s_iota = sem("pool_iota_done")
        s_idx = [[sem(f"idx_loaded_{l}_{s}") for s in range(2)] for l in range(4)]
        s_gat = [[sem(f"rows_gathered_{l}_{s}") for s in range(2)] for l in range(4)]
        s_use = [[sem(f"rows_used_{l}_{s}") for s in range(2)] for l in range(4)]
        s_val = [sem(f"values_kept_{s}") for s in range(2)]
        s_hidx = sem("end_rows_ready")
        s_begun = sem("gathers_begun")
        s_acc = sem("sums_ready")
        s_rows = sem("sum_rows_copied")
        s_krep = sem("keep_repeated")
        s_kclr = sem("keep_cleared")
        s_sum = sem("sums_written")
        s_acc3 = sem("sums3_ready")
        s_rows3 = sem("sums3_rows_copied")
        s_sum3 = [sem(f"sums3_written_{s}") for s in range(2)]
        s_onehot = sem("block_onehots_ready")
        s_bidx = sem("block_indices_ready")
        s_blk = sem("blocks_gathered")
        s_hist = sem("histogram_ready")
        s_zero = sem("zero_ready")
        s_qz = sem("qstart_cleared")
        v_done = sem("vector_done")
        s_tail = sem("vector_to_tensor")
        s_tback = sem("tensor_to_vector")
        s_bnd = sem("bounds_written")
        s_bld = sem("bounds_loaded")
        s_gidx = sem("node_indices_ready")
        s_attn = sem("attention_ready")
        s_quad = sem("quadrupoles_done")
        s_end = sem("ends_gathered")
        s_spill = sem("spill_summed")
        s_var = sem("variance_ready")
        s_std = sem("deviation_ready")
        s_xn = sem("x_ready")
        s_tp = sem("x_transposed")
        s_tc = sem("xT_copied")
        s_pj = sem("projected")
        s_pc = sem("projection_copied")
        s_nw = sem("node_rows_written")
        s_qg = sem("first_queries_gathered")
        s_qw = sem("queries_scattered")
        s_ql = sem("qstart_loaded")
        s_qu = sem("qstart_used")
        s_ef = [sem(f"edge_feat_loaded_{s}") for s in range(2)]
        s_eft = [sem(f"edge_feat_transposed_{s}") for s in range(2)]
        s_efc = sem("edge_feat_T_copied")
        s_hp = sem("hidden_summed")
        s_hc = sem("hidden_ready")
        s_wp = sem("edge_weights_summed")
        s_wc = sem("edge_weights_copied")
        s_red = sem("channels_summed")
        s_exp = sem("exponentials_ready")
        s_max = sem("maxima_subtracted")
        s_out = sem("out_written")
        s_src = sem("src_loaded")
        s_rcf = sem("src_split")
        s_rct = sem("src_split_turned")
        s_rcc = sem("src_turned_copied")
        s_rcw = sem("rcrow_written")
        s_rc = [sem(f"rc_loaded_{s}") for s in range(2)]
        s_idxfree = sem("indices_used")
        s_stk = sem("stacks_loaded")
        s_parts = sem("parts_ready")
        s_oh = sem("onehot_halves_ready")
        s_lk = sem("candidates_summed")
        s_mk = sem("candidates_masked")
        s_lp = sem("rows_turned")
        s_lc = sem("looked_up_rows_copied")

        NG = -(-H // 4)
        PROJ = [GW, D, 3 * D, D]
        SCOL = [16, 16, 16, 14]
        SWID = [D, D, D, RW]
        ZW = B * D // 2
        WBANKS = [0, 1, 2, 7]
        TQ = T // 4
        PAIRS = T // 2

        def rep(ap, dims):
            return ap.unsqueeze(len(ap.shape)).broadcast_to(dims)

        RC0 = [0, 16 * ITERS, 0, 2 * 16 * ITERS]

        wlist = [(wmix[0:M, 0:M], w_tp[0, :, :]), (wmix[0:M, 7 * M:8 * M], w_tp[2, :, :])]
        for c, first, comps in ((1, 1, (0, 1, 2)), (3, 4, (0, 1, 2)), (4, 8, (1, 2, 0, 1)), (5, 12, (0, 1, 2))):
            for n, j in enumerate(comps):
                wlist.append((wmix[M + j:M + j + 22:3, (first + n) * M:(first + n + 1) * M], w_tp[c, :, :]))
        for k in range(Q):
            wlist.append((w1blk[k * D:(k + 1) * D, k, 0:HID], w_mlp1))
        wlist.append((b1[0:HID, :], b_mlp1.rearrange("(k a) -> k a", a=1)))
        for n, b in enumerate((0, 1, 3, 2)):
            wlist.append((w2v[0:HID, :, n * M:(n + 1) * M],
                          w_mlp2.rearrange("k (b i o) -> k b i o", b=4, i=M)[:, b, :, :]))
            wlist.append((w2v[HID:HID + 1, :, n * M:(n + 1) * M],
                          b_mlp2.rearrange("(a b i o) -> a b i o", a=1, b=4, i=M)[:, b, :, :]))
        wlist.append((wsi[0:M, 0:M], si0))
        for m in range(3):
            wlist.append((wsi[M + m:M + m + 22:3, M + m:M + m + 22:3], si1))
        wlist += [(wkvq[:, 0:D], wk), (wkvq[:, D:2 * D], wv), (wkvq[:, 2 * D:3 * D], wq), (wos[:, :], wo)]

        block = ctx.enter_context(nc.Block())

        @block.sync
        def _(sp):
            dst2 = dst.rearrange("(p t) -> p t", p=P)
            src2 = src.rearrange("(p t) -> p t", p=P)
            sums_v = sums.rearrange("(p t) c -> p t c", p=P)
            sums3_v = sums3.rearrange("(p t) c -> p t c", p=P)
            ef_v = ea32.rearrange("(p t) c -> p (t c)", p=P)
            qs_v = qstart[0:E, :].rearrange("(p t) c -> p (t c)", p=P)

            sp.dma_start(dst_i[0:P, :], dst2).then_inc(s_dst, 16)
            sp.dma_start(src_i[0:P, :], src2).then_inc(s_src, 16)
            sp.dma_start(ew_s[0:P, :], ew.rearrange("(p t) -> p t", p=P)).then_inc(s_ew, 16)
            sp.wait_ge(s_prev0, 1)
            sp.dma_start(before[1:P, 0:1], dst2[0:P - 1, TE - 1:TE], allow_slow_non_contiguous=True).then_inc(s_prev, 16)
            sp.dma_start(before[0:P, 1:2], dst2[:, 0:1], allow_slow_non_contiguous=True).then_inc(s_prev, 16)

            def node_rows(l):
                if l == 1:
                    sp.wait_ge(s_pc, NG)
                    sp.dma_start(node_g.rearrange("(h l) c -> l h c", l=L), nodeout).then_inc(s_nw, 16)
                elif l == 2:
                    sp.wait_ge(s_xn, 2)
                    sp.dma_start(node_x.rearrange("(h l) c -> l h c", l=L), xn[:, :, :]).then_inc(s_nw, 16)
                else:
                    sp.wait_ge(s_pc, 3 * NG)
                    sp.dma_start(node_kv.rearrange("(h l) c -> l h c", l=L), kvout).then_inc(s_nw, 16)
                    sp.dma_start(node_q.rearrange("(h l) c -> l h c", l=L), qout).then_inc(s_nw, 16)

            for l in range(4):
                if l:
                    for s in range(2):
                        sp.wait_ge(s_gat[l - 1][s], ITERS * 16 * GATHERED[l - 1][s])
                if l == 3:
                    sp.wait_ge(s_qw, 16 * H)

                if l == 0:
                    def rc_out():
                        for b in range(8):
                            for a in range(2):
                                sp.dma_start(rcrow[a:a + 1, b * 100 * P:(b + 1) * 100 * P].rearrange("a (t e) -> (a t) e", e=P),
                                             turned[0:100, b, a, :]).then_inc(s_rcw, 16)
                        sp.wait_ge(s_rcw, 256)

                def rc_in(i, s):
                    n = Q * LOOK[l][s] * P
                    if not isinstance(i, int):
                        sp.wait_ge(s_mk, group(l, i, s, LOOK[l][s] - PER[l]))
                    sp.dma_start(rc[s][:, :, 0:n],
                                 rcrow[:, bass.ds((i * B + s * T + GATHERED[l][s]) * P, n)].partition_broadcast(128)).then_inc(s_rc[s], 16)

                def loads(i):
                    for s in range(2):
                        if not isinstance(i, int):
                            if PER[l]:
                                rc_in(i, s)
                            sp.wait_ge(s_gat[l][s], i * (16 * GATHERED[l][s]))
                            sp.sem_inc(s_idxfree, 1)
                        sp.dma_start(idx[s][0:P, :], src2[:, bass.ds(i * B + s * T, T)]).then_inc(s_idx[l][s], 16)
                        if l == 0 and s == 1 and isinstance(i, int):
                            sp.wait_ge(s_rcc, 16)
                            rc_out()
                            for k in range(2):
                                rc_in(0, k)
                        elif PER[l] and l and isinstance(i, int):
                            rc_in(i, s)
                        if l == 2:
                            if not isinstance(i, int):
                                sp.wait_ge(s_eft[s], i)
                            sp.dma_start(ef[0:P, s, :], ef_v[:, bass.ds((i * B + s * T) * D, T * D)]).then_inc(s_ef[s], 16)
                        if l == 3 and s == 0:
                            if not isinstance(i, int):
                                sp.wait_ge(s_qu, i)
                            sp.dma_start(qs[0:P, :, :].rearrange("p t c -> p (t c)"),
                                         qs_v[:, bass.ds(i * (B * D), B * D)]).then_inc(s_ql, 16)

                def sums_out(i):
                    sp.wait_ge(s_rows, i + (l * ITERS + 1))
                    sp.dma_start(sums_v[:, bass.ds(i * B, B), :], sumrows_of[l][0:P]).then_inc(s_sum, 16)

                loads(0)
                with sp.Fori(1, ITERS) as i:
                    loads(i)
                    if l < 3:
                        sums_out(i - 1)
                if l < 3:
                    sums_out(ITERS - 1)
                if l < 3:
                    node_rows(l + 1)
            with sp.Fori(0, BLOCKS // 2) as i:
                for s in range(2):
                    sp.wait_ge(s_rows3, i * 2 + s + 1)
                    sp.dma_start(sums3_v[:, bass.ds((i * 2 + s) * EB, EB), :], accs[s][0:P, :, :]).then_inc(s_sum3[s], 16)
            sp.wait_ge(s_xn, 4)
            sp.dma_start(out[0:L * HF, :].rearrange("(h l) c -> l h c", l=L), xn[:, 0:HF, :]).then_inc(s_out, 16)
            sp.dma_start(out[L * HF:N, :], xn[0:REST, HF, :]).then_inc(s_out, 16)
            sp.wait_ge(s_out, 32)

        @block.gpsimd
        def _(pool):
            pool.iota(iota_i[:, :], [[1, L]], base=0, channel_multiplier=0).then_inc(s_iota, 1)
            pool.iota(before[:, 2:3], [[0, 1]], base=TE, channel_multiplier=TE).then_inc(s_iota, 1)
            pool.iota(start_i[:, :], [[L, H]], base=DUMP, channel_multiplier=1).then_inc(s_iota, 1)
            pool.iota(pnum[:, 0:1], [[0, 1]], base=0, channel_multiplier=1).then_inc(s_iota, 1)
            pool.iota(pnum[:, 1:1 + A], [[L, A]], base=0, channel_multiplier=1).then_inc(s_iota, 1)
            pool.memset(ident[:, :], 0.0).then_inc(s_iota, 1)
            pool.memset(last_l[:, :], 0.0).then_inc(s_iota, 1)
            pool.wait_ge(s_iota, 7)
            pool.affine_select(out=ident[:, :], in_=ident[:, :], compare_op=ALU.not_equal, fill=1.0,
                               base=0, pattern=[[-1, 128]], channel_multiplier=1).then_inc(s_const, 1)
            pool.affine_select(out=last_l[:, :], in_=last_l[:, :], compare_op=ALU.not_equal, fill=1.0,
                               base=-127, pattern=[[0, 128]], channel_multiplier=1).then_inc(s_const, 1)
            for l in range(4):
                for s in range(2):
                    pool.sem_inc(s_use[l][s], 1)
            for s in range(2):
                pool.sem_inc(s_val[s], 1)
            tables = [x, node_g, node_x, node_kv]
            slots = [rows0, rows1, rows0, rows3]
            for l in range(4):
                if l:
                    pool.wait_ge(s_nw, (16, 32, 64)[l - 1])
                if l == 3:
                    pool.indirect_dma_start(qcarry[0:P, :], None, node_q,
                                            bass.IndirectOffsetOnAxis(ap=before[0:P, 1:2], axis=0)).then_inc(s_qg, 16)
                    pool.wait_ge(s_qz, 16 * 2 * ITERS)
                    for h in range(H):
                        pool.indirect_dma_start(qstart, bass.IndirectOffsetOnAxis(ap=start_i[:, h:h + 1], axis=0),
                                                qout[:, h, :], None).then_inc(s_qw, 16)
                    pool.wait_ge(s_qw, 16 * H)
                def gathers(i):
                    for s in range(2):
                        pool.wait_ge(s_idx[l][s], i * 16 + 16)
                        pool.wait_ge(s_use[l][s], i + 1)
                        if l == 3:
                            pool.wait_ge(s_val[s], i + 1)
                        pool.sem_inc(s_begun, 1)
                        for t in range(GATHERED[l][s]):
                            pool.indirect_dma_start(slots[l][0:P, s * T + t, :], None, tables[l],
                                                    bass.IndirectOffsetOnAxis(ap=idx[s][0:P, t:t + 1], axis=0)
                                                    ).then_inc(s_gat[l][s], 16)

                if l == 0:
                    gathers(0)
                    pool.wait_ge(s_bidx, 1)
                    for h in range(H):
                        pool.indirect_dma_start(block_i[:, h, :], None, dst.rearrange("(b k) -> b k", k=K),
                                                bass.IndirectOffsetOnAxis(ap=end_i[:, h:h + 1], axis=0)).then_inc(s_blk, 16)
                with pool.Fori(1 if l == 0 else 0, ITERS) as i:
                    gathers(i)
                if l == 0:
                    pool.wait_ge(s_gidx, 1)
                if l < 3:
                    pool.wait_ge(s_sum, (l + 1) * ITERS * 16)
                else:
                    for s in range(2):
                        pool.wait_ge(s_sum3[s], BLOCKS // 2 * 16)
                w = SWID[l]
                for h in range(H):
                    pool.indirect_dma_start(ends[:, h * w:(h + 1) * w], None, sums if l < 3 else sums3,
                                            bass.IndirectOffsetOnAxis(ap=end_i[:, h:h + 1], axis=0)).then_inc(s_end, 16)

        @block.vector
        def _(vec):
            ch = Chain(vec, v_done)

            vec.memset(before[:, 0:1], -1).then_inc(s_prev0, 1)
            vec.memset(xn[:, :, :], 0.0).then_inc(s_wclr, 1)
            vec.memset(wmix[:, :], 0.0).then_inc(s_wclr, 1)
            vec.memset(w1blk[:, :, :], 0.0).then_inc(s_wclr, 1)
            vec.memset(wsi[:, :], 0.0).then_inc(s_wclr, 1)
            vec.memset(w2[:, :], 0.0).then_inc(s_wclr, 1)
            vec.memset(b1[HID:128, :], 0.0).then_inc(s_wclr, 1)
            vec.wait_ge(s_wclr, 6)
            vec.memset(b1[HID:HID + 1, :], 1.0).then_inc(s_wclr, 1)
            vec.memset(zero[:, :], 0.0).then_inc(s_zero, 1)
            ch.step(vec.memset(hist[:, :], 0.0))
            vec.wait_ge(s_dst, 16)
            vec.wait_ge(s_prev, 32)
            ch.step(vec.tensor_tensor(keep[0:P, 1:TE], dst_i[0:P, 1:TE], dst_i[0:P, 0:TE - 1], ALU.is_equal))
            ch.step(vec.tensor_tensor(keep[0:P, 0:1], before[0:P, 0:1], before[0:P, 1:2], ALU.is_equal))
            vec.wait_ge(s_const, 2)
            ch.step(vec.tensor_copy(iota_l[:, :], iota_i[:, :]))
            ch.step(vec.tensor_copy(edge_end[:, 0:1], before[:, 2:3]))
            ch.step(vec.tensor_copy(start_c[:, :], start_i[:, :]))
            ch.settle()

            vec.wait_ge(s_src, 16)
            ch.step(vec.tensor_copy(src_f[0:P, 0, :], src_i[0:P, :]))
            ch.step(vec.tensor_copy(cval[:, 0:1], pnum[:, 0:1]))
            ch.step(vec.tensor_copy(table[:, :, :], rep(pnum[:, 1:1 + A], [128, A, Q * P])))
            ch.step(vec.tensor_reduce(stack_i[:, :], ident[:, :].rearrange("p (c f) -> p f c", c=C), AX.X, ALU.add))
            ch.step(vec.memset(parts[:, :, :, :], 0.0))
            ch.settle()
            ch.step(vec.tensor_scalar(src_f[0:P, 2, :], src_f[0:P, 0, :], float(L * A), None, ALU.is_ge))
            ch.step(vec.tensor_scalar(cval[:, 1:2], cval[:, 0:1], float(D), None, ALU.is_ge))
            for c in range(2, C):
                ch.settle()
                ch.step(vec.scalar_tensor_tensor(src_f[0:P, 2, :], src_f[0:P, 0, :], float(L * A * c), src_f[0:P, 2, :], ALU.is_ge, ALU.add))
                ch.step(vec.scalar_tensor_tensor(cval[:, 1:2], cval[:, 0:1], float(D * c), cval[:, 1:2], ALU.is_ge, ALU.add))
            ch.settle()
            vec.scalar_tensor_tensor(src_f[0:P, 1, :], src_f[0:P, 2, :], -float(L * A), src_f[0:P, 0, :], ALU.mult, ALU.add).then_inc(s_rcf, 1)

            def split(l):
                if l:
                    vec.wait_ge(s_lk, LOOKED[l])
                    vec.wait_ge(s_xn, l)
                def at_(k, a, c0, c1):
                    return parts[:, 0:a, k, c0 * D:c1 * D].rearrange("p a (c f) -> p c a f", f=D)
                views = [(slice(0, 21), 7, 0, 3), (slice(21, 25), 4, 3, 4)]
                ch.settle()
                for k in range(S):
                    for hs, a, c0, c1 in views:
                        from_ = (xn[:, hs, :] if k == 0 else rest[:, hs, :]).rearrange("p (c a) f -> p c a f", a=a)
                        ch.step(vec.tensor_copy(at_(k, a, c0, c1), from_))
                    ch.settle()
                    if k < S - 1:
                        for hs, a, c0, c1 in views:
                            from_ = (xn[:, hs, :] if k == 0 else rest[:, hs, :]).rearrange("p (c a) f -> p c a f", a=a)
                            ch.step(vec.tensor_tensor(rest[:, hs, :].rearrange("p (c a) f -> p c a f", a=a), from_,
                                                      at_(k, a, c0, c1), ALU.subtract))
                        ch.settle()
                vec.memset(beforef[:, 3:4], 0.0).then_inc(s_parts, 1)

            def onehots(l, i, s, g):
                n, (slot, back) = group(l, i, s, g), slot_of(l, s, g)
                if g == 0:
                    vec.wait_ge(s_rc[s], RC0[l] + i * 16 + 16)
                if not isinstance(n, int) or n >= back:
                    vec.wait_ge(s_lk, n + (1 - back))
                for a, b in ((0, 4), (4, A)):
                    vec.tensor_tensor(onehots_of[l][slot][:, a:b, :],
                                      rc[s][:, 0, g * Q * P:(g + 1) * Q * P].unsqueeze(1).broadcast_to([128, b - a, Q * P]),
                                      table[:, a:b, :], ALU.is_equal).then_inc(s_oh, 1)

            def mask(l, i, s, g):
                n, (slot, back) = group(l, i, s, g), slot_of(l, s, g)
                vec.wait_ge(s_lk, n + 1)
                if not isinstance(n, int) or n >= back:
                    vec.wait_ge(s_lp, n + (1 - back))
                vec.scalar_tensor_tensor(masked_of[l][slot], rc[s][:, 1, g * Q * P:(g + 1) * Q * P], cval[:, 1:2],
                                         bank[3 + slot][:, 0:Q * P], ALU.is_equal, ALU.mult).then_inc(s_mk, 1)

            def ahead(l, i, s, stage, last):
                if PER[l] == 0 or (last and s == 1):
                    return
                g = stage // 2
                if stage % 2 == 0 and g < LOOK[l][1 - s]:
                    mask(l, *((i, 1) if s == 0 else (i + 1, 0)), g)
                elif stage % 2 == 1 and g < LOOK[l][s] and not last:
                    onehots(l, i + 1, s, g)

            def first_lookups(l):
                groups = [(0, s, g) for s in range(2) for g in range(LOOK[l][s])]
                for k in range(2):
                    onehots(l, *groups[k]) if k < len(groups) else None
                for k in range(LOOK[l][0]):
                    mask(l, *groups[k])
                    if k + 2 < len(groups):
                        onehots(l, *groups[k + 2])

            def bodies(body, per):
                with vec.Fori(0, ITERS - 1) as i:
                    ch.enter(i, per)
                    body(i, False)
                ch.leave(ITERS - 1)
                body(ITERS - 1, True)

            def clear_carry(l):
                if l:
                    vec.wait_ge(s_xn, l)
                ch.step(vec.memset(msgT[:, :, 0], 0.0))
                vec.memset(krep_of[l].rearrange("p (f t) -> p f t", f=D)[:, :, 0], 0.0).then_inc(s_kclr, 1)
                ch.settle()

            def scans(i, l):
                vec.wait_ge(s_krep, i + (l * ITERS + 1))
                if l or not isinstance(i, int) or i:
                    vec.wait_ge(s_rows, i + l * ITERS)
                ch.step(vec.tensor_tensor_scan(acc_flat[0:P, :], krep_of[l][0:P, :], msgT_flat[0:P, :], 0.0, ALU.mult, ALU.add))
                ch.settle()
                vec.tensor_copy(msgT[0:P, :, 0], acc[0:P, :, B]).then_inc(s_acc, 1)
                vec.wait_ge(s_acc, i + (l * ITERS + 1))

            def looked_up(l, s, i):
                vec.wait_ge(s_lc, group(l, i, s, LOOK[l][s]))

            def gathered(l, s, i):
                vec.wait_ge(s_gat[l][s], (i + 1) * (16 * GATHERED[l][s]))
                if PER[l]:
                    looked_up(l, s, i)

            ch.step(vec.tensor_scalar(hilo[0:P, 0, :], dst_i[0:P, K - 1::K], 7, None, ALU.arith_shift_right))
            ch.step(vec.tensor_scalar(hilo[0:P, 1, :], dst_i[0:P, K - 1::K], L - 1, None, ALU.bitwise_and))
            ch.settle()
            ch.step(vec.tensor_copy(hilof[0:P, :, :], hilo[0:P, :, :]))
            ch.settle()
            ch.step(vec.tensor_tensor(hi_eq[0:P, :, :], iota_l[0:P, 0:H].unsqueeze(1).broadcast_to([P, TB, H]),
                                      rep(hilof[0:P, 0, :], [P, TB, H]), ALU.is_equal))
            vec.tensor_tensor(lo_le[0:P, :, :], iota_l[0:P, :].unsqueeze(1).broadcast_to([P, TB, L]),
                              rep(hilof[0:P, 1, :], [P, TB, L]), ALU.is_ge).then_inc(s_onehot, 1)
            vec.wait_ge(s_x, 32)
            split(0)
            vec.wait_ge(s_hist, 1)
            ch.step(vec.tensor_copy(hist[:, :], bank[0][:, 0:H]))
            vec.tensor_copy(tot[:, :], bank[0][:, 0:H]).then_inc(s_tail, 1)
            vec.wait_ge(s_tback, 1)
            ch.step(vec.tensor_copy(end_c[:, :], bank[0][:, 64:64 + H]))
            ch.settle()
            ch.step(vec.tensor_tensor_scan(cum[:, :], end_c[:, :], zero[:, 0:H], 0.0, ALU.add, ALU.add))
            ch.settle()
            ch.step(vec.tensor_tensor(hist[:, 1:H], hist[:, 1:H], cum[:, 0:H - 1], ALU.add))
            ch.settle()
            ch.step(vec.tensor_scalar(hist[:, :], hist[:, :], float(NB - 1), None, ALU.min))
            ch.settle()
            vec.tensor_copy(end_i[:, :], hist[:, :]).then_inc(s_bidx, 1)

            vec.wait_ge(s_ew, 16)
            first_lookups(0)

            def weighted(i, last):
                for s in range(2):
                    col = i * B + s * T
                    here = slice(s * T, (s + 1) * T)
                    ahead(0, i, s, 0, last)
                    gathered(0, s, i)
                    vec.tensor_tensor(msg[0:P, here, :], rows0[0:P, here, :],
                                      rep(ew_s[0:P, bass.ds(col, T)], [P, T, D]), ALU.mult).then_inc(s_use[0][s], 1)
                    for stage in (1, 2, 3):
                        ahead(0, i, s, stage, last)
                for s in range(2):
                    vec.wait_ge(s_use[0][s], i + 2)
                scans(i, 0)

            def bounds_out():
                ch.step(vec.tensor_scalar(cum[:, :], start_c[:, :], -float(DUMP), None, ALU.add))
                vec.wait_ge(s_blk, 16 * H)
                ch.step(vec.tensor_copy(block_f, block_i))
                ch.settle()
                ch.step(vec.tensor_tensor(block_f, block_f, rep(cum[:, :], [L, H, K]), ALU.is_le))
                ch.settle()
                ch.step(vec.tensor_reduce(tot[:, :], block_f, AX.X, ALU.add))
                ch.settle()
                vec.scalar_tensor_tensor(end_c[:, :], hist[:, :], float(K), tot[:, :], ALU.mult, ALU.add).then_inc(s_hidx, 1)
                vec.wait_ge(s_tback, 2)
                vec.tensor_copy(brow[:, :], bank[0][0:H, 128:256]).then_inc(s_tail, 1)

            def bounds_in():
                vec.wait_ge(s_tback, 3)
                ch.step(vec.tensor_copy(cum[:, :], bank[0][:, 256:256 + H]))
                vec.wait_ge(s_bld, 48)
                ch.settle()
                ch.step(vec.tensor_tensor(has[:, :], end_c[:, :], cum[:, :], ALU.is_gt))
                ch.step(vec.tensor_scalar(tot[:, :], end_c[:, :], -1.0, 0.0, ALU.add, ALU.max))
                ch.step(vec.tensor_tensor(cum[:, :], cum[:, :], start_c[:, :], ALU.subtract))
                ch.step(vec.tensor_scalar(spill[0:P, :], spill[0:P, :], edge_end[0:P, 0:1], None, ALU.is_lt))
                ch.settle()
                ch.step(vec.tensor_copy(end_i[:, :], tot[:, :]))
                ch.step(vec.tensor_tensor(cum[:, :], cum[:, :], has[:, :], ALU.mult))
                ch.step(vec.scalar_tensor_tensor(spill[0:P, :], next_b[0:P, :], edge_end[0:P, 0:1], spill[0:P, :],
                                                 ALU.is_gt, ALU.mult))
                ch.settle()
                vec.tensor_tensor(start_i[:, :], cum[:, :], start_c[:, :], ALU.add).then_inc(s_gidx, 1)

            def weights():
                alpha = 0.25
                vec.wait_ge(s_wts, 16 * len(wlist))
                ch.step(vec.tensor_scalar(wmix[:, M:8 * M], wmix[:, M:8 * M], 1 / math.sqrt(3), None, ALU.mult))
                ch.step(vec.tensor_scalar(wmix[:, 8 * M:12 * M], wmix[:, 8 * M:12 * M], 1 / math.sqrt(6), None, ALU.mult))
                for n, c in ((0, alpha), (1, alpha), (2, alpha / math.sqrt(3)), (3, alpha)):
                    ch.step(vec.tensor_scalar(w2v[:, :, n * M:(n + 1) * M], w2v[:, :, n * M:(n + 1) * M], c, None, ALU.mult))
                ch.step(vec.tensor_scalar(wsi[:, :], wsi[:, :], 1 / math.sqrt(M), None, ALU.mult))
                ch.settle()
                vec.tensor_scalar(wkvq[:, 2 * D:3 * D], wkvq[:, 2 * D:3 * D], 1 / math.sqrt(DH), None, ALU.mult).then_inc(s_scaled, 1)

            vec.wait_ge(s_hist, 1)
            clear_carry(0)
            weighted(0, False)
            bounds_out()
            with vec.Fori(1, ITERS - 1) as i:
                ch.enter(i, 1, 1)
                weighted(i, False)
            ch.leave(ITERS - 2)
            bounds_in()
            weights()
            weighted(ITERS - 1, True)

            def summed(l):
                w, cols = SWID[l], SCOL[l]
                rows = ends[:, 0:H * w].rearrange("p (h c) -> p h c", h=H)
                vec.wait_ge(s_end, (l + 1) * H * 16)
                ch.step(vec.tensor_tensor(rows, rows, rep(has[:, :], [L, H, w]), ALU.mult))
                vec.wait_ge(s_spill, l + 1)
                ch.settle()
                for n, (a, b) in enumerate(((0, cols), (cols, H))):
                    ch.step(vec.tensor_tensor(rows[:, a:b, :], rows[:, a:b, :],
                                              bank[1 + n][:, 0:(b - a) * w].rearrange("p (h c) -> p h c", c=w), ALU.add))
                ch.settle()
                return rows

            def layernorm(l):
                ch.settle()
                ch.step(vec.tensor_reduce(stat[:, 0, :], xn[:, :, :], AX.X, ALU.add))
                ch.settle()
                ch.step(vec.tensor_scalar(stat[:, 0, :], stat[:, 0, :], 1 / D, None, ALU.mult))
                ch.settle()
                ch.step(vec.tensor_tensor(centred, xn[:, :, :], rep(stat[:, 0, :], [L, H, D]), ALU.subtract))
                ch.settle()
                ch.step(vec.tensor_tensor(squares, centred, centred, ALU.mult))
                ch.settle()
                ch.step(vec.tensor_reduce(stat[:, 1, :], squares, AX.X, ALU.add))
                ch.settle()
                vec.tensor_scalar(stat[:, 1, :], stat[:, 1, :], 1 / D, EPS, ALU.mult, ALU.add).then_inc(s_var, 1)
                vec.wait_ge(s_std, l + 1)
                ch.step(vec.reciprocal(stat[:, 1, :], stat[:, 0, :]))
                ch.settle()
                vec.tensor_tensor(xn[:, :, :], centred, rep(stat[:, 1, :], [L, H, D]), ALU.mult).then_inc(s_xn, 1)

            rows = summed(0)
            ch.step(vec.tensor_tensor(xn[:, :, :], xn[:, :, :], rows, ALU.add))
            layernorm(0)

            split(1)
            clear_carry(1)
            vec.wait_ge(s_pj, NG)
            vec.wait_ge(s_attr, 4 * 16)
            a, d = math.sqrt(0.1), math.sqrt(1 / 30)
            for j, k, c, f in ((0, 2, 0, a), (2, 0, 0, a), (0, 1, 1, a), (1, 0, 1, a), (1, 1, 2, 2 * d),
                               (1, 2, 3, a), (2, 1, 3, a), (0, 0, 4, -a), (2, 2, 4, a)):
                ch.step(vec.tensor_scalar(quad[0:P, :, 3 * j + k], sh5[0:P, :, c], f, None, ALU.mult))
            ch.settle()
            for jk in (0, 8):
                ch.step(vec.scalar_tensor_tensor(quad[0:P, :, jk], sh5[0:P, :, 2], -d, quad[0:P, :, jk], ALU.mult, ALU.add))
            ch.settle()

            def by3(ap):
                return ap.rearrange("p t (k o) -> p t k o", k=3)

            def mixed(i, last):
                for s in range(2):
                    col = i * B + s * T
                    here = slice(s * T, (s + 1) * T)
                    r, m = rows1[0:P, here, :], msg[0:P, here, :]
                    sh = sh3[0:P, bass.ds(col, T), :]
                    ta, tb = tmp[0:P, :, :], tmp2[0:P, :, :]
                    ch.settle()
                    ch.step(vec.tensor_copy(shx[0:P, :, 0:2], sh[:, :, 1:3]))
                    ch.step(vec.tensor_copy(shx[0:P, :, 2:4], sh[:, :, 0:2]))
                    ahead(1, i, s, 0, last)
                    gathered(1, s, i)
                    ch.step(vec.tensor_tensor(m, r[:, :, 0:4 * M], rep(ew1_s[0:P, bass.ds(col, T)], [P, T, D]), ALU.mult))
                    ch.step(vec.tensor_tensor(by3(ta), by3(r[:, :, 4 * M:7 * M]), rep(sh, [P, T, 3, M]), ALU.mult))
                    ch.step(vec.tensor_tensor(by3(tb), r[:, :, 7 * M:8 * M].unsqueeze(2).broadcast_to([P, T, 3, M]),
                                              rep(sh, [P, T, 3, M]), ALU.mult))
                    ch.settle()
                    ch.step(vec.tensor_reduce(dots[0:P, :, :], ta.rearrange("p t (k o) -> p t o k", k=3), AX.X, ALU.add))
                    ch.step(vec.tensor_tensor(m[:, :, M:D], m[:, :, M:D], tb, ALU.add))
                    ch.settle()
                    ch.step(vec.tensor_tensor(m[:, :, 0:M], m[:, :, 0:M], dots[0:P, :, :], ALU.add))
                    ch.step(vec.tensor_tensor(by3(ta), by3(r[:, :, 9 * M:12 * M]), rep(shx[0:P, :, 0:3], [P, T, 3, M]), ALU.mult))
                    ch.step(vec.tensor_tensor(by3(tb), by3(r[:, :, 8 * M:11 * M]), rep(shx[0:P, :, 1:4], [P, T, 3, M]), ALU.mult))
                    ch.settle()
                    ch.step(vec.tensor_tensor(m[:, :, M:D], m[:, :, M:D], ta, ALU.add))
                    ch.settle()
                    ch.step(vec.tensor_tensor(m[:, :, M:D], m[:, :, M:D], tb, ALU.subtract))
                    ahead(1, i, s, 1, last)
                    for j in range(3):
                        t_ = ta if j % 2 == 0 else tb
                        g5 = r[:, :, (12 + j) * M:(13 + j) * M].unsqueeze(2).broadcast_to([P, T, 3, M])
                        q3 = rep(quad[0:P, bass.ds(col, T), 3 * j:3 * j + 3], [P, T, 3, M])
                        if j < 2:
                            ch.step(vec.tensor_tensor(by3(t_), g5, q3, ALU.mult))
                            ch.settle()
                        else:
                            vec.tensor_tensor(by3(t_), g5, q3, ALU.mult).then_inc(s_use[1][s], 1)
                            vec.wait_ge(s_use[1][s], i + 2)
                        ch.step(vec.tensor_tensor(m[:, :, M:D], m[:, :, M:D], t_, ALU.add))
                        if j == 0:
                            ahead(1, i, s, 2, last)
                    ahead(1, i, s, 3, last)
                ch.settle()
                scans(i, 1)

            first_lookups(1)
            bodies(mixed, 2 * 17 + 1)

            def add_swapped(rows):
                ch.step(vec.tensor_tensor(xn[:, :, 0:M], xn[:, :, 0:M], rows[:, :, 0:M], ALU.add))
                ch.step(vec.tensor_tensor(xn[:, :, M:D].rearrange("p h (o k) -> p h k o", k=3),
                                          xn[:, :, M:D].rearrange("p h (o k) -> p h k o", k=3),
                                          rows[:, :, M:D].rearrange("p h (k o) -> p h k o", k=3), ALU.add))

            rows = summed(1)
            add_swapped(rows)
            layernorm(1)

            clear_carry(2)

            def weighed(i, last):
                for s in range(2):
                    col = i * B + s * T
                    here = slice(s * T, (s + 1) * T)
                    r, m, w, pr, rd = rows0[0:P, here, :], msg[0:P, here, :], wide[0:P], prod[0:P], red[0:P, :, :]
                    v = r[:, :, M:D].rearrange("p t (i m) -> p t i m", m=3)
                    sh0 = sh4[0:P, bass.ds(col, T), 0]
                    sh1 = sh4[0:P, bass.ds(col, T), 1:4]
                    gathered(2, s, i)
                    ch.settle()
                    ch.step(vec.tensor_tensor(tmp[0:P, :, :].rearrange("p t (i m) -> p t i m", m=3), v,
                                              sh1.unsqueeze(2).broadcast_to([P, T, M, 3]), ALU.mult))
                    ch.settle()
                    ch.step(vec.tensor_reduce(dots[0:P, :, :], tmp[0:P, :, :].rearrange("p t (i m) -> p t i m", m=3), AX.X, ALU.add))
                    ch.settle()
                    vec.wait_ge(s_wc, i * (2 * PAIRS) + (s + 1) * PAIRS)
                    ch.step(vec.tensor_tensor(pr[:, :, :, 0:2 * M], w[:, :, :, 0:2 * M], rep(r[:, :, 0:M], [P, T, M, 2 * M]), ALU.mult))
                    ch.step(vec.tensor_tensor(pr[:, :, :, 2 * M:3 * M], w[:, :, :, 2 * M:3 * M], rep(dots[0:P, :, :], [P, T, M, M]), ALU.mult))
                    for k in range(2):
                        ch.step(vec.tensor_tensor(pr[:, :, :, (3 + k) * M:(4 + k) * M], w[:, :, :, 3 * M:4 * M],
                                                  rep(v[:, :, :, k], [P, T, M, M]), ALU.mult))
                    vec.tensor_tensor(pr[:, :, :, 5 * M:6 * M], w[:, :, :, 3 * M:4 * M],
                                      rep(v[:, :, :, 2], [P, T, M, M]), ALU.mult).then_inc(s_use[2][s], 1)
                    vec.wait_ge(s_use[2][s], i + 2)
                    ch.step(vec.tensor_reduce(rd, pr[:, :, :, 0:4 * M].rearrange("p t i c -> p t c i"), AX.X, ALU.add))
                    ch.settle()
                    ch.step(vec.tensor_tensor(m[:, :, 0:M], rd[:, :, 0:M], rep(sh0, [P, T, M]), ALU.mult))
                    ch.step(vec.tensor_tensor(m[:, :, M:2 * M], rd[:, :, 3 * M:4 * M], rep(sh0, [P, T, M]), ALU.mult))
                    ch.step(vec.tensor_tensor(by3(tmp2[0:P, :, :]), rd[:, :, M:2 * M].unsqueeze(2).broadcast_to([P, T, 3, M]),
                                              rep(sh1, [P, T, 3, M]), ALU.mult))
                    vec.wait_ge(s_red, i * 2 + (s + 1))
                    ch.step(vec.tensor_tensor(m[:, :, 2 * M:D], bank[4][0:P, 0:T * 2 * M].rearrange("p (t c) -> p t c", t=T),
                                              rep(sh0, [P, T, 2 * M]), ALU.mult))
                    ch.settle()
                    ch.step(vec.tensor_tensor(m[:, :, 0:M], m[:, :, 0:M], rd[:, :, 2 * M:3 * M], ALU.add))
                    ch.step(vec.tensor_tensor(m[:, :, M:D], m[:, :, M:D], tmp2[0:P, :, :], ALU.add))
                ch.settle()
                scans(i, 2)

            first_lookups(2)
            bodies(weighed, 2 * 13 + 1)

            rows = summed(2)
            add_swapped(rows)
            ch.settle()
            vec.wait_ge(s_pc, 2 * NG)
            ch.step(vec.tensor_tensor(xn[:, :, :], xn[:, :, :], si_s[:, :, :], ALU.add))
            layernorm(2)

            split(3)
            ch.step(vec.memset(neg[:, :], 0.0))
            ch.settle()
            ch.step(vec.tensor_scalar(neg[0:P, 0:TE], keep[0:P, :], -1.0, BIG, ALU.add, ALU.mult))
            vec.wait_ge(s_qg, 16)
            def scored(i, last):
                vec.wait_ge(s_ql, i * 16 + 16)
                for f in range(D):
                    ch.step(vec.tensor_tensor_scan(qe[0:P, :, f], keep[0:P, bass.ds(i * B, B)], qs[0:P, :, f],
                                                   qcarry[0:P, f:f + 1], ALU.mult, ALU.add))
                ch.settle()
                vec.tensor_copy(qcarry[0:P, :], qe[0:P, B - 1, :]).then_inc(s_qu, 1)
                vec.wait_ge(s_qu, i + 1)
                ch.step(vec.memset(beforef[:, 3:4], 0.0))
                for s in range(2):
                    here = slice(s * T, (s + 1) * T)
                    ahead(3, i, s, 0, last)
                    gathered(3, s, i)
                    ch.step(vec.tensor_tensor(rows3[0:P, here, 0:D], rows3[0:P, here, 0:D], qe[0:P, here, :], ALU.mult))
                    ahead(3, i, s, 1, last)
                    ch.settle()
                    vec.tensor_reduce(sc[0:P, :, bass.ds(i * B + s * T, T)].rearrange("p h t -> p t h"),
                                      rows3[0:P, here, 0:D].rearrange("p t (h d) -> p t h d", h=HEADS),
                                      AX.X, ALU.add).then_inc(s_use[3][s], 1)
                    ahead(3, i, s, 2, last)
                    ahead(3, i, s, 3, last)

            first_lookups(3)
            bodies(scored, D + 1 + 2)

            for s in range(2):
                vec.wait_ge(s_use[3][s], ITERS + 1)

            def maxima(first_f, first_b):
                for h in range(HEADS):
                    ch.step(vec.tensor_tensor_scan(fwd[0:P, h, :], neg[0:P, 0:TE], sc[0:P, h, :],
                                                   first_f(h), ALU.add, ALU.max))
                    ch.step(vec.tensor_tensor_scan(bwd[0:P, h, ::-1], neg[0:P, TE:0:-1], sc[0:P, h, ::-1],
                                                   first_b(h), ALU.add, ALU.max))

            for s in range(2):
                vec.wait_ge(s_val[s], ITERS + 1)
            maxima(lambda h: -BIG, lambda h: -BIG)
            ch.step(vec.tensor_reduce(stretch[0:P, :], keep[0:P, :], AX.X, ALU.min))
            ch.settle()
            ch.step(vec.tensor_copy(packed[0:P, 0, :], fwd[0:P, :, TE - 1]))
            ch.step(vec.tensor_copy(packed[0:P, 1, :], bwd[0:P, :, 0]))
            ch.step(vec.tensor_copy(packed[0:P, 2, :], stretch[0:P, 0:1].broadcast_to([P, HEADS])))
            ch.step(vec.memset(fT[:, :, :], -BIG))
            ch.settle()
            vec.tensor_copy(packed[0:P, 3, :], keep[0:P, 0:1].broadcast_to([P, HEADS])).then_inc(s_tail, 1)
            vec.wait_ge(s_tback, 4)
            pk = bank[0][0:HEADS, :].rearrange("p (a c) -> p a c", a=4)
            ch.step(vec.tensor_copy(fT[:, 0:2, 0:P], pk[:, 0:2, 0:P]))
            ch.step(vec.tensor_scalar(fT[:, 2:4, 0:P], pk[:, 2:4, 0:P], -1.0, BIG, ALU.add, ALU.mult))
            ch.settle()
            ch.step(vec.tensor_tensor_scan(fT[:, 4, 1:P + 1], fT[:, 2, 0:P], fT[:, 0, 0:P], -BIG, ALU.add, ALU.max))
            ch.step(vec.tensor_tensor(fT[:, 2, 0:P], fT[:, 2, 0:P], fT[:, 3, 1:P + 1], ALU.add))
            ch.settle()
            ch.step(vec.tensor_tensor_scan(fT[:, 5, P - 1::-1], fT[:, 2, P - 1::-1], fT[:, 1, P - 1::-1], -BIG, ALU.add, ALU.max))
            ch.settle()
            vec.tensor_tensor(fT[:, 6, 0:P], fT[:, 5, 1:P + 1], fT[:, 3, 1:P + 1], ALU.add).then_inc(s_tail, 1)
            vec.wait_ge(s_tback, 5)
            ch.step(vec.tensor_copy(inits[0:P, :], bank[0][0:P, 0:2 * HEADS]))
            ch.settle()
            maxima(lambda h: inits[0:P, h:h + 1], lambda h: inits[0:P, HEADS + h:HEADS + h + 1])
            ch.settle()
            ch.step(vec.tensor_tensor(fwd[0:P], fwd[0:P], bwd[0:P], ALU.max))
            ch.settle()
            vec.tensor_tensor(sc[0:P], sc[0:P], fwd[0:P], ALU.subtract).then_inc(s_max, 1)
            vec.wait_ge(s_max, 1)
            ch.step(vec.memset(wvT[:, :, 0], 0.0))
            vec.memset(wkrep.rearrange("p (f t) -> p f t", f=RW)[:, :, 0], 0.0).then_inc(s_kclr, 1)
            ch.settle()

            vec.wait_ge(s_exp, 1)

            def weighted_values(i):
                for s in range(2):
                    cols = bass.ds((i * 2 + s) * EB, EB)
                    for h in range(HEADS):
                        ch.step(vec.tensor_tensor(wvT[0:P, h * DH:(h + 1) * DH, 1:EX].rearrange("p f t -> p t f"),
                                                  vals[0:P, cols, h * DH:(h + 1) * DH],
                                                  rep(sc[0:P, h, cols], [P, EB, DH]), ALU.mult))
                    ch.step(vec.tensor_copy(wvT[0:P, D:RW, 1:EX], sc[0:P, :, cols]))
                    ch.settle()
                    vec.wait_ge(s_krep, i * 2 + (3 * ITERS + s + 1))
                    if not isinstance(i, int):
                        vec.wait_ge(s_rows3, i * 2 + (s - 1))
                    ch.step(vec.tensor_tensor_scan(waccT_flat[s][0:P, :], wkrep[0:P, :], wvT_flat[0:P, :], 0.0, ALU.mult, ALU.add))
                    ch.settle()
                    vec.tensor_copy(wvT[0:P, :, 0], waccT[s][0:P, :, EB]).then_inc(s_acc3, 1)
                    vec.wait_ge(s_acc3, i * 2 + (s + 1))

            weighted_values(0)
            with vec.Fori(1, BLOCKS // 2) as i:
                ch.enter(i, 2 * (HEADS + 2), 1)
                weighted_values(i)
            ch.leave(BLOCKS // 2 - 1)

            rows = summed(3)
            den = rows[:, :, D:RW]
            ch.step(vec.tensor_scalar(den, den, 1e-16, None, ALU.max))
            ch.settle()
            ch.step(vec.reciprocal(den, den))
            ch.settle()
            for h in range(HEADS):
                o = vec.tensor_tensor(si_s[:, :, h * DH:(h + 1) * DH], rows[:, :, h * DH:(h + 1) * DH],
                                      rep(rows[:, :, D + h], [L, H, DH]), ALU.mult)
                if h < HEADS - 1:
                    ch.step(o)
                else:
                    o.then_inc(s_attn, 1)
            vec.wait_ge(s_pc, 4 * NG)
            ch.step(vec.scalar_tensor_tensor(xn[:, :, :], xn[:, :, :], 2.0, si_s[:, :, :], ALU.mult, ALU.add))
            layernorm(3)

        @block.tensor
        def _(pe):
            def spilled(l):
                w, cols = SWID[l], SCOL[l]
                if l < 3:
                    pe.wait_ge(s_acc, (l + 1) * ITERS)
                    state = msgT[0:P, :, 0]
                else:
                    pe.wait_ge(s_acc3, BLOCKS)
                    state = wvT[0:P, :, 0]
                for h in range(H):
                    n, c = (0, h) if h < cols else (1, h - cols)
                    last = pe.matmul(bank[1 + n][:, c * w:(c + 1) * w], spill[0:P, h * L:(h + 1) * L], state,
                                     start=True, stop=True)
                last.then_inc(s_spill, 1)

            def candidates(l, n, slot):
                for half, (a0, a1) in enumerate(((0, 4), (4, A))):
                    pe.wait_ge(s_oh, n * 2 + half + 1)
                    for a in range(a0, a1):
                        for k in range(S):
                            last = pe.matmul(bank[3 + slot][:, 0:Q * P], parts[:, a, k, :], onehots_of[l][slot][:, a, :],
                                             start=(a == 0 and k == 0), stop=(a == A - 1 and k == S - 1))
                last.then_inc(s_lk, 1)

            def turned_rows(l, n, slot, back):
                pe.wait_ge(s_mk, n + 1)
                if not isinstance(n, int) or n >= back:
                    pe.wait_ge(s_lc, n + (1 - back))
                w = stacks[l].shape[1]
                for j in range(Q):
                    last = pe.matmul(bank[5 + slot][0:P, j * w:(j + 1) * w], masked_of[l][slot][:, j * P:(j + 1) * P],
                                     stacks[l][:, :], start=True, stop=True)
                last.then_inc(s_lp, 1)

            def lookups(l, between=None):
                per = PER[l]
                places = [slot_of(l, s, g) for s in range(2) for g in range(LOOK[l][s])]
                pe.wait_ge(s_parts, (1, 2, 0, 3)[l])
                candidates(l, LOOKED[l], 0)

                def body(i, last=False, between=None):
                    for j in range(per):
                        if between and j == 1:
                            between()
                        slot, back = places[(j + 1) % per]
                        n = i * per + (LOOKED[l] + j)
                        if back == 1:
                            turned_rows(l, n, *places[j])
                        if not (last and j == per - 1):
                            candidates(l, n + 1, slot)
                        if back > 1:
                            turned_rows(l, n, *places[j])

                if between:
                    body(0)
                    body(1, between=between)
                with pe.Fori(2 if between else 0, ITERS - 1) as i:
                    body(i)
                body(ITERS - 1, True)

            def project(call, rows, weights):
                w = PROJ[call]
                for g in range(NG + 1):
                    if g < NG:
                        if g >= 2:
                            pe.wait_ge(s_tc, call * NG + g - 1)
                        for k in range(min(4, H - 4 * g)):
                            last = pe.transpose(bank[3 + g % 2][0:D, k * L:(k + 1) * L], rows[:, 4 * g + k, :], ident[:, :])
                        last.then_inc(s_tp, 1)
                    if g:
                        j = g - 1
                        pe.wait_ge(s_tc, call * NG + j + 1)
                        if j >= 2:
                            pe.wait_ge(s_pc, call * NG + j - 1)
                        for k in range(min(4, H - 4 * j)):
                            h = 4 * j + k
                            last = pe.matmul(bank[5 + j % 2][:, k * w:(k + 1) * w], xT[0:D, h * L:(h + 1) * L], weights,
                                             start=True, stop=True)
                        last.then_inc(s_pj, 1)

            pe.wait_ge(s_const, 2)
            pe.wait_ge(s_rcf, 1)
            for b in range(8):
                if b >= 2:
                    pe.wait_ge(s_rcc, 2 * (b - 1))
                for a in range(2):
                    pe.transpose(bank[5 + b % 2][0:100, a * 128:a * 128 + P], src_f[0:P, 1 + a, b * 100:(b + 1) * 100],
                                 ident[0:P, 0:P]).then_inc(s_rct, 1)

            pe.wait_ge(s_onehot, 1)
            for t in range(TB):
                last = pe.matmul(bank[0][:, 0:H], lo_le[0:P, t, :], hi_eq[0:P, t, :], start=(t == 0), stop=(t == TB - 1))
            last.then_inc(s_hist, 1)
            pe.wait_ge(s_tail, 1)
            pe.matmul(bank[0][:, 64:64 + H], last_l[:, :], tot[:, :], start=True, stop=True).then_inc(s_tback, 1)

            def turned_bounds():
                pe.wait_ge(s_hidx, 1)
                pe.transpose(bank[0][0:H, 128:256], end_c[:, :], ident[:, :]).then_inc(s_tback, 1)
                pe.wait_ge(s_bld, 48)
                pe.transpose(bank[0][:, 256:256 + H], brow[:, :], ident[0:H, 0:H]).then_inc(s_tback, 1)

            lookups(0, turned_bounds)
            pe.wait_ge(s_gidx, 1)
            spilled(0)
            pe.wait_ge(s_scaled, 1)
            pe.wait_ge(s_xn, 1)
            project(0, xn, wmix[:, :])
            pe.wait_ge(s_stk, 16 * 8)
            lookups(1)
            spilled(1)
            pe.wait_ge(s_xn, 2)
            project(1, xn, wsi[:, :])

            pe.wait_ge(s_tc, 2 * NG)
            pe.wait_ge(s_pc, 2 * NG)

            def channels_summed(i, s):
                pe.wait_ge(s_use[2][s], i + 2)
                for c in range(M):
                    last = pe.matmul(bank[4][0:P, 0:T * 2 * M], ident[0:P, 0:P], prod[0:P, :, c, 4 * M:6 * M],
                                     start=(c == 0), stop=(c == M - 1))
                last.then_inc(s_red, 1)

            def features_turned(i, s):
                pe.wait_ge(s_ef[s], i * 16 + 16)
                for g in range(TQ):
                    place = bank[3][:, g * P:(g + 1) * P] if g < 4 else bank[5][:, 0:P]
                    last = pe.transpose(place, ef[0:P, s, g * 4 * D:(g + 1) * 4 * D], ident[0:P, 0:P])
                last.then_inc(s_eft[s], 1)

            def mlp(i, end=False):
                for s in range(2):
                    pe.wait_ge(s_efc, i * 4 + 2 * s + 2)
                    for k in range(Q):
                        if k >= 2:
                            pe.wait_ge(s_hc, i * 10 + (5 * s + k - 1))
                        pe.matmul(bank[5 + k % 2][:, 0:4 * P], w1blk[:, k, :], efT[:, 0:4 * P], start=True, stop=True).then_inc(s_hp, 1)
                    for k in range(Q):
                        last = pe.matmul(bank[3][:, k * P:(k + 1) * P], w1blk[:, k, :], efT[:, 4 * P:5 * P], start=True, stop=True)
                    last.then_inc(s_hp, 1)
                    pe.wait_ge(s_hc, i * 10 + (5 * s + 5))
                    for j in range(PAIRS):
                        if j == 4 and s == 1:
                            channels_summed(i, 0)
                        elif j == 4 and (not isinstance(i, int) or i):
                            channels_summed(i - 1, 1)
                        if j == 8 and not (end and s == 1):
                            features_turned(*((i, 1) if s == 0 else (i + 1, 0)))
                        if j >= 4:
                            pe.wait_ge(s_wc, i * (2 * PAIRS) + (s * PAIRS + j - 3))
                        for r in range(2):
                            g, k = divmod(2 * j + r, Q)
                            h_ = hid[:, k, g * P:(g + 1) * P] if g < 4 else hid_last[:, k, :]
                            last = pe.matmul(bank[WBANKS[(s * PAIRS + j) % 4]][0:P, r * 256:(r + 1) * 256], h_, w2[:, :],
                                             start=True, stop=True)
                        last.then_inc(s_wp, 1)

            features_turned(0, 0)
            mlp(0)
            with pe.Fori(1, ITERS - 1) as i:
                mlp(i)
            mlp(ITERS - 1, True)
            channels_summed(ITERS - 1, 1)
            pe.wait_ge(s_wc, ITERS * 2 * PAIRS)
            spilled(2)
            pe.wait_ge(s_xn, 3)
            project(2, xn, wkvq[:, :])

            lookups(3)

            pe.wait_ge(s_tail, 3)
            for k in range(4):
                last = pe.transpose(bank[0][0:HEADS, k * 128:k * 128 + P], packed[0:P, k, :], ident[0:P, 0:P])
            last.then_inc(s_tback, 1)
            pe.wait_ge(s_tail, 4)
            pe.transpose(bank[0][0:P, 0:HEADS], fT[:, 4, 0:P], ident[0:HEADS, 0:HEADS])
            pe.transpose(bank[0][0:P, HEADS:2 * HEADS], fT[:, 6, 0:P], ident[0:HEADS, 0:HEADS]).then_inc(s_tback, 1)
            spilled(3)
            pe.wait_ge(s_attn, 1)
            project(3, si_s, wos[:, :])

        @block.scalar
        def _(act):
            qstart_v = qstart[0:E, :].rearrange("(p t) c -> p (t c)", p=P)
            bounds_hl = [bounds[0:1, k:k + NPAD].rearrange("a (h l) -> (a h) l", l=L) for k in range(2)]

            for b in range(8):
                act.wait_ge(s_rct, 2 * b + 2)
                for a in range(2):
                    act.copy(turned[0:100, b, a, :], bank[5 + b % 2][0:100, a * 128:a * 128 + P]).then_inc(s_rcc, 1)
            act.wait_ge(s_wclr, 7)
            act.dma_start(xn[:, 0:HF, :], x[0:L * HF, :].rearrange("(h l) c -> l h c", l=L)).then_inc(s_x, 16)
            act.dma_start(xn[0:REST, HF, :], x[L * HF:N, :]).then_inc(s_x, 16)
            def copies(l, i, s):
                for g in range(LOOK[l][s]):
                    w = stacks[l].shape[1]
                    n, slot = group(l, i, s, g), slot_of(l, s, g)[0]
                    t = s * T + GATHERED[l][s] + g * Q
                    act.wait_ge(s_use[l][s], i + 1)
                    act.wait_ge(s_lp, n + 1)
                    act.copy([rows0, rows1, None, rows3][l][0:P, t:t + Q, :],
                             bank[5 + slot][0:P, 0:Q * w].rearrange("p (t c) -> p t c", c=w)).then_inc(s_lc, 1)

            def repeated(i, l):
                if l or not isinstance(i, int) or i:
                    act.wait_ge(s_acc, i + l * ITERS)
                act.copy(krep_of[l].rearrange("p (f t) -> p f t", f=D)[0:P, :, 1:BX],
                         keep[0:P, bass.ds(i * B, B)].unsqueeze(1).broadcast_to([P, D, B])).then_inc(s_krep, 1)

            def sum_rows(i, l):
                act.wait_ge(s_acc, i + (l * ITERS + 1))
                if l or not isinstance(i, int) or i:
                    act.wait_ge(s_sum, i * 16 + l * (ITERS * 16))
                act.copy(sumrows_of[l][0:P], acc[0:P, :, 1:BX].rearrange("p f t -> p t f")).then_inc(s_rows, 1)

            def cleared(i):
                for r in range(2):
                    act.dma_start(qstart_v[:, bass.ds(i * (B * D) + r * ZW, ZW)], zero[0:P, 0:ZW]).then_inc(s_qz, 16)

            def looked_up_bodies(l):
                def body(i):
                    copies(l, i, 0)
                    sum_rows(i - 1, l)
                    repeated(i, l)
                    if l == 1:
                        cleared(i)
                    copies(l, i, 1)

                if l == 0:
                    body(1)
                with act.Fori(2 if l == 0 else 1, ITERS) as i:
                    body(i)
                sum_rows(ITERS - 1, l)

            def root(l):
                act.wait_ge(s_var, l + 1)
                act.activation(stat[:, 0, :], stat[:, 1, :], ACT.Sqrt).then_inc(s_std, 1)

            def evacuate(call):
                w = PROJ[call]
                for g in range(NG + 1):
                    if g < NG:
                        n = min(4, H - 4 * g)
                        act.wait_ge(s_tp, call * NG + g + 1)
                        act.copy(xT[0:D, 4 * g * L:(4 * g + n) * L], bank[3 + g % 2][0:D, 0:n * L]).then_inc(s_tc, 1)
                    if g:
                        j = g - 1
                        n = min(4, H - 4 * j)
                        hs = slice(4 * j, 4 * j + n)
                        got = bank[5 + j % 2][:, 0:n * w].rearrange("p (h c) -> p h c", c=w)
                        act.wait_ge(s_pj, call * NG + j + 1)
                        if call == 0:
                            act.copy(nodeout[:, hs, :], got).then_inc(s_pc, 1)
                        elif call == 2:
                            act.copy(kvout[:, hs, :], got[:, :, 0:KV])
                            act.copy(qout[:, hs, :], got[:, :, KV:3 * D]).then_inc(s_pc, 1)
                        else:
                            act.copy(si_s[:, hs, :], got).then_inc(s_pc, 1)

            copies(0, 0, 0)
            act.wait_ge(s_kclr, 1)
            act.wait_ge(s_hist, 1)
            repeated(0, 0)
            copies(0, 0, 1)
            act.wait_ge(s_tail, 2)
            act.dma_start(bounds_hl[1], brow[:, :]).then_inc(s_bnd, 16)
            act.dma_start(bounds[0:1, 0:1], zero[0:1, 0:1]).then_inc(s_bnd, 16)
            act.wait_ge(s_bnd, 32)
            act.dma_start(brow[:, :], bounds_hl[0]).then_inc(s_bld, 16)
            act.dma_start(spill[0:P, :], bounds[0:1, 0:NPAD].broadcast_to([P, NPAD])).then_inc(s_bld, 16)
            act.dma_start(next_b[0:P, :], bounds[0:1, 1:NPAD + 1].broadcast_to([P, NPAD])).then_inc(s_bld, 16)
            act.dma_start(ew1_s[0:P, :], ew1.rearrange("(p t) c -> p (t c)", p=P)).then_inc(s_attr, 16)
            act.dma_start(sh3_flat[0:P, :], ea3.rearrange("(p t) c -> p (t c)", p=P)).then_inc(s_attr, 16)
            act.dma_start(sh4_flat[0:P, :], ea4.rearrange("(p t) c -> p (t c)", p=P)).then_inc(s_attr, 16)
            act.dma_start(sh5_flat[0:P, :], ea5.rearrange("(p t) c -> p (t c)", p=P)).then_inc(s_attr, 16)
            for place, weights in wlist:
                act.dma_start(place, weights, allow_slow_non_contiguous=True).then_inc(s_wts, 16)
            looked_up_bodies(0)
            act.wait_ge(s_scaled, 1)
            for c in range(C):
                act.dma_start(stack_mix[c * D:(c + 1) * D, :], wmix[:, :]).then_inc(s_stk, 16)
                act.dma_start(stack_kv[c * D:(c + 1) * D, :], wkvq[:, 0:KV]).then_inc(s_stk, 16)
            root(0)
            evacuate(0)
            copies(1, 0, 0)
            act.wait_ge(s_kclr, 2)
            cleared(0)
            repeated(0, 1)
            copies(1, 0, 1)
            looked_up_bodies(1)
            root(1)
            evacuate(1)
            act.wait_ge(s_kclr, 3)

            def features_copied(i, s):
                act.wait_ge(s_eft[s], i + 1)
                act.copy(efT[:, 0:4 * P], bank[3][:, 0:4 * P]).then_inc(s_efc, 1)
                act.copy(efT[:, 4 * P:5 * P], bank[5][:, 0:P]).then_inc(s_efc, 1)

            def mlp(i, end=False):
                for s in range(2):
                    for k in range(Q):
                        act.wait_ge(s_hp, i * 10 + (5 * s + k + 1))
                        act.activation(hid[:, k, :], bank[5 + k % 2][:, 0:4 * P], ACT.Relu, bias=b1[:, 0:1]).then_inc(s_hc, 1)
                    act.wait_ge(s_hp, i * 10 + (5 * s + 5))
                    act.activation(hid_last, bank[3][:, 0:4 * P].rearrange("p (k e) -> p k e", k=Q), ACT.Relu,
                                   bias=b1[:, 0:1]).then_inc(s_hc, 1)
                    act.wait_ge(s_use[2][1 - s], i + (1 + s))
                    for j in range(PAIRS):
                        if j == 8 and not (end and s == 1):
                            features_copied(*((i, 1) if s == 0 else (i + 1, 0)))
                        act.wait_ge(s_wp, i * (2 * PAIRS) + (s * PAIRS + j + 1))
                        act.copy(wide[0:P, 2 * j:2 * j + 2, :, :].rearrange("p t i c -> p (t i c)"),
                                 bank[WBANKS[(s * PAIRS + j) % 4]][0:P, :]).then_inc(s_wc, 1)
                    if s == 0:
                        if not isinstance(i, int) or i:
                            sum_rows(i - 1, 2)
                        repeated(i, 2)

            features_copied(0, 0)
            mlp(0)
            with act.Fori(1, ITERS - 1) as i:
                mlp(i)
            mlp(ITERS - 1, True)
            sum_rows(ITERS - 1, 2)
            root(2)
            evacuate(2)
            def keep_values(i, s):
                act.wait_ge(s_gat[3][s], (i + 1) * (16 * GATHERED[3][s]))
                act.wait_ge(s_lc, group(3, i, s, LOOK[3][s]))
                act.copy(vals[0:P, bass.ds(i * B + s * T, T), :], rows3[0:P, s * T:(s + 1) * T, D:KV]).then_inc(s_val[s], 1)

            copies(3, 0, 0)
            with act.Fori(0, ITERS - 1) as i:
                keep_values(i, 0)
                copies(3, i, 1)
                keep_values(i, 1)
                copies(3, i + 1, 0)
            keep_values(ITERS - 1, 0)
            copies(3, ITERS - 1, 1)
            keep_values(ITERS - 1, 1)
            act.wait_ge(s_max, 1)
            act.activation(sc[0:P], sc[0:P], ACT.Exp).then_inc(s_exp, 1)

            def repeated3(n):
                if not isinstance(n, int) or n:
                    act.wait_ge(s_acc3, n)
                act.copy(wkrep.rearrange("p (f t) -> p f t", f=RW)[0:P, :, 1:EX],
                         keep[0:P, bass.ds(n * EB, EB)].unsqueeze(1).broadcast_to([P, RW, EB])).then_inc(s_krep, 1)

            def sum_rows3(i, s):
                act.wait_ge(s_acc3, i * 2 + (s + 1))
                if not isinstance(i, int) or i:
                    act.wait_ge(s_sum3[s], i * 16)
                act.copy(accs[s][0:P], waccT[s][0:P, :, 1:EX].rearrange("p f t -> p t f")).then_inc(s_rows3, 1)

            act.wait_ge(s_kclr, 4)
            repeated3(0)
            for s in range(2):
                repeated3(s + 1)
                sum_rows3(0, s)
            with act.Fori(1, BLOCKS // 2 - 1) as i:
                for s in range(2):
                    repeated3(i * 2 + (s + 1))
                    sum_rows3(i, s)
            repeated3(BLOCKS - 1)
            for s in range(2):
                sum_rows3(BLOCKS // 2 - 1, s)
            evacuate(3)
            root(3)


_INS = ['x', 'src', 'dst', 'edge_attr_3', 'edge_attr_32', 'edge_attr_4', 'edge_attr_5', 'edge_weight', 'edge_weight1',
        'L1_gnn_W', 'L2_gnn_W1', 'L2_gnn_b1', 'L2_gnn_W2', 'L2_gnn_b2', 'L2_gnn_si_w0', 'L2_gnn_si_w1',
        'L3_gnn_Wq', 'L3_gnn_Wk', 'L3_gnn_Wv', 'L3_gnn_Wo']


def kernel(**inputs):
    import numpy as _np
    import concourse.bacc as _bacc
    from concourse import mybir as _mybir
    from concourse.bass_utils import run_bass_kernel_spmd as _run

    nc = _bacc.Bacc("TRN2", target_bir_lowering=False, num_devices=1)
    arrays, args = {}, []
    for name in _INS:
        a = _np.ascontiguousarray(inputs[name])
        arrays[f"in_{name}_dram"] = a
        args.append(nc.dram_tensor(f"in_{name}_dram", a.shape, _mybir.dt.from_np(a.dtype), kind="ExternalInput").ap())
    out = nc.dram_tensor("out_0_dram", (N, D), F32, kind="ExternalOutput").ap()
    gnn_kernel(nc, *args, out)
    r = _run(nc, [arrays], core_ids=[0])
    return r.results[0]["out_0_dram"]
```
